# Optimizing a Trainium2 kernel written in Bass

```python
import numpy as np
import jax
import jax.numpy as jnp

def _softmax(x, axis=-1):
    return jax.nn.softmax(x, axis=axis)

def _gelu(x):
    return jax.nn.gelu(x, approximate=True)

def _silu(x):
    return jax.nn.silu(x)

def _sigmoid(x):
    return jax.nn.sigmoid(x)

def _layernorm(x, axis=-1, eps=1e-05):
    m = jnp.mean(x, axis=axis, keepdims=True)
    v = jnp.var(x, axis=axis, keepdims=True)
    return (x - m) / jnp.sqrt(v + eps)

def _scatter_add(tgt, idx, src, axis=0):
    return tgt.at[idx].add(src)

def _segment_sum(src, seg, n):
    return jax.ops.segment_sum(src, seg, n)
kernel_name = 'mk_flamingo_gated_d4_seqx_r4_0b0c73'

def setup_inputs(seed: int=0):
    np.random.seed(seed)
    _w = jnp.asarray

    def _rec_inputs():
        import jax
        import jax.numpy as jnp
        _rk = jax.random.key(seed)
        x = -0.000125 + 0.9999 * jax.random.normal(jax.random.fold_in(_rk, 1), (2, 512, 512), jnp.float32)
        _lenS = 512 - jax.random.randint(jax.random.fold_in(_rk, 7), (2,), 0, max(1, 512 // 4) + 1, jnp.int32)
        _lenS2 = 1024 - jax.random.randint(jax.random.fold_in(_rk, 8), (2,), 0, max(1, 1024 // 4) + 1, jnp.int32)
        _ctx_2048P = jax.random.normal(jax.random.fold_in(_rk, 11), (2, 16, 512), jnp.float32)
        _ctx_2048c = jax.random.dirichlet(jax.random.fold_in(_rk, 511), 0.3 * jnp.ones((16,), jnp.float32), (2, 1024))
        _ctx_2048t = jnp.einsum('bsk,bkd->bsd', _ctx_2048c, _ctx_2048P)
        _ctx_2048t = _ctx_2048t * jax.lax.rsqrt(jnp.mean(jnp.square(_ctx_2048t)) + 1e-12) * 0.953939
        ctx_2048 = -1.52775e-05 + 0.999936 * (_ctx_2048t + 0.3 * jax.random.normal(jax.random.fold_in(_rk, 611), (2, 1024, 512), jnp.float32))
        _validS = jnp.arange(512)[None, :] < _lenS[:, None]
        _validS2 = jnp.arange(1024)[None, :] < _lenS2[:, None]
        _causal = jnp.tril(jnp.ones((512, 512), dtype=bool))
        mask_BxS2_ff1 = jnp.where(jnp.ones((2, 1024), dtype=bool), 1.0, 0.0).astype(jnp.float32)
        mask_BxS2_ik0 = jnp.where(jnp.broadcast_to(_validS2[:, :], (2, 1024)), 0, 1).astype(jnp.int32)
        _g = jax.random.normal(jax.random.fold_in(_rk, 9001), (2, 4), jnp.float32)
        _g = jnp.sign(_g) * jnp.maximum(jnp.abs(_g), 1.0) + (_g == 0) * 1.0
        g_xattn = _g[0]
        g_ffn = _g[1]
        return (x, ctx_2048, mask_BxS2_ff1, mask_BxS2_ik0, g_xattn, g_ffn)
    x, ctx_2048, mask_BxS2_ff1, mask_BxS2_ik0, g_xattn, g_ffn = _rec_inputs()

    def _L0_xattn_setup():
        import jax, jax.numpy as jnp
        import numpy as np
        H = 512
        NH = 16
        HD = H // NH
        FD = 64
        key = jax.random.key(seed)
        ks = jax.random.split(key, 12)
        B, S = (4, 1024)
        s = 1.0 / np.sqrt(H)
        sf = 1.0 / np.sqrt(HD)
        return {'query': jax.random.normal(ks[0], (B, S, H), jnp.float32), 'key': jax.random.normal(ks[1], (B, S, H), jnp.float32), 'value': jax.random.normal(ks[2], (B, S, H), jnp.float32), 'attention_mask': jnp.ones((B, S), jnp.float32), 'Wq': jax.random.normal(ks[3], (H, H), jnp.float32) * s, 'bq': jnp.zeros((H,), jnp.float32), 'Wk': jax.random.normal(ks[4], (H, H), jnp.float32) * s, 'bk': jnp.zeros((H,), jnp.float32), 'Wv': jax.random.normal(ks[5], (H, H), jnp.float32) * s, 'bv': jnp.zeros((H,), jnp.float32), 'Wqf': jax.random.normal(ks[6], (FD, HD), jnp.float32) * sf, 'Wkf': jax.random.normal(ks[7], (FD, HD), jnp.float32) * sf, 'Wo': jax.random.normal(ks[8], (H, H), jnp.float32) * s, 'bo': jnp.zeros((H,), jnp.float32)}
    _L0_xattn_all = _L0_xattn_setup()
    _L0_xattn_in = {k: v for k, v in _L0_xattn_all.items() if k in ('Wq', 'bq', 'Wk', 'bk', 'Wv', 'bv', 'Wqf', 'Wkf', 'Wo', 'bo')}
    del _L0_xattn_all

    def _L0_ffn_setup():
        import jax, jax.numpy as jnp
        import numpy as np
        D_MODEL = 512
        D_EXPERT = 2048
        EPS = 1e-08

        def ternary_quant(w):
            scale = jnp.mean(jnp.abs(w)) + EPS
            q = jnp.clip(jnp.round(w / scale), -1.0, 1.0) * scale
            return w + jax.lax.stop_gradient(q - w)
        key = jax.random.key(seed)
        k_x, k_up, k_gate, k_down = jax.random.split(key, 4)
        std_in = 1.0 / np.sqrt(D_MODEL)
        std_exp = 1.0 / np.sqrt(D_EXPERT)
        return {'x': jax.random.normal(k_x, (4, 512, D_MODEL), dtype=jnp.float32), 'W_up': jax.random.normal(k_up, (D_EXPERT, D_MODEL), dtype=jnp.float32) * std_in, 'W_gate': jax.random.normal(k_gate, (D_EXPERT, D_MODEL), dtype=jnp.float32) * std_in, 'W_down': jax.random.normal(k_down, (D_MODEL, D_EXPERT), dtype=jnp.float32) * std_exp}
    _L0_ffn_all = _L0_ffn_setup()
    _L0_ffn_in = {k: v for k, v in _L0_ffn_all.items() if k in ('W_up', 'W_gate', 'W_down')}
    del _L0_ffn_all

    def _L1_xattn_setup():
        import jax, jax.numpy as jnp
        import numpy as np
        import math
        H = 512
        NH = 16
        HD = H // NH
        EPS_LN = 1e-05
        RES_SCALE_MAX = 0.3

        def _nan_clean(x, lim=10000.0):
            return jnp.nan_to_num(x, nan=0.0, posinf=lim, neginf=-lim)
        key = jax.random.key(seed)
        ks = jax.random.split(key, 12)
        B, S, T = (4, 512, 64)
        std = 1.0 / math.sqrt(H)
        return {'hidden_states': jax.random.normal(ks[0], (B, S, H), jnp.float32), 'audio_tokens': jax.random.normal(ks[1], (B, T, H), jnp.float32), 'attention_mask': jax.random.randint(ks[2], (B, T), 0, 2, jnp.int32), 'Wq': jax.random.normal(ks[3], (H, H), jnp.float32) * std, 'bq': jnp.zeros((H,), jnp.float32), 'Wk': jax.random.normal(ks[4], (H, H), jnp.float32) * std, 'bk': jnp.zeros((H,), jnp.float32), 'Wv': jax.random.normal(ks[5], (H, H), jnp.float32) * std, 'bv': jnp.zeros((H,), jnp.float32), 'Wo': jax.random.normal(ks[6], (H, H), jnp.float32) * std, 'bo': jnp.zeros((H,), jnp.float32), 'ln_gamma': jnp.ones((H,), jnp.float32), 'ln_beta': jnp.zeros((H,), jnp.float32), 'residual_scale': jnp.float32(0.05)}
    _L1_xattn_all = _L1_xattn_setup()
    _L1_xattn_in = {k: v for k, v in _L1_xattn_all.items() if k in ('Wq', 'bq', 'Wk', 'bk', 'Wv', 'bv', 'Wo', 'bo', 'ln_gamma', 'ln_beta', 'residual_scale')}
    del _L1_xattn_all

    def _L1_ffn_setup():
        import jax, jax.numpy as jnp
        import numpy as np
        B, T, D = (2, 256, 512)
        H, K, DK = (4, 8, 64)
        E = 4096
        NK = 128
        key = jax.random.key(seed)
        k1, k2, k3, k4, k5 = jax.random.split(key, 5)
        x = jax.random.normal(k1, (B, T, D), dtype=jnp.float32)
        Wq = jax.random.normal(k2, (D, 2 * H * DK), dtype=jnp.float32) * 0.02
        keys = jax.random.normal(k3, (H, NK, 2, DK), dtype=jnp.float32) * 0.02
        e_down = jax.random.normal(k4, (E, D), dtype=jnp.float32) * 0.01
        e_up = jax.random.normal(k5, (E, D), dtype=jnp.float32) * 0.01
        return {'x': x, 'Wq': Wq, 'keys': keys, 'e_down': e_down, 'e_up': e_up}
    _L1_ffn_all = _L1_ffn_setup()
    _L1_ffn_in = {k: v for k, v in _L1_ffn_all.items() if k in ('Wq', 'keys', 'e_down', 'e_up')}
    del _L1_ffn_all

    def _L2_xattn_setup():
        import jax, jax.numpy as jnp
        import numpy as np
        NUM_HEADS = 16

        def _qdq(x):
            s = jnp.maximum(jnp.max(jnp.abs(x), axis=-1, keepdims=True) / 127.0, 1e-08)
            return jnp.clip(jnp.round(x / s), -127.0, 127.0) * s
        key = jax.random.key(seed)
        ks = jax.random.split(key, 8)
        B, N, M, D = (2, 1024, 128, 512)
        w_std = 0.02
        return {'x': jax.random.normal(ks[0], (B, N, D), jnp.float32), 'cond': jax.random.normal(ks[1], (B, M, D), jnp.float32), 'wq': jax.random.normal(ks[2], (D, D), jnp.float32) * w_std, 'bq': jax.random.normal(ks[3], (D,), jnp.float32) * w_std, 'wkv': jax.random.normal(ks[4], (2 * D, D), jnp.float32) * w_std, 'bkv': jax.random.normal(ks[5], (2 * D,), jnp.float32) * w_std, 'wp': jax.random.normal(ks[6], (D, D), jnp.float32) * w_std, 'bp': jax.random.normal(ks[7], (D,), jnp.float32) * w_std}
    _L2_xattn_all = _L2_xattn_setup()
    _L2_xattn_in = {k: v for k, v in _L2_xattn_all.items() if k in ('wq', 'bq', 'wkv', 'bkv', 'wp', 'bp')}
    del _L2_xattn_all

    def _L2_ffn_setup():
        import jax, jax.numpy as jnp
        import numpy as np
        B, S, D = (4, 512, 512)
        E, K, M = (8, 2, 256)
        key = jax.random.key(seed)
        k0, k1, k2, k3, k4 = jax.random.split(key, 5)
        d_scale = D ** (-0.5)
        m_scale = M ** (-0.5)
        return {'x': jax.random.normal(k0, (B, S, D), jnp.float32), 'w_gate': jax.random.normal(k1, (D, E), jnp.float32) * d_scale, 'wi_0': jax.random.normal(k2, (E, D, M), jnp.float32) * d_scale, 'wi_1': jax.random.normal(k3, (E, D, M), jnp.float32) * d_scale, 'wo': jax.random.normal(k4, (E, M, D), jnp.float32) * m_scale}
    _L2_ffn_all = _L2_ffn_setup()
    _L2_ffn_in = {k: v for k, v in _L2_ffn_all.items() if k in ('w_gate', 'wi_0', 'wi_1', 'wo')}
    del _L2_ffn_all

    def _L3_xattn_setup():
        import jax, jax.numpy as jnp
        import numpy as np
        D_MODEL = 512
        NUM_HEADS = 16
        HEAD_DIM = D_MODEL // NUM_HEADS
        key = jax.random.key(seed)
        ks = jax.random.split(key, 10)
        B, S, T = (4, 1024, 256)
        s = 1.0 / np.sqrt(D_MODEL)
        inp = {'query': jax.random.normal(ks[0], (B, S, D_MODEL), jnp.float32), 'key_value': jax.random.normal(ks[1], (B, T, D_MODEL), jnp.float32), 'Wq': jax.random.normal(ks[2], (D_MODEL, D_MODEL), jnp.float32) * s, 'bq': jnp.zeros((D_MODEL,), jnp.float32), 'Wk': jax.random.normal(ks[3], (D_MODEL, D_MODEL), jnp.float32) * s, 'bk': jnp.zeros((D_MODEL,), jnp.float32), 'Wv': jax.random.normal(ks[4], (D_MODEL, D_MODEL), jnp.float32) * s, 'bv': jnp.zeros((D_MODEL,), jnp.float32), 'Wo': jax.random.normal(ks[5], (D_MODEL, D_MODEL), jnp.float32) * s, 'bo': jnp.zeros((D_MODEL,), jnp.float32)}
        return inp
    _L3_xattn_all = _L3_xattn_setup()
    _L3_xattn_in = {k: v for k, v in _L3_xattn_all.items() if k in ('Wq', 'bq', 'Wk', 'bk', 'Wv', 'bv', 'Wo', 'bo')}
    del _L3_xattn_all

    def _L3_ffn_setup():
        import jax, jax.numpy as jnp
        import numpy as np
        HIDDEN = 512
        NUM_EXPERTS = 8
        TOP_K = 2
        MOE_INTER = 352
        SHARED_INTER = 1408

        def _silu_and_mul(gu):
            i = gu.shape[-1] // 2
            return jax.nn.silu(gu[:, :i]) * gu[:, i:]
        key = jax.random.key(seed)
        ks = jax.random.split(key, 7)
        s = 0.02
        return {'hidden_states': jax.random.normal(ks[0], (2, 512, HIDDEN), dtype=jnp.float32), 'gate_w': jax.random.normal(ks[1], (NUM_EXPERTS, HIDDEN), dtype=jnp.float32) * s, 'shared_gate_w': jax.random.normal(ks[2], (1, HIDDEN), dtype=jnp.float32) * s, 'shared_gate_up_w': jax.random.normal(ks[3], (2 * SHARED_INTER, HIDDEN), dtype=jnp.float32) * s, 'shared_down_w': jax.random.normal(ks[4], (HIDDEN, SHARED_INTER), dtype=jnp.float32) * s, 'w13': jax.random.normal(ks[5], (NUM_EXPERTS, 2 * MOE_INTER, HIDDEN), dtype=jnp.float32) * s, 'w2': jax.random.normal(ks[6], (NUM_EXPERTS, HIDDEN, MOE_INTER), dtype=jnp.float32) * s}
    _L3_ffn_all = _L3_ffn_setup()
    _L3_ffn_in = {k: v for k, v in _L3_ffn_all.items() if k in ('gate_w', 'shared_gate_w', 'shared_gate_up_w', 'shared_down_w', 'w13', 'w2')}
    del _L3_ffn_all
    return {'x': x, 'ctx_2048': ctx_2048, 'mask_BxS2_ff1': mask_BxS2_ff1, 'mask_BxS2_ik0': mask_BxS2_ik0, 'g_xattn': g_xattn, 'g_ffn': g_ffn, 'L0_xattn_Wq': _L0_xattn_in['Wq'], 'L0_xattn_bq': _L0_xattn_in['bq'], 'L0_xattn_Wk': _L0_xattn_in['Wk'], 'L0_xattn_bk': _L0_xattn_in['bk'], 'L0_xattn_Wv': _L0_xattn_in['Wv'], 'L0_xattn_bv': _L0_xattn_in['bv'], 'L0_xattn_Wqf': _L0_xattn_in['Wqf'], 'L0_xattn_Wkf': _L0_xattn_in['Wkf'], 'L0_xattn_Wo': _L0_xattn_in['Wo'], 'L0_xattn_bo': _L0_xattn_in['bo'], 'L0_ffn_W_up': _L0_ffn_in['W_up'], 'L0_ffn_W_gate': _L0_ffn_in['W_gate'], 'L0_ffn_W_down': _L0_ffn_in['W_down'], 'L1_xattn_Wq': _L1_xattn_in['Wq'], 'L1_xattn_bq': _L1_xattn_in['bq'], 'L1_xattn_Wk': _L1_xattn_in['Wk'], 'L1_xattn_bk': _L1_xattn_in['bk'], 'L1_xattn_Wv': _L1_xattn_in['Wv'], 'L1_xattn_bv': _L1_xattn_in['bv'], 'L1_xattn_Wo': _L1_xattn_in['Wo'], 'L1_xattn_bo': _L1_xattn_in['bo'], 'L1_xattn_ln_gamma': _L1_xattn_in['ln_gamma'], 'L1_xattn_ln_beta': _L1_xattn_in['ln_beta'], 'L1_xattn_residual_scale': _L1_xattn_in['residual_scale'], 'L1_ffn_Wq': _L1_ffn_in['Wq'], 'L1_ffn_keys': _L1_ffn_in['keys'], 'L1_ffn_e_down': _L1_ffn_in['e_down'], 'L1_ffn_e_up': _L1_ffn_in['e_up'], 'L2_xattn_wq': _L2_xattn_in['wq'], 'L2_xattn_bq': _L2_xattn_in['bq'], 'L2_xattn_wkv': _L2_xattn_in['wkv'], 'L2_xattn_bkv': _L2_xattn_in['bkv'], 'L2_xattn_wp': _L2_xattn_in['wp'], 'L2_xattn_bp': _L2_xattn_in['bp'], 'L2_ffn_w_gate': _L2_ffn_in['w_gate'], 'L2_ffn_wi_0': _L2_ffn_in['wi_0'], 'L2_ffn_wi_1': _L2_ffn_in['wi_1'], 'L2_ffn_wo': _L2_ffn_in['wo'], 'L3_xattn_Wq': _L3_xattn_in['Wq'], 'L3_xattn_bq': _L3_xattn_in['bq'], 'L3_xattn_Wk': _L3_xattn_in['Wk'], 'L3_xattn_bk': _L3_xattn_in['bk'], 'L3_xattn_Wv': _L3_xattn_in['Wv'], 'L3_xattn_bv': _L3_xattn_in['bv'], 'L3_xattn_Wo': _L3_xattn_in['Wo'], 'L3_xattn_bo': _L3_xattn_in['bo'], 'L3_ffn_gate_w': _L3_ffn_in['gate_w'], 'L3_ffn_shared_gate_w': _L3_ffn_in['shared_gate_w'], 'L3_ffn_shared_gate_up_w': _L3_ffn_in['shared_gate_up_w'], 'L3_ffn_shared_down_w': _L3_ffn_in['shared_down_w'], 'L3_ffn_w13': _L3_ffn_in['w13'], 'L3_ffn_w2': _L3_ffn_in['w2']}

def reference(x, ctx_2048, mask_BxS2_ff1, mask_BxS2_ik0, g_xattn, g_ffn, L0_xattn_Wq, L0_xattn_bq, L0_xattn_Wk, L0_xattn_bk, L0_xattn_Wv, L0_xattn_bv, L0_xattn_Wqf, L0_xattn_Wkf, L0_xattn_Wo, L0_xattn_bo, L0_ffn_W_up, L0_ffn_W_gate, L0_ffn_W_down, L1_xattn_Wq, L1_xattn_bq, L1_xattn_Wk, L1_xattn_bk, L1_xattn_Wv, L1_xattn_bv, L1_xattn_Wo, L1_xattn_bo, L1_xattn_ln_gamma, L1_xattn_ln_beta, L1_xattn_residual_scale, L1_ffn_Wq, L1_ffn_keys, L1_ffn_e_down, L1_ffn_e_up, L2_xattn_wq, L2_xattn_bq, L2_xattn_wkv, L2_xattn_bkv, L2_xattn_wp, L2_xattn_bp, L2_ffn_w_gate, L2_ffn_wi_0, L2_ffn_wi_1, L2_ffn_wo, L3_xattn_Wq, L3_xattn_bq, L3_xattn_Wk, L3_xattn_bk, L3_xattn_Wv, L3_xattn_bv, L3_xattn_Wo, L3_xattn_bo, L3_ffn_gate_w, L3_ffn_shared_gate_w, L3_ffn_shared_gate_up_w, L3_ffn_shared_down_w, L3_ffn_w13, L3_ffn_w2):
    import jax
    import jax.numpy as jnp

    def _L0_xattn_ref(query, key, value, attention_mask, Wq, bq, Wk, bk, Wv, bv, Wqf, Wkf, Wo, bo):
        import jax, jax.numpy as jnp
        import numpy as np
        H = 512
        NH = 16
        HD = H // NH
        FD = 64
        B, Sq, _ = query.shape
        Sk = key.shape[1]

        def heads(x, W, b, S):
            return (x @ W.T + b).reshape(B, S, NH, HD).transpose(0, 2, 1, 3)
        q = heads(query, Wq, bq, Sq)
        k = heads(key, Wk, bk, Sk)
        v = heads(value, Wv, bv, Sk)
        q_prime = jax.nn.relu(jnp.einsum('bhnd,fd->bhnf', q, Wqf))
        k_prime = jax.nn.relu(jnp.einsum('bhnd,fd->bhnf', k, Wkf))
        k_prime = k_prime * attention_mask[:, None, :, None]
        kv = jnp.einsum('bhnf,bhne->bhfe', k_prime, v)
        qkv = jnp.einsum('bhmf,bhfe->bhme', q_prime, kv)
        k_sum = jnp.sum(k_prime, axis=2)
        qk_sum = jnp.einsum('bhmf,bhf->bhm', q_prime, k_sum)[..., None]
        out = qkv / (qk_sum + 1e-08)
        out = out.transpose(0, 2, 1, 3).reshape(B, Sq, H)
        return out @ Wo.T + bo

    def _L0_ffn_ref(x, W_up, W_gate, W_down):
        import jax, jax.numpy as jnp
        import numpy as np
        D_MODEL = 512
        D_EXPERT = 2048
        EPS = 1e-08

        def ternary_quant(w):
            scale = jnp.mean(jnp.abs(w)) + EPS
            q = jnp.clip(jnp.round(w / scale), -1.0, 1.0) * scale
            return w + jax.lax.stop_gradient(q - w)
        wu = ternary_quant(W_up)
        wg = ternary_quant(W_gate)
        wd = ternary_quant(W_down)
        up = jnp.einsum('bsd,ed->bse', x, wu)
        gate = jnp.einsum('bsd,ed->bse', x, wg)
        hidden = jax.nn.silu(up) * gate
        return jnp.einsum('bse,de->bsd', hidden, wd)

    def _L1_xattn_ref(hidden_states, audio_tokens, attention_mask, Wq, bq, Wk, bk, Wv, bv, Wo, bo, ln_gamma, ln_beta, residual_scale):
        import jax, jax.numpy as jnp
        import numpy as np
        import math
        H = 512
        NH = 16
        HD = H // NH
        EPS_LN = 1e-05
        RES_SCALE_MAX = 0.3

        def _nan_clean(x, lim=10000.0):
            return jnp.nan_to_num(x, nan=0.0, posinf=lim, neginf=-lim)
        B, S, _ = hidden_states.shape
        T = audio_tokens.shape[1]
        hs = _nan_clean(hidden_states).astype(jnp.float32)
        at = _nan_clean(audio_tokens).astype(jnp.float32)

        def proj(x, W, b, L):
            y = x @ W.T + b
            return y.reshape(B, L, NH, HD).transpose(0, 2, 1, 3)
        q = _nan_clean(proj(hs, Wq, bq, S))
        k = _nan_clean(proj(at, Wk, bk, T))
        v = _nan_clean(proj(at, Wv, bv, T))
        scale = max(math.sqrt(HD), 1e-08)
        scores = jnp.einsum('bhsd,bhtd->bhst', q, k) / scale
        scores = jnp.clip(scores, -50.0, 50.0)
        scores = jnp.nan_to_num(scores, nan=0.0, posinf=50.0, neginf=-50.0)
        attend = (attention_mask.astype(jnp.float32) > 0.5)[:, None, None, :]
        scores = jnp.where(attend, scores, -10000.0)
        scores = jnp.clip(scores, -50.0, 50.0)
        probs = jax.nn.softmax(scores, axis=-1)
        probs = jnp.nan_to_num(probs, nan=0.0, posinf=1.0, neginf=0.0)
        probs = probs / (probs.sum(axis=-1, keepdims=True) + 1e-08)
        ctx = jnp.einsum('bhst,bhtd->bhsd', probs, v)
        ctx = ctx.transpose(0, 2, 1, 3).reshape(B, S, H)
        delta = _nan_clean(ctx @ Wo.T + bo)
        rs = jnp.clip(residual_scale, 0.0, RES_SCALE_MAX)
        delta = rs * delta
        mu = delta.mean(axis=-1, keepdims=True)
        var = jnp.mean((delta - mu) ** 2, axis=-1, keepdims=True)
        delta = (delta - mu) / jnp.sqrt(var + EPS_LN) * ln_gamma + ln_beta
        return delta

    def _L1_ffn_ref(x, Wq, keys, e_down, e_up):
        import jax, jax.numpy as jnp
        import numpy as np
        B, T, D = (2, 256, 512)
        H, K, DK = (4, 8, 64)
        E = 4096
        NK = 128
        b, t, d = x.shape
        q = (x @ Wq).reshape(b, t, H, 2, DK)
        q1, q2 = (q[..., 0, :], q[..., 1, :])
        sim1 = jnp.einsum('bthd,hkd->bthk', q1, keys[:, :, 0, :])
        sim2 = jnp.einsum('bthd,hkd->bthk', q2, keys[:, :, 1, :])
        s1, i1 = jax.lax.top_k(sim1, K)
        s2, i2 = jax.lax.top_k(sim2, K)
        all_scores = (s1[..., :, None] + s2[..., None, :]).reshape(b, t, H, K * K)
        all_indices = (i1[..., :, None] * NK + i2[..., None, :]).reshape(b, t, H, K * K)
        final_scores, pk_idx = jax.lax.top_k(all_scores, K)
        final_indices = jnp.take_along_axis(all_indices, pk_idx, axis=-1)
        w_down = e_down[final_indices]
        w_up = e_up[final_indices]
        hidden = jnp.einsum('btd,bthkd->bthk', x, w_down)
        hidden = jax.nn.silu(hidden)
        hidden = hidden * jax.nn.relu(final_scores)
        out = jnp.einsum('bthk,bthkd->btd', hidden, w_up)
        return out

    def _L2_xattn_ref(x, cond, wq, bq, wkv, bkv, wp, bp):
        import jax, jax.numpy as jnp
        import numpy as np
        NUM_HEADS = 16

        def _qdq(x):
            s = jnp.maximum(jnp.max(jnp.abs(x), axis=-1, keepdims=True) / 127.0, 1e-08)
            return jnp.clip(jnp.round(x / s), -127.0, 127.0) * s
        B, N, C = x.shape
        M = cond.shape[1]
        H = NUM_HEADS
        Dh = C // H
        q = _qdq(x) @ _qdq(wq).T + bq
        kv = cond @ wkv.T + bkv
        k, v = jnp.split(kv, 2, axis=-1)
        q = q.reshape(B, N, H, Dh)
        k = k.reshape(B, M, H, Dh)
        v = v.reshape(B, M, H, Dh)
        scale = 1.0 / np.sqrt(Dh)
        attn = jax.nn.softmax(jnp.einsum('bnhd,bmhd->bhnm', q, k) * scale, axis=-1)
        o = jnp.einsum('bhnm,bmhd->bnhd', attn, v).reshape(B, N, C)
        out = _qdq(o) @ _qdq(wp).T + bp
        return out

    def _L2_ffn_ref(x, w_gate, wi_0, wi_1, wo):
        import jax, jax.numpy as jnp
        import numpy as np
        B, S, D = (4, 512, 512)
        E, K, M = (8, 2, 256)
        b, s, d = x.shape
        e = w_gate.shape[1]
        xf = x.reshape(-1, d)
        logits = jnp.dot(xf, w_gate)
        top_logits, top_idx = jax.lax.top_k(logits, K)
        weights = jax.nn.softmax(top_logits, axis=-1)
        flat_idx = top_idx.reshape(-1)
        sort_order = jnp.argsort(flat_idx)
        token_ids = sort_order // K
        sorted_x = jnp.take(xf, token_ids, axis=0)
        group_sizes = jnp.bincount(flat_idx, length=E).astype(jnp.int32)
        h0 = jax.lax.ragged_dot(sorted_x, wi_0, group_sizes)
        h1 = jax.lax.ragged_dot(sorted_x, wi_1, group_sizes)
        inter = jax.nn.silu(h0) * h1
        out_sorted = jax.lax.ragged_dot(inter, wo, group_sizes)
        unsort = jnp.argsort(sort_order)
        out = jnp.take(out_sorted, unsort, axis=0).reshape(-1, K, d)
        out = jnp.einsum('tkd,tk->td', out, weights)
        return out.reshape(b, s, d)

    def _L3_xattn_ref(query, key_value, Wq, bq, Wk, bk, Wv, bv, Wo, bo):
        import jax, jax.numpy as jnp
        import numpy as np
        D_MODEL = 512
        NUM_HEADS = 16
        HEAD_DIM = D_MODEL // NUM_HEADS
        B, S, _ = query.shape
        T = key_value.shape[1]
        Q = query @ Wq.T + bq
        K = key_value @ Wk.T + bk
        V = key_value @ Wv.T + bv
        Q = Q.reshape(B, S, NUM_HEADS, HEAD_DIM).transpose(0, 2, 1, 3)
        K = K.reshape(B, T, NUM_HEADS, HEAD_DIM).transpose(0, 2, 1, 3)
        V = V.reshape(B, T, NUM_HEADS, HEAD_DIM).transpose(0, 2, 1, 3)
        scale = 1.0 / np.sqrt(HEAD_DIM).astype(np.float32)
        scores = jnp.einsum('bhsd,bhtd->bhst', Q, K) * scale
        attn = jax.nn.softmax(scores, axis=-1)
        ctx = jnp.einsum('bhst,bhtd->bhsd', attn, V)
        ctx = ctx.transpose(0, 2, 1, 3).reshape(B, S, D_MODEL)
        return ctx @ Wo.T + bo

    def _L3_ffn_ref(hidden_states, gate_w, shared_gate_w, shared_gate_up_w, shared_down_w, w13, w2):
        import jax, jax.numpy as jnp
        import numpy as np
        HIDDEN = 512
        NUM_EXPERTS = 8
        TOP_K = 2
        MOE_INTER = 352
        SHARED_INTER = 1408

        def _silu_and_mul(gu):
            i = gu.shape[-1] // 2
            return jax.nn.silu(gu[:, :i]) * gu[:, i:]
        orig_shape = hidden_states.shape
        x = hidden_states.reshape(-1, orig_shape[-1])
        shared = _silu_and_mul(x @ shared_gate_up_w.T) @ shared_down_w.T
        shared = shared * jax.nn.sigmoid(x @ shared_gate_w.T)
        router_logits = x @ gate_w.T
        probs = jax.nn.softmax(router_logits.astype(jnp.float32), axis=-1)
        routing_weights, selected_experts = jax.lax.top_k(probs, TOP_K)
        combined = jnp.zeros(x.shape, dtype=jnp.float32)
        E = w13.shape[0]
        for e in range(E):
            w_e = jnp.where(selected_experts == e, routing_weights, 0.0).sum(-1)
            h = _silu_and_mul(x @ w13[e].T) @ w2[e].T
            combined = combined + w_e[:, None] * h.astype(jnp.float32)
        out = shared + combined.astype(x.dtype)
        return out.reshape(orig_shape)
    x = x + jnp.tanh(g_xattn[0]) * _L0_xattn_ref(_layernorm(x, axis=-1), ctx_2048, ctx_2048, mask_BxS2_ff1, L0_xattn_Wq, L0_xattn_bq, L0_xattn_Wk, L0_xattn_bk, L0_xattn_Wv, L0_xattn_bv, L0_xattn_Wqf, L0_xattn_Wkf, L0_xattn_Wo, L0_xattn_bo)
    x = x + jnp.tanh(g_ffn[0]) * _L0_ffn_ref(_layernorm(x, axis=-1), L0_ffn_W_up, L0_ffn_W_gate, L0_ffn_W_down)
    x = x + jnp.tanh(g_xattn[1]) * _L1_xattn_ref(_layernorm(x, axis=-1), ctx_2048, mask_BxS2_ik0, L1_xattn_Wq, L1_xattn_bq, L1_xattn_Wk, L1_xattn_bk, L1_xattn_Wv, L1_xattn_bv, L1_xattn_Wo, L1_xattn_bo, L1_xattn_ln_gamma, L1_xattn_ln_beta, L1_xattn_residual_scale)
    x = x + jnp.tanh(g_ffn[1]) * _L1_ffn_ref(_layernorm(x, axis=-1), L1_ffn_Wq, L1_ffn_keys, L1_ffn_e_down, L1_ffn_e_up)
    x = x + jnp.tanh(g_xattn[2]) * _L2_xattn_ref(_layernorm(x, axis=-1), ctx_2048, L2_xattn_wq, L2_xattn_bq, L2_xattn_wkv, L2_xattn_bkv, L2_xattn_wp, L2_xattn_bp)
    x = x + jnp.tanh(g_ffn[2]) * _L2_ffn_ref(_layernorm(x, axis=-1), L2_ffn_w_gate, L2_ffn_wi_0, L2_ffn_wi_1, L2_ffn_wo)
    x = x + jnp.tanh(g_xattn[3]) * _L3_xattn_ref(_layernorm(x, axis=-1), ctx_2048, L3_xattn_Wq, L3_xattn_bq, L3_xattn_Wk, L3_xattn_bk, L3_xattn_Wv, L3_xattn_bv, L3_xattn_Wo, L3_xattn_bo)
    x = x + jnp.tanh(g_ffn[3]) * _L3_ffn_ref(_layernorm(x, axis=-1), L3_ffn_gate_w, L3_ffn_shared_gate_w, L3_ffn_shared_gate_up_w, L3_ffn_shared_down_w, L3_ffn_w13, L3_ffn_w2)
    return x

_drawn_inputs = setup_inputs


def setup_inputs(seed=0):
    import zlib

    import numpy as np

    out = dict(_drawn_inputs(seed))
    spreads = {'L0_xattn_bq': (0.0, 0.534),
     'L0_xattn_bk': (0.0, 0.452),
     'L0_xattn_bv': (0.0, 0.1),
     'L0_xattn_bo': (0.0, 0.1),
     'L1_xattn_bq': (0.0, 0.1),
     'L1_xattn_bk': (0.0, 2.0),
     'L1_xattn_bv': (0.0, 0.1),
     'L1_xattn_bo': (0.0, 0.1),
     'L1_xattn_ln_gamma': (1.0, 0.2),
     'L1_xattn_ln_beta': (0.0, 0.1),
     'L3_xattn_bq': (0.0, 0.79),
     'L3_xattn_bk': (0.0, 2.0),
     'L3_xattn_bv': (0.0, 0.1),
     'L3_xattn_bo': (0.0, 0.1)}
    factors = {'g_ffn': 8.0,
     'L1_ffn_Wq': 5.442,
     'L1_ffn_keys': 6.045,
     'L1_ffn_e_down': 3.03,
     'L1_ffn_e_up': 2.902,
     'L2_xattn_wq': 5.916,
     'L2_xattn_bq': 49.219,
     'L2_xattn_bkv': 4.969,
     'L2_xattn_bp': 2.678,
     'L3_ffn_gate_w': 8.0,
     'L3_ffn_shared_gate_w': 8.0,
     'L3_ffn_shared_gate_up_w': 2.843,
     'L3_ffn_shared_down_w': 2.838,
     'L3_ffn_w13': 8.0,
     'L3_ffn_w2': 8.0}
    for name, (base, spread) in spreads.items():
        noise = np.random.default_rng([zlib.crc32(name.encode()), seed]).standard_normal(out[name].shape)
        drawn = base * np.exp(spread * noise) if base else spread * noise
        out[name] = jnp.asarray(drawn.astype(out[name].dtype))
    for name, factor in factors.items():
        out[name] = (out[name] * factor).astype(out[name].dtype)
    return out
```

```python
from contextlib import ExitStack, contextmanager

import concourse.bass as bass
from concourse import mybir

F32 = mybir.dt.float32
F32R = mybir.dt.float32r
U32 = mybir.dt.uint32
I32 = mybir.dt.int32
ALU = mybir.AluOpType
ACT = mybir.ActivationFunctionType
AX_X = mybir.AxisListType.X

P = 128
D = 512
DC = D // P
BATCH = 2
SEQ = 512
CTX = 1024
TOK = BATCH * SEQ
TILES = TOK // P
HALF = 512
HALVES = TOK // HALF
EPS_LN = 1e-5
EPS_TERNARY = 1e-8
NK = 128
PEER_HEADS = 4


class Env:

    def __init__(self, nc, stack, io):
        self.nc, self.stack, self.io = nc, stack, io
        self.prefix = ""

    def sem(self, name):
        return self.nc.alloc_semaphore(name=f"{self.prefix}_{name}")


def setup_block(env):
    nc, io = env.nc, env.io
    env.prefix = "setup"
    x_loaded, gates_loaded = env.sem("x_loaded"), env.sem("gates_loaded")
    zeroed, made, tanh_done = env.sem("zeroed"), env.sem("made"), env.sem("tanh_done")
    iota_done = env.sem("iota_done")
    iota = env.stack.enter_context(nc.sbuf_tensor("iota", [P, 8], I32))
    with nc.Block() as block:
        @block.sync
        def _(sp):
            sp.dma_start(env.x[:], io["x"].rearrange("b (t p) d -> p (b t) d", p=P)).then_inc(x_loaded, 16)
            sp.dma_start(env.gates[:, 0:4], io["g_xattn"].partition_broadcast(P)).then_inc(gates_loaded, 16)
            sp.dma_start(env.gates[:, 4:8], io["g_ffn"].partition_broadcast(P)).then_inc(gates_loaded, 16)
            sp.wait_ge(x_loaded, 16)

        @block.gpsimd
        def _(pool):
            nc.gpsimd.memset(env.ident[:], 0.0).then_inc(zeroed, 1)
            nc.gpsimd.memset(env.eps_ln[:], EPS_LN).then_inc(made, 1)
            nc.gpsimd.iota(iota[:], pattern=[[1, 8]], base=0, channel_multiplier=0).then_inc(iota_done, 1)
            pool.wait_ge(iota_done, 1)
            nc.gpsimd.tensor_copy(env.iota8[:], iota[:]).then_inc(made, 1)
            pool.wait_ge(zeroed, 1)
            nc.gpsimd.affine_select(out=env.ident[:], in_=env.ident[:], compare_op=ALU.not_equal, fill=1.0,
                                    base=0, pattern=[[-1, P]], channel_multiplier=1).then_inc(made, 1)
            pool.wait_ge(made, 3)

        @block.scalar
        def _(act):
            act.wait_ge(gates_loaded, 32)
            nc.scalar.activation(env.tanh_gates[:], env.gates[:], ACT.Tanh).then_inc(tanh_done, 1)
            act.wait_ge(tanh_done, 1)


def store_block(env, out):
    nc = env.nc
    env.prefix = "store"
    stored = env.sem("stored")
    with nc.Block() as block:
        @block.sync
        def _(sp):
            sp.dma_start(out.rearrange("b (t p) d -> p (b t) d", p=P), env.x[:]).then_inc(stored, 16)
            sp.wait_ge(stored, 16)


def norm_block(env, name, split=None, quantised=False):
    nc = env.nc
    env.prefix = f"{name}_norm"
    stats_done, var_done, sd_done = env.sem("stats_done"), env.sem("var_done"), env.sem("sd_done")
    rstd_done, xn_done, transposed = env.sem("rstd_done"), env.sem("xn_done"), env.sem("transposed")
    copied, high_done, low_done = env.sem("copied"), env.sem("high_done"), env.sem("low_done")
    with ExitStack() as local:
        stats = local.enter_context(nc.sbuf_tensor(f"{name}_stats", [P, TILES, 6], F32))
        meanvar = local.enter_context(nc.sbuf_tensor(f"{name}_meanvar", [P, TILES, 2], F32))
        sd = local.enter_context(nc.sbuf_tensor(f"{name}_sd", [P, TILES], F32))
        rstd = local.enter_context(nc.sbuf_tensor(f"{name}_rstd", [P, TILES], F32))
        xn = local.enter_context(nc.sbuf_tensor(f"{name}_xn", [P, 4, D], F32))
        top = local.enter_context(nc.sbuf_tensor(f"{name}_norm_top", [P, 2], F32))
        tmp = local.enter_context(nc.sbuf_tensor(f"{name}_norm_tmp", [P, D], F32))
        turned = local.enter_context(nc.psum_tensor(f"{name}_turned", [P, 4, DC, P], F32))
        with nc.Block() as block:
            @block.vector
            def _(dve):
                links, count = env.sem("links"), [0]

                def link(ins):
                    count[0] += 1
                    ins.then_inc(links, 1)
                    dve.wait_ge(links, count[0])

                for t in range(TILES):
                    nc.vector.bn_stats(stats[:, t, :], env.x[:, t, :]).then_inc(stats_done, 1)
                for t in range(TILES):
                    dve.wait_ge(stats_done, t + 1)
                    nc.vector.bn_aggr(meanvar[:, t, :], stats[:, t, :]).then_inc(var_done, 1)
                dve.wait_ge(sd_done, 1)
                nc.vector.reciprocal(rstd[:], sd[:]).then_inc(rstd_done, 1)
                dve.wait_ge(rstd_done, 1)
                for t in range(TILES):
                    if t >= 4:
                        dve.wait_ge(transposed, t - 3)
                    row = xn[:, t % 4, :]
                    last = nc.vector.tensor_scalar(row, env.x[:, t, :], meanvar[:, t, 0:1], rstd[:, t:t + 1],
                                                   ALU.subtract, ALU.mult)
                    if quantised:
                        link(last)
                        quantise_rows(nc, link, row, row, top, tmp[:])
                        dve.sem_inc(xn_done, 1)
                    else:
                        last.then_inc(xn_done, 1)
                if split:
                    high, low = split
                    for t in range(TILES):
                        cols = slice(t * P, (t + 1) * P)
                        dve.wait_ge(copied, t + 1)
                        dve.wait_ge(high_done, t + 1)
                        nc.vector.tensor_tensor(low[:, :, cols], env.xT[:, :, cols], high[:, :, cols].bitcast(F32),
                                                ALU.subtract).then_inc(low_done, 1)
                    dve.wait_ge(low_done, TILES)

            @block.tensor
            def _(pe):
                for t in range(TILES):
                    pe.wait_ge(xn_done, t + 1)
                    if t >= 4:
                        pe.wait_ge(copied, t - 3)
                    for c in range(DC):
                        last = nc.tensor.transpose(turned[:, t % 4, c, :], xn[:, t % 4, c * P:(c + 1) * P], env.ident[:])
                    last.then_inc(transposed, 1)

            @block.scalar
            def _(act):
                act.wait_ge(var_done, TILES)
                nc.scalar.activation(sd[:], meanvar[:, :, 1], ACT.Sqrt, bias=env.eps_ln[:]).then_inc(sd_done, 1)
                for t in range(TILES):
                    act.wait_ge(transposed, t + 1)
                    cols = slice(t * P, (t + 1) * P)
                    nc.scalar.copy(env.xT[:, :, cols], turned[:, t % 4]).then_inc(copied, 1)
                    if split:
                        act.wait_ge(copied, t + 1)
                        nc.scalar.copy(split[0][:, :, cols], env.xT[:, :, cols]).then_inc(high_done, 1)
                act.wait_ge(copied, TILES)


def ternary_scales(env, name, scale, half, neg_half, gate, weight):
    nc, io = env.nc, env.io
    env.prefix = f"{name}_scales"
    G, E = io["w1"].shape[0], io["w1"].shape[2] // DC
    elements = G * E * D
    loaded = [env.sem(f"loaded{s}") for s in range(3)]
    summed, total_done, used = env.sem("summed"), env.sem("total_done"), env.sem("used")
    ones_made, steps, scaled = env.sem("ones_made"), env.sem("steps"), env.sem("scaled")
    with ExitStack() as local:
        raw = local.enter_context(nc.sbuf_tensor(f"{name}_absw", [P, 3, G * E * D // P], F32))
        partial = local.enter_context(nc.sbuf_tensor(f"{name}_partial", [P, 3], F32))
        ones = local.enter_context(nc.sbuf_tensor(f"{name}_ones", [P, P], F32))
        total = local.enter_context(nc.psum_tensor(f"{name}_total", [P, 512], F32))
        with nc.Block() as block:
            @block.sync
            def _(sp):
                for m, w in enumerate(("w1", "w2")):
                    sp.dma_start(raw[:, m, :].rearrange("p (g n) -> p g n", g=G),
                                 io[w].rearrange("g p n -> p g n")).then_inc(loaded[m], 16)
                sp.dma_start(raw[:, 2, :].rearrange("p (r n) -> p r n", n=D),
                             io["w3"].rearrange("g (r p) n -> p (g r) n", p=P)).then_inc(loaded[2], 16)

            @block.vector
            def _(dve):
                nc.vector.memset(ones[:], 1.0).then_inc(ones_made, 1)
                for m in range(3):
                    dve.wait_ge(loaded[m], 16)
                    nc.vector.tensor_reduce(partial[:, m:m + 1], raw[:, m, :], AX_X, ALU.add,
                                            apply_absolute_value=True).then_inc(summed, 1)
                dve.wait_ge(total_done, 1)
                nc.vector.tensor_scalar(scale[:], total[:, 0:3], 1.0 / elements, EPS_TERNARY, ALU.mult,
                                        ALU.add).then_inc(scaled, 1)
                dve.wait_ge(scaled, 1)
                nc.vector.tensor_scalar(half[:], scale[:], 0.5, None, ALU.mult).then_inc(scaled, 1)
                nc.vector.tensor_scalar(neg_half[:], scale[:], -0.5, None, ALU.mult).then_inc(scaled, 1)
                dve.wait_ge(scaled, 3)
                nc.vector.tensor_scalar(weight[:], scale[:, 1:2], scale[:, 2:3], gate, ALU.mult, ALU.mult).then_inc(scaled, 1)
                dve.wait_ge(scaled, 4)

            @block.tensor
            def _(pe):
                pe.wait_ge(ones_made, 1)
                pe.wait_ge(summed, 3)
                nc.tensor.matmul(total[:, 0:3], ones[:], partial[:], start=True, stop=True).then_inc(total_done, 1)


def ffn_block(env, name, chunks, weight, ternary=None, peer=None):
    nc, io = env.nc, env.io
    env.prefix = name
    w1, w2, w3 = io["w1"], io.get("w2"), io["w3"]
    G, E = w1.shape[0], w1.shape[2] // DC
    NCH = len(chunks)
    starts = [sum(chunks[:c]) for c in range(NCH)]
    FULL = E // P
    STEPS = NCH * HALVES
    PAIRS = 2
    YB = 4
    SIDES = 1 if peer else 2
    UP_INC, DOWN_INC = 16 * SIDES, 16 * (bool(FULL) + bool(E % P))
    ADDS = TILES * (PEER_HEADS - 1) + 1
    assert G % 2 == 0
    up_loaded = [env.sem(f"up_loaded{s}") for s in range(2)]
    down_loaded = [env.sem(f"down_loaded{s}") for s in range(2)]
    hidden_psum, silu_done = env.sem("hidden_psum"), env.sem("silu_done")
    hidden_done = env.sem("hidden_done")
    y_done = env.sem("y_done")
    y_used = env.sem("y_used")
    if ternary:
        product_done, high_done = env.sem("product_done"), env.sem("high_done")
        sign_done = env.sem("sign_done")
        up_quantised, down_quantised = env.sem("up_quantised"), env.sem("down_quantised")
    if peer:
        sums_done, added = env.sem("sums_done"), env.sem("added")
        kept_done = env.sem("kept_done")
    with ExitStack() as local:
        def sb(n, shape, dt=F32):
            return local.enter_context(nc.sbuf_tensor(f"{name}_{n}", shape, dt))

        up_in = sb("up_in", [P, 2, SIDES, DC * E])
        down_in = sb("down_in", [P, 2, NCH, D])
        if ternary:
            xh, xl, scale, half, neg_half = ternary
            up_w, down_w = sb("up_q", [P, 2, SIDES, DC * E], F32R), sb("down_q", [P, 2, NCH, D], F32R)
            low_sign = sb("low_sign", [P, DC * E])
            h_parts = [sb("h_high", [P, 2, NCH, TOK], F32R), sb("h_low", [P, 2, NCH, TOK], F32R)]
            product = sb("product", [P, PAIRS, HALF])
            x_parts = [xh, xl]
        else:
            up_w, down_w = up_in, down_in
            h_parts = [sb("h", [P, 2, NCH, TOK])]
            x_parts = [env.xT]
        silu_sb = sb("silu", [P, PAIRS, HALF])
        if peer:
            sims, bar, extra = peer
            I1 = E // NK
            routes = sb("routes", [P, 2, TILES, E])
            sums = sb("sums", [P, 2, E])
            kept = sb("kept", [P, 2, E])
        hidden_ps = local.enter_context(nc.psum_tensor(f"{name}_hidden", [P, PAIRS, 2, HALF], F32))
        y_ps = local.enter_context(nc.psum_tensor(f"{name}_y", [P, YB, D], F32))

        with nc.Block() as block:
            @block.sync
            def _(sp):
                def load_up(g, s):
                    for side, w in enumerate((w1, w2)[:SIDES]):
                        sp.dma_start(up_in[:, s, side, :], w[bass.ds(g, 1)].rearrange("g p n -> p (g n)")).then_inc(
                            up_loaded[s], 16)

                def load_down(g, s):
                    if FULL:
                        sp.dma_start(down_in[:, s, 0:FULL, :],
                                     w3[bass.ds(g, 1), 0:FULL * P, :].rearrange("g (c p) n -> p (g c) n", p=P)).then_inc(
                                         down_loaded[s], 16)
                    if E % P:
                        sp.dma_start(down_in[0:E % P, s, FULL, :],
                                     w3[bass.ds(g, 1), FULL * P:E, :].rearrange("g p n -> p (g n)")).then_inc(
                                         down_loaded[s], 16)

                for g in range(2):
                    load_up(g, g)
                    load_down(g, g)
                with sp.Fori(1, G // 2) as j:
                    for s in range(2):
                        g = 2 * j + s
                        if ternary:
                            sp.wait_ge(up_quantised, 2 * (g - 1))
                            load_up(g, s)
                            sp.wait_ge(down_quantised, g - 1)
                            load_down(g, s)
                        else:
                            sp.wait_ge(hidden_done, PAIRS + (g - 1) * STEPS)
                            load_up(g, s)
                            sp.wait_ge(y_used, g * TILES)
                            load_down(g, s)

            @block.tensor
            def _(pe):
                def up(g, s, j):
                    if ternary:
                        pe.wait_ge(up_quantised, 2 * (g + 1))
                    else:
                        pe.wait_ge(up_loaded[s], UP_INC * (j + 1))
                    if peer:
                        pe.wait_ge(added, ADDS * (g + 1))
                    for k in range(STEPS):
                        c, h, b = k // HALVES, k % HALVES, k % PAIRS
                        m, e0 = chunks[c], starts[c]
                        pe.wait_ge(hidden_done, g * STEPS + k + 1)
                        for side in range(SIDES):
                            w = up_w[:, s, side].rearrange("p (c e) -> p c e", c=DC)
                            for i in range(DC):
                                for n, xp in enumerate(x_parts):
                                    last = nc.tensor.matmul(hidden_ps[0:m, b, side, :], w[:, i, e0:e0 + m],
                                                            xp[:, i, h * HALF:(h + 1) * HALF],
                                                            start=(i == 0 and n == 0),
                                                            stop=(i == DC - 1 and n == len(x_parts) - 1))
                        if peer:
                            for t in range(HALF // P):
                                last = nc.tensor.transpose(hidden_ps[:, b, 1, t * P:(t + 1) * P],
                                                           routes[:, s, h * (HALF // P) + t, c * P:(c + 1) * P],
                                                           env.ident[:])
                        last.then_inc(hidden_psum, 1)

                def down(g, s, j):
                    pe.wait_ge(hidden_done, PAIRS + (g + 1) * STEPS)
                    if ternary:
                        pe.wait_ge(down_quantised, g + 1)
                    else:
                        pe.wait_ge(down_loaded[s], DOWN_INC * (j + 1))
                    terms = [(c, hp) for c in range(NCH) for hp in h_parts]
                    for t in range(TILES):
                        pe.wait_ge(y_used, g * TILES + t + 1 + TILES - YB)
                        for n, (c, hp) in enumerate(terms):
                            m = chunks[c]
                            last = nc.tensor.matmul(y_ps[:, t % YB, :], hp[0:m, s, c, t * P:(t + 1) * P],
                                                    down_w[0:m, s, c, :], start=(n == 0), stop=(n == len(terms) - 1))
                        last.then_inc(y_done, 1)

                up(0, 0, 0)
                with pe.Fori(0, G // 2 - 1) as j:
                    up(2 * j + 1, 1, j)
                    down(2 * j, 0, j)
                    up(2 * j + 2, 0, j + 1)
                    down(2 * j + 1, 1, j)
                up(G - 1, 1, G // 2 - 1)
                down(G - 2, 0, G // 2 - 1)
                down(G - 1, 1, G // 2 - 1)

            @block.scalar
            def _(act):
                with act.Fori(0, G) as g:
                    for k in range(STEPS):
                        m, b = chunks[k // HALVES], k % PAIRS
                        act.wait_ge(hidden_psum, g * STEPS + k + 1)
                        act.wait_ge(hidden_done, g * STEPS + k + 1)
                        nc.scalar.activation(silu_sb[0:m, b, :], hidden_ps[0:m, b, 0, :], ACT.Silu,
                                             scale=scale[0:m, 0:1] if ternary else 1.0).then_inc(silu_done, 1)

            if peer:
                @block.gpsimd
                def _(pool):
                    with pool.Fori(0, G) as g:
                        for t in range(TILES):
                            for h in range(PEER_HEADS):
                                n = t * PEER_HEADS + h
                                pool.wait_ge(kept_done, g * TILES * PEER_HEADS + n + 1)
                                first = sims[:, t, h, bass.ds(g * I1, I1)].unsqueeze(2).to_broadcast([P, I1, NK])
                                second = sims[:, t, h, NK:2 * NK].unsqueeze(1).to_broadcast([P, I1, NK])
                                nc.gpsimd.tensor_tensor(sums[:, n % 2, :].rearrange("p (a b) -> p a b", a=I1),
                                                        first, second, ALU.add).then_inc(sums_done, 1)

            @block.vector
            def _(dve):
                def hidden(g, s, k):
                    c, h, b = k // HALVES, k % HALVES, k % PAIRS
                    m, cols, n = chunks[c], slice(h * HALF, (h + 1) * HALF), g * STEPS + k + 1
                    dve.wait_ge(silu_done, n)
                    out = product[0:m, b, :] if ternary else h_parts[0][0:m, s, c, cols]
                    nc.vector.tensor_tensor(out, silu_sb[0:m, b, :], hidden_ps[0:m, b, 1, :], ALU.mult).then_inc(
                        product_done if ternary else hidden_done, 1)
                    if ternary:
                        high, low = (hp[0:m, s, c, cols] for hp in h_parts)
                        dve.wait_ge(product_done, n)
                        nc.vector.tensor_copy(high, out).then_inc(high_done, 1)
                        dve.wait_ge(high_done, n)
                        nc.vector.tensor_tensor(low, out, high.bitcast(F32), ALU.subtract).then_inc(hidden_done, 1)

                def outputs(g):
                    for t in range(TILES):
                        w = weight[:, 0:1] if len(weight.shape) == 2 else weight[:, t, bass.ds(g, 1)]
                        dve.wait_ge(y_done, g * TILES + t + 1)
                        dve.wait_ge(y_used, g * TILES + t + 1)
                        nc.vector.scalar_tensor_tensor(env.x[:, t, :], y_ps[:, t % YB, :], w, env.x[:, t, :],
                                                       ALU.mult, ALU.add).then_inc(y_used, 1)

                def quantise_up(g, s, j):
                    dve.wait_ge(up_loaded[s], UP_INC * (j + 1))
                    for side in range(SIDES):
                        nc.vector.tensor_scalar(low_sign[:], up_in[:, s, side, :], neg_half[:, side:side + 1], None,
                                                ALU.is_lt).then_inc(sign_done, 1)
                        dve.wait_ge(sign_done, 3 * g + side + 1)
                        nc.vector.scalar_tensor_tensor(up_w[:, s, side, :], up_in[:, s, side, :], half[:, side:side + 1],
                                                       low_sign[:], ALU.is_gt, ALU.subtract).then_inc(up_quantised, 1)
                        dve.wait_ge(up_quantised, 2 * g + side + 1)

                def quantise_down(g, s, j):
                    dve.wait_ge(down_loaded[s], DOWN_INC * (j + 1))
                    src = down_in[:, s].rearrange("p c e -> p (c e)")
                    nc.vector.tensor_scalar(low_sign[:], src, neg_half[:, 2:3], None, ALU.is_lt).then_inc(sign_done, 1)
                    dve.wait_ge(sign_done, 3 * g + 3)
                    nc.vector.scalar_tensor_tensor(down_w[:, s].rearrange("p c e -> p (c e)"), src, half[:, 2:3],
                                                   low_sign[:], ALU.is_gt, ALU.subtract).then_inc(down_quantised, 1)
                    dve.wait_ge(down_quantised, g + 1)

                def routes_tile(g, s, t):
                    row = routes[:, s, t, :]
                    for h in range(PEER_HEADS):
                        n = t * PEER_HEADS + h
                        n_all = g * TILES * PEER_HEADS + n
                        b = bar[:, n:n + 1]
                        dve.wait_ge(sums_done, n_all + 1)
                        to = kept[:, n % 2, :] if h else row
                        nc.vector.scalar_tensor_tensor(to, sums[:, n % 2, :], b, sums[:, n % 2, :], ALU.is_ge,
                                                       ALU.mult).then_inc(kept_done, 1)
                        dve.wait_ge(kept_done, 2 + n_all + 1)
                        if h:
                            nc.vector.tensor_tensor(row, row, kept[:, n % 2, :], ALU.add).then_inc(added, 1)
                            dve.wait_ge(added, g * ADDS + t * (PEER_HEADS - 1) + h)

                def routes_end(g, s):
                    nc.vector.tensor_tensor(routes[:, s, :, E - 1], routes[:, s, :, E - 1],
                                            extra[:, bass.ds(g, 1), :].rearrange("p g t -> p (g t)"), ALU.add).then_inc(
                                                added, 1)

                dve.sem_inc(hidden_done, PAIRS)
                dve.sem_inc(y_used, TILES)
                if peer:
                    dve.sem_inc(kept_done, 2)

                def prepare_down(g, s, j):
                    if ternary:
                        quantise_down(g, s, j)

                def next_and_hidden(g, s, j):
                    for k in range(STEPS):
                        if peer:
                            routes_tile(g + 1, 1 - s, k)
                        hidden(g, s, k)
                    if peer:
                        routes_end(g + 1, 1 - s)
                    if ternary:
                        quantise_up(g + 1, 1 - s, j + s)

                if peer:
                    for t in range(TILES):
                        routes_tile(0, 0, t)
                    routes_end(0, 0)
                if ternary:
                    quantise_up(0, 0, 0)
                    quantise_down(0, 0, 0)
                next_and_hidden(0, 0, 0)
                prepare_down(1, 1, 0)
                with dve.Fori(0, G // 2 - 1) as j:
                    next_and_hidden(2 * j + 1, 1, j)
                    outputs(2 * j)
                    prepare_down(2 * j + 2, 0, j + 1)
                    next_and_hidden(2 * j + 2, 0, j + 1)
                    outputs(2 * j + 1)
                    prepare_down(2 * j + 3, 1, j + 1)
                for k in range(STEPS):
                    hidden(G - 1, 1, k)
                outputs(G - 2)
                outputs(G - 1)
                dve.wait_ge(y_used, TILES + G * TILES)


def expert_weights_block(env, name, G, shared, normalise, gate, weight):
    nc, io = env.nc, env.io
    env.prefix = f"{name}_experts"
    EX = 8
    N = EX + (1 if shared else 0)
    loaded, logits_done, step, exp_done = env.sem("loaded"), env.sem("logits_done"), env.sem("step"), env.sem("exp_done")
    with ExitStack() as local:
        def sb(n, shape, dt=F32):
            return local.enter_context(nc.sbuf_tensor(f"{name}_{n}", shape, dt))

        w = sb("router", [P, DC, N])
        logits, top, index = sb("logits", [P, TILES, N]), sb("top", [P, TILES, 8]), sb("index", [P, TILES, 8], U32)
        index_f, less_max, exps = sb("index_f", [P, TILES, 8]), sb("less_max", [P, TILES, 9]), sb("exps", [P, TILES, 9])
        total, inv, pick = sb("total", [P, TILES, 2]), sb("inv", [P, TILES, 2]), sb("pick", [P, 2, TILES, EX])
        ps = local.enter_context(nc.psum_tensor(f"{name}_router_ps", [P, TILES, 16], F32))
        with nc.Block() as block:
            @block.sync
            def _(sp):
                sp.dma_start(w[:], io["router"]).then_inc(loaded, 16)

            @block.tensor
            def _(pe):
                pe.wait_ge(loaded, 16)
                for t in range(TILES):
                    for i in range(DC):
                        last = nc.tensor.matmul(ps[:, t, 0:N], env.xT[:, i, t * P:(t + 1) * P], w[:, i, :],
                                                start=(i == 0), stop=(i == DC - 1))
                last.then_inc(logits_done, 1)

            @block.scalar
            def _(act):
                act.wait_ge(step, 1)
                nc.scalar.activation(exps[:, :, 0:N], less_max[:, :, 0:N], ACT.Exp).then_inc(exp_done, 1)

            @block.vector
            def _(dve):
                links = env.sem("links")
                count = [0]

                def link(ins):
                    count[0] += 1
                    ins.then_inc(links, 1)
                    dve.wait_ge(links, count[0])

                def spread(ap, n=EX):
                    return ap.to_broadcast([P, TILES, n])

                dve.wait_ge(logits_done, 1)
                link(nc.vector.tensor_copy(logits[:], ps[:, :, 0:N]))
                for t in range(TILES):
                    link(nc.vector.max(top[:, t, :], logits[:, t, 0:EX]))
                    link(nc.vector.max_index(index[:, t, :], top[:, t, :], logits[:, t, 0:EX]))
                link(nc.vector.tensor_copy(index_f[:], index[:]))
                link(nc.vector.tensor_tensor(less_max[:, :, 0:EX], top[:], spread(top[:, :, 0:1]), ALU.subtract))
                if shared:
                    link(nc.vector.tensor_scalar(less_max[:, :, EX:N], logits[:, :, EX:N], -1.0, None, ALU.mult))
                dve.sem_inc(step, 1)
                dve.wait_ge(exp_done, 1)
                link(nc.vector.tensor_reduce(total[:, :, 0], exps[:, :, 0:2 if normalise else EX], AX_X, ALU.add))
                if shared:
                    link(nc.vector.tensor_scalar(total[:, :, 1:2], exps[:, :, EX:N], 1.0, None, ALU.add))
                n = 2 if shared else 1
                link(nc.vector.reciprocal(inv[:, :, 0:n], total[:, :, 0:n]))
                for p in range(2):
                    link(nc.vector.tensor_tensor(pick[:, p], spread(index_f[:, :, p:p + 1]),
                                                 env.iota8[:].unsqueeze(1).to_broadcast([P, TILES, EX]), ALU.is_equal))
                    link(nc.vector.tensor_tensor(pick[:, p], pick[:, p], spread(exps[:, :, p:p + 1]), ALU.mult))
                link(nc.vector.tensor_tensor(pick[:, 0], pick[:, 0], pick[:, 1], ALU.add))
                link(nc.vector.tensor_tensor(pick[:, 1], pick[:, 0], spread(inv[:, :, 0:1]), ALU.mult))
                link(nc.vector.tensor_scalar(weight[:, :, shared:G], pick[:, 1], gate, None, ALU.mult))
                if shared:
                    link(nc.vector.tensor_scalar(weight[:, :, 0:shared], spread(inv[:, :, 1:2], shared), gate, None,
                                                 ALU.mult))


def product_keys_block(env, name, sims, bar, extra, G):
    nc, io = env.nc, env.io
    env.prefix = f"{name}_keys"
    H, ROWS = PEER_HEADS, 32
    wq_loaded, keys_loaded, keys_clear = env.sem("wq_loaded"), env.sem("keys_loaded"), env.sem("keys_clear")
    q_psum, q_done, sims_psum, sims_done = env.sem("q_psum"), env.sem("q_done"), env.sem("sims_psum"), env.sem("sims_done")
    with ExitStack() as local:
        def sb(n, shape, dt=F32):
            return local.enter_context(nc.sbuf_tensor(f"{name}_{n}", shape, dt))

        wq, keys, qT = sb("wq", [P, DC, D]), sb("keys", [P, H, 2 * NK]), sb("qT", [P, H, TOK])
        best, index = sb("best", [P, 2, H, 2, 8]), sb("index", [P, 2, H, 8], U32)
        past, pairs, top = sb("past", [P, H, 8]), sb("pairs", [P, H, 8, 8]), sb("top", [P, H, 8])
        reach = sb("reach", [P, H, 8, 8])
        q_ps = local.enter_context(nc.psum_tensor(f"{name}_q_ps", [P, 4, HALF], F32))
        sims_ps = local.enter_context(nc.psum_tensor(f"{name}_sims_ps", [P, 2, H, 2 * NK], F32))
        with nc.Block() as block:
            @block.sync
            def _(sp):
                sp.dma_start(wq[:], io["wq"]).then_inc(wq_loaded, 16)
                sp.wait_ge(keys_clear, 1)
                for side in range(2):
                    sp.dma_start(keys[64 * side:64 * side + 64, :, side * NK:(side + 1) * NK],
                                 io["keys"][:, side]).then_inc(keys_loaded, 16)

            @block.tensor
            def _(pe):
                pe.wait_ge(wq_loaded, 16)
                for n in range(H * HALVES):
                    f, h = n // HALVES, n % HALVES
                    if n >= 4:
                        pe.wait_ge(q_done, n - 3)
                    for i in range(DC):
                        last = nc.tensor.matmul(q_ps[:, n % 4, :], wq[:, i, f * P:(f + 1) * P],
                                                env.xT[:, i, h * HALF:(h + 1) * HALF], start=(i == 0), stop=(i == DC - 1))
                    last.then_inc(q_psum, 1)
                pe.wait_ge(keys_loaded, 32)
                pe.wait_ge(q_done, H * HALVES)
                for t in range(TILES):
                    if t >= 2:
                        pe.wait_ge(sims_done, t - 1)
                    for f in range(H):
                        last = nc.tensor.matmul(sims_ps[:, t % 2, f, :], qT[:, f, t * P:(t + 1) * P], keys[:, f, :],
                                                start=True, stop=True)
                    last.then_inc(sims_psum, 1)

            @block.scalar
            def _(act):
                for n in range(H * HALVES):
                    f, h = n // HALVES, n % HALVES
                    act.wait_ge(q_psum, n + 1)
                    nc.scalar.copy(qT[:, f, h * HALF:(h + 1) * HALF], q_ps[:, n % 4, :]).then_inc(q_done, 1)
                for t in range(TILES):
                    act.wait_ge(sims_psum, t + 1)
                    nc.scalar.copy(sims[:, t], sims_ps[:, t % 2]).then_inc(sims_done, 1)

            @block.vector
            def _(dve):
                links = env.sem("links")
                count = [0]

                def link(ins, wait=True):
                    count[0] += 1
                    ins.then_inc(links, 1)
                    if wait:
                        dve.wait_ge(links, count[0])

                nc.vector.memset(keys[:], 0.0).then_inc(keys_clear, 1)
                link(nc.vector.memset(extra[:], 0.0))
                for t in range(TILES):
                    u = t % 2
                    dve.wait_ge(sims_done, t + 1)
                    for f in range(H):
                        for side in range(2):
                            link(nc.vector.max(best[:, u, f, side, :], sims[:, t, f, side * NK:(side + 1) * NK]),
                                 wait=(f == H - 1 and side == 1))
                    for f in range(H):
                        link(nc.vector.max_index(index[:, u, f, :], best[:, u, f, 0, :], sims[:, t, f, 0:NK]), wait=False)
                        link(nc.vector.tensor_tensor(pairs[:, f],
                                                     best[:, u, f, 0, :].unsqueeze(2).to_broadcast([P, 8, 8]),
                                                     best[:, u, f, 1, :].unsqueeze(1).to_broadcast([P, 8, 8]), ALU.add),
                             wait=(f == H - 1))
                    for f in range(H):
                        link(nc.vector.max(top[:, f, :], pairs[:, f].rearrange("p a b -> p (a b)")), wait=(f == H - 1))
                    link(nc.vector.tensor_scalar(bar[:, t * H:(t + 1) * H], top[:, :, 7], 0.0, None, ALU.max), wait=False)
                    link(nc.vector.tensor_scalar(past[:], index[:, u], ROWS - 0.5, None, ALU.is_gt))
                    for f in range(H):
                        b = bar[:, t * H + f:t * H + f + 1]
                        flat = pairs[:, f].rearrange("p a b -> p (a b)")
                        link(nc.vector.scalar_tensor_tensor(reach[:, f].rearrange("p a b -> p (a b)"), flat, b, flat,
                                                            ALU.is_ge, ALU.mult), wait=(f == H - 1))
                    link(nc.vector.tensor_tensor(reach[:].rearrange("p f a b -> p (f a) b"),
                                                 reach[:].rearrange("p f a b -> p (f a) b"),
                                                 past[:].rearrange("p f a -> p (f a)").unsqueeze(2).to_broadcast([P, H * 8, 8]),
                                                 ALU.mult))
                    link(nc.vector.tensor_reduce(extra[:, G - 1, t:t + 1], reach[:].rearrange("p f a b -> p (f a b)"),
                                                 AX_X, ALU.add))


def softmax_attention_block(env, name, heads_out, keep_mask=None):
    nc, io = env.nc, env.io
    env.prefix = f"{name}_attn"
    bounded = keep_mask is not None
    HEADS, HD = 16, 32
    FG, HG = 4, 4
    VC = HD + 1
    KT, QT = CTX // P, SEQ // P
    CT = BATCH * KT
    SCALE = HD ** -0.5
    BOUND = 50.0
    UNITS = HG * (KT if bounded else QT)
    PRODUCTS = CTX // HALF + 1
    S_SLOTS, O_SLOTS, P_SLOTS = (3, 4, 1) if bounded else (2, 2, 2)
    ctx_loaded, wv_loaded, w_loaded = (env.sem("ctx_loaded"), env.sem("wv_loaded"),
                                       env.sem("w_loaded"))
    ones_made, v_psum, v_done = env.sem("ones_made"), env.sem("v_psum"), env.sem("v_done")
    proj_psum, high_done, low_done = env.sem("proj_psum"), env.sem("high_done"), env.sem("low_done")
    k_stacked, q_stacked, group_done = env.sem("k_stacked"), env.sem("q_stacked"), env.sem("group_done")
    scores_done, exp_done = env.sem("scores_done"), env.sem("exp_done")
    pv_done, norm_done, inv_done = env.sem("pv_done"), env.sem("norm_done"), env.sem("inv_done")
    if bounded:
        clipped = env.sem("clipped")
    else:
        max_done, bias_done = env.sem("max_done"), env.sem("bias_done")
        turned = [env.sem(f"turned{i}") for i in range(2)]
        copied = [env.sem(f"copied{i}") for i in range(2)]
    with ExitStack() as local:
        def sb(n, shape, dt=F32):
            return local.enter_context(nc.sbuf_tensor(f"{name}_{n}", shape, dt))

        def psum(n, shape):
            return local.enter_context(nc.psum_tensor(f"{name}_{n}", shape, F32))

        ctxT = sb("ctxT", [P, DC, BATCH * CTX])
        values = sb("values", [P, CT, HEADS, VC])
        k_stack, q_stack = sb("k_stack", [P, 2, HG, CTX], F32R), sb("q_stack", [P, 2, HG, SEQ], F32R)
        kh, kl = sb("kh", [P, CTX], F32R), sb("kl", [P, CTX], F32R)
        qh, ql = sb("qh", [P, SEQ], F32R), sb("ql", [P, SEQ], F32R)
        wk, wq = sb("wk", [P, DC * P]), sb("wq", [P, DC * P])
        bk, bq = sb("bk", [P, 1]), sb("bq", [P, 1])
        probs, probsT = sb("probs", [P, 2, CTX]), sb("probsT", [P, 2, KT * P])
        wv = probs[:].rearrange("p a (b n) -> p (a b) n", n=D)
        bv = probsT[:, 0, 0:D]
        inv = sb("inv", [P, 2, HG, 1])
        small = sb("small", [P, 2, 2])
        o_ps = psum("o_ps", [P, O_SLOTS, HALF])
        s_ps = psum("s_ps", [P, S_SLOTS, HALF if bounded else CTX])
        t_ps = psum("t_ps", [P, P_SLOTS, HALF])

        pT4 = probsT[:].rearrange("p a (b n) -> p (a b) n", n=SEQ)

        with nc.Block() as block:
            @block.sync
            def _(sp):
                sp.dma_start(wv, io["wv"]).then_inc(wv_loaded, 16)
                sp.dma_start(bv, io["bv"].partition_broadcast(P)).then_inc(wv_loaded, 16)
                for b in range(BATCH):
                    sp.dma_start(ctxT[:, :, b * CTX:(b + 1) * CTX], io["ctxT"][:, :, b * CTX:(b + 1) * CTX]).then_inc(
                        ctx_loaded, 16)
                    sp.wait_ge(ctx_loaded, 16 * (b + 1))

                def load_weights(f):
                    for to, of in ((wk, "wk"), (wq, "wq"), (bk, "bk"), (bq, "bq")):
                        sp.dma_start(to[:], io[of][bass.ds(f, 1)].rearrange("g p n -> p (g n)")).then_inc(w_loaded, 16)

                def stack(n, s):
                    if not isinstance(n, int) or n >= 2:
                        sp.wait_ge(group_done, n - 1)
                    for what, (dst, halves, sem) in enumerate(((k_stack, (kh, kl, kh, kl), k_stacked),
                                                               (q_stack, (qh, qh, ql, ql), q_stacked))):
                        sp.wait_ge(low_done, P_SLOTS + PRODUCTS * n + (PRODUCTS - 1 if what == 0 else PRODUCTS))
                        for r in range(4):
                            for h in range(HG):
                                sp.dma_start(dst[32 * r:32 * r + 32, s, h, :].bitcast(F32),
                                             halves[r][32 * h:32 * h + 32, :].bitcast(F32)).then_inc(sem, 16)

                load_weights(0)
                stack(0, 0)
                with sp.Fori(0, FG - 1) as f:
                    stack(2 * f + 1, 1)
                    load_weights(f + 1)
                    stack(2 * f + 2, 0)
                stack(2 * FG - 1, 1)

            STACKS = 16 * 16

            @block.tensor
            def _(pe):
                pe.wait_ge(wv_loaded, 32)
                for t in range(CT):
                    pe.wait_ge(ctx_loaded, 16 * (t // KT + 1))
                    if t >= S_SLOTS:
                        pe.wait_ge(v_done, t - S_SLOTS + 1)
                    for i in range(DC):
                        last = nc.tensor.matmul(s_ps[:, t % S_SLOTS, 0:D], ctxT[:, i, t * P:(t + 1) * P], wv[:, i, :],
                                                start=(i == 0), stop=(i == DC - 1))
                    last.then_inc(v_psum, 1)

                def project(f, b):
                    n = 2 * f + b
                    pe.wait_ge(w_loaded, 64 * (f + 1))
                    for i in range(PRODUCTS):
                        w, moving = (wk, ctxT[:, :, b * CTX + i * HALF:b * CTX + (i + 1) * HALF]) if i < PRODUCTS - 1 \
                            else (wq, env.xT[:, :, b * SEQ:(b + 1) * SEQ])
                        pe.wait_ge(low_done, PRODUCTS * n + i + 1)
                        for c in range(DC):
                            last = nc.tensor.matmul(t_ps[:, (PRODUCTS * b + i) % P_SLOTS, :], w[:, c * P:(c + 1) * P], moving[:, c, :],
                                                    start=(c == 0), stop=(c == DC - 1))
                        last.then_inc(proj_psum, 1)

                def attend(f, b):
                    n = 2 * f + b
                    pe.wait_ge(k_stacked, STACKS * (n + 1))
                    pe.wait_ge(q_stacked, STACKS * (n + 1))
                    if not bounded:
                        ahead = n + 1 if isinstance(n, int) and n == 2 * FG - 1 else n + 2
                        pe.wait_ge(low_done, P_SLOTS + PRODUCTS * ahead)

                    def value(h, kt):
                        return values[:, b * KT + kt, bass.ds(HG * f + h, 1), :].rearrange("p a e -> p (a e)")

                    def bounded_scores(u):
                        h, kt = u // KT, u % KT
                        pe.wait_ge(clipped, UNITS * n + u + 1)
                        nc.tensor.matmul(s_ps[:, u % S_SLOTS, :], k_stack[:, b, h, kt * P:(kt + 1) * P], q_stack[:, b, h, :],
                                         start=True, stop=True).then_inc(scores_done, 1)

                    def bounded_pv(u):
                        h, kt = u // KT, u % KT
                        pe.wait_ge(exp_done, UNITS * n + u + 1 + 2)
                        if u == 0:
                            pe.wait_ge(norm_done, QT * (n + 1))
                        for q in range(QT):
                            last = nc.tensor.matmul(o_ps[:, q, h * VC:(h + 1) * VC],
                                                    pT4[:, u % 4, q * P:(q + 1) * P], value(h, kt),
                                                    start=(kt == 0), stop=(kt == KT - 1))
                        last.then_inc(pv_done, 1)

                    def scores(u):
                        q, h = u // HG, u % HG
                        pe.wait_ge(exp_done, UNITS * n + u + 1)
                        for i in range(CTX // HALF):
                            last = nc.tensor.matmul(s_ps[:, u % 2, i * HALF:(i + 1) * HALF],
                                                    q_stack[:, b, h, q * P:(q + 1) * P],
                                                    k_stack[:, b, h, i * HALF:(i + 1) * HALF], start=True, stop=True)
                        last.then_inc(scores_done, 1)

                    def turn(u):
                        pe.wait_ge(exp_done, UNITS * n + u + 1 + 2)
                        for i in range(2):
                            pe.wait_ge(copied[i], UNITS * n + u + 1)
                            for k in range(4):
                                kt = 4 * i + k
                                last = nc.tensor.transpose(t_ps[:, i, k * P:(k + 1) * P],
                                                           probs[:, u % 2, kt * P:(kt + 1) * P], env.ident[:])
                            last.then_inc(turned[i], 1)

                    def pv(u):
                        q, h = u // HG, u % HG
                        if h == 0:
                            pe.wait_ge(norm_done, QT * n + q + 1)
                        for i in range(2):
                            pe.wait_ge(copied[i], UNITS * n + u + 1 + 1)
                            for k in range(4):
                                kt = 4 * i + k
                                last = nc.tensor.matmul(o_ps[:, q % 2, h * VC:(h + 1) * VC], probsT[:, u % 2, kt * P:(kt + 1) * P],
                                                        value(h, kt), start=(kt == 0), stop=(kt == KT - 1))
                        last.then_inc(pv_done, 1)

                    if bounded:
                        LAG = 3
                        for u in range(UNITS + LAG):
                            if u < UNITS:
                                bounded_scores(u)
                            if u >= LAG:
                                bounded_pv(u - LAG)
                    else:
                        for u in range(UNITS + 2):
                            if u < UNITS:
                                scores(u)
                            if 1 <= u <= UNITS:
                                turn(u - 1)
                            if u >= 2:
                                pv(u - 2)
                    pe.drain().then_inc(group_done, 1)

                project(0, 0)
                with pe.Fori(0, FG - 1) as f:
                    project(f, 1)
                    attend(f, 0)
                    project(f + 1, 0)
                    attend(f, 1)
                project(FG - 1, 1)
                attend(FG - 1, 0)
                attend(FG - 1, 1)

            @block.scalar
            def _(act):

                def highs(f, b):
                    n = 2 * f + b
                    for i in range(PRODUCTS):
                        key = i < PRODUCTS - 1
                        if (i == 0 or not key) and (not isinstance(n, int) or n):
                            act.wait_ge(k_stacked if key else q_stacked, STACKS * n)
                        dst = kh[:, i * HALF:(i + 1) * HALF] if key else qh[:]
                        act.wait_ge(proj_psum, PRODUCTS * n + i + 1)
                        nc.scalar.activation(dst, t_ps[:, (PRODUCTS * b + i) % P_SLOTS, :], ACT.Identity,
                                             bias=(bk if key else bq)[:]).then_inc(high_done, 1)

                def attend(f, b):
                    n = 2 * f + b
                    if bounded:
                        for u in range(UNITS):
                            kt = u % KT
                            tile = b * KT + kt
                            act.wait_ge(clipped, UNITS * n + u + 1 + S_SLOTS)
                            act.wait_ge(pv_done, UNITS * n + u + 1)
                            nc.scalar.activation(pT4[:, u % 4, :], probs[:, 0, (u % 2) * HALF:(u % 2 + 1) * HALF], ACT.Exp,
                                                 bias=keep_mask[:, 1, tile:tile + 1],
                                                 scale=keep_mask[:, 0, tile:tile + 1]).then_inc(exp_done, 1)
                        return
                    for u in range(UNITS + 1):
                        if u < UNITS:
                            act.wait_ge(bias_done, UNITS * n + u + 1)
                            act.wait_ge(turned[1], UNITS * n + u + 1)
                            nc.scalar.activation(probs[:, u % 2, :], s_ps[:, u % 2, :], ACT.Exp,
                                                 bias=small[:, u % 2, 1:2], scale=SCALE).then_inc(exp_done, 1)
                        if u >= 1:
                            v = u - 1
                            act.wait_ge(turned[1], UNITS * n + v + 1 + 2)
                            act.wait_ge(pv_done, UNITS * n + v + 1)
                            nc.scalar.copy(probsT[:, v % 2, HALF:2 * HALF], t_ps[:, 1, :]).then_inc(copied[1], 1)

                act.sem_inc(exp_done, 2)
                if not bounded:
                    act.sem_inc(copied[1], 1)
                    act.sem_inc(turned[1], 2)
                highs(0, 0)
                with act.Fori(0, FG - 1) as f:
                    highs(f, 1)
                    attend(f, 0)
                    highs(f + 1, 0)
                    attend(f, 1)
                highs(FG - 1, 1)
                attend(FG - 1, 0)
                attend(FG - 1, 1)

            @block.vector
            def _(dve):
                nc.vector.memset(values[:, :, :, HD:VC], 1.0).then_inc(ones_made, 1)
                dve.wait_ge(ones_made, 1)
                dve.wait_ge(wv_loaded, 32)
                for t in range(CT):
                    dve.wait_ge(v_psum, t + 1)
                    nc.vector.tensor_tensor(values[:, t, :, 0:HD],
                                            s_ps[:, t % S_SLOTS, 0:D].rearrange("p (h e) -> p h e", e=HD),
                                            bv.rearrange("p (h e) -> p h e", e=HD), ALU.add).then_inc(v_done, 1)
                dve.wait_ge(v_done, CT)

                def lows(f, b):
                    n = 2 * f + b
                    for i in range(PRODUCTS):
                        key = i < PRODUCTS - 1
                        high = kh[:, i * HALF:(i + 1) * HALF] if key else qh[:]
                        low = kl[:, i * HALF:(i + 1) * HALF] if key else ql[:]
                        if (i == 0 or not key) and (not isinstance(n, int) or n):
                            dve.wait_ge(k_stacked if key else q_stacked, STACKS * n)
                        dve.wait_ge(high_done, PRODUCTS * n + i + 1)
                        nc.vector.scalar_tensor_tensor(low, t_ps[:, (PRODUCTS * b + i) % P_SLOTS, :], (bk if key else bq)[:],
                                                       high.bitcast(F32), ALU.add, ALU.subtract).then_inc(low_done, 1)

                def normalise(f, b, q):
                    k = (2 * f + b) * QT + q
                    o = o_ps[:, q % O_SLOTS, 0:HG * VC].rearrange("p (h e) -> p h e", e=VC)
                    nc.vector.reciprocal(inv[:, q % 2], o[:, :, HD:VC]).then_inc(inv_done, 1)
                    dve.wait_ge(inv_done, k + 1)
                    nc.vector.tensor_tensor(heads_out[:, b * QT + q, bass.ds(P * f, P)].rearrange("p (h e) -> p h e", e=HD),
                                            o[:, :, 0:HD], inv[:, q % 2].to_broadcast([P, HG, HD]), ALU.mult).then_inc(
                                                norm_done, 1)

                def attend(f, b):
                    n = 2 * f + b
                    if bounded:
                        for u in range(UNITS):
                            dve.wait_ge(scores_done, UNITS * n + u + 1)
                            dve.wait_ge(exp_done, UNITS * n + u + 1)
                            nc.vector.tensor_scalar(probs[:, 0, (u % 2) * HALF:(u % 2 + 1) * HALF], s_ps[:, u % S_SLOTS, :],
                                                    BOUND / SCALE, -BOUND / SCALE, ALU.min, ALU.max).then_inc(clipped, 1)
                        dve.wait_ge(pv_done, UNITS * (n + 1) + 4)
                        for q in range(QT):
                            normalise(f, b, q)
                        return
                    for u in range(UNITS + 3):
                        if u < UNITS:
                            dve.wait_ge(scores_done, UNITS * n + u + 1)
                            nc.vector.tensor_reduce(small[:, u % 2, 0:1], s_ps[:, u % 2, :], AX_X, ALU.max).then_inc(max_done, 1)
                            dve.wait_ge(max_done, UNITS * n + u + 1)
                            nc.vector.tensor_scalar(small[:, u % 2, 1:2], small[:, u % 2, 0:1], -SCALE, None,
                                                    ALU.mult).then_inc(bias_done, 1)
                        if 1 <= u <= UNITS:
                            v = u - 1
                            dve.wait_ge(turned[0], UNITS * n + v + 1)
                            dve.wait_ge(pv_done, UNITS * n + v + 1)
                            nc.vector.tensor_copy(probsT[:, v % 2, 0:HALF], t_ps[:, 0, :]).then_inc(copied[0], 1)
                        if u >= 6 and u % HG == 2:
                            q = (u - 6) // HG
                            dve.wait_ge(pv_done, UNITS * n + HG * (q + 1) + 2)
                            normalise(f, b, q)

                dve.sem_inc(low_done, P_SLOTS)
                dve.sem_inc(norm_done, QT if bounded else 2)
                dve.sem_inc(pv_done, 4 if bounded else 2)
                if bounded:
                    dve.sem_inc(clipped, S_SLOTS)
                else:
                    dve.sem_inc(copied[0], 1)
                lows(0, 0)
                with dve.Fori(0, FG - 1) as f:
                    lows(f, 1)
                    attend(f, 0)
                    lows(f + 1, 0)
                    attend(f, 1)
                lows(FG - 1, 1)
                attend(FG - 1, 0)
                attend(FG - 1, 1)
                dve.wait_ge(norm_done, QT * 2 * FG + (QT if bounded else 2))


def linear_attention_block(env, name, heads_out):
    nc, io = env.nc, env.io
    env.prefix = f"{name}_attn"
    HEADS, HD, FD = 16, 32, 64
    FG, HG = 4, 4
    VC = HD + 1
    KT, QT = CTX // P, SEQ // P
    CT = BATCH * KT
    PAIR = 2 * VC
    K_PARTS, Q_PARTS = BATCH * CTX // HALF, TOK // HALF
    MAPPED = BATCH * 2
    PRODUCTS = K_PARTS + Q_PARTS + MAPPED
    EPS = 1e-8
    ctx_loaded, wv_loaded, w_loaded, maps_loaded = (env.sem("ctx_loaded"), env.sem("wv_loaded"), env.sem("w_loaded"),
                                                    env.sem("maps_loaded"))
    cleared, v_psum, v_done = env.sem("cleared"), env.sem("v_psum"), env.sem("v_done")
    proj_psum, proj_done = env.sem("proj_psum"), env.sem("proj_done")
    kf_psum, kf_done = env.sem("kf_psum"), env.sem("kf_done")
    kv_step, kv_copied = env.sem("kv_step"), env.sem("kv_copied")
    o_done, norm_done, inv_step = env.sem("o_done"), env.sem("norm_done"), env.sem("inv_step")
    with ExitStack() as local:
        def sb(n, shape, dt=F32):
            return local.enter_context(nc.sbuf_tensor(f"{name}_{n}", shape, dt))

        def psum(n):
            return local.enter_context(nc.psum_tensor(f"{name}_{n}", [P, 2, HALF], F32))

        ctxT, values = sb("ctxT", [P, DC, BATCH * CTX]), sb("values", [P, CT, HEADS, VC])
        wv, bv, wk, wq = sb("wv", [P, DC, D]), sb("bv", [P, D]), sb("wk", [P, DC * P]), sb("wq", [P, DC * P])
        bk, bq, mask = sb("bk", [P, 1]), sb("bq", [P, 1]), sb("mask", [P, CT])
        wqf, wkf = sb("wqf", [P, HG * FD]), sb("wkf", [P, HG * FD])
        kT, qT = sb("kT", [P, BATCH * CTX]), sb("qT", [P, TOK])
        kf, qf = sb("kf", [P, 2, HG * FD]), sb("qf", [P, MAPPED, SEQ])
        kv = sb("kv", [P, BATCH, 2, PAIR])
        inv = sb("inv", [P, 2, HG, 1])
        proj_ps, kf_ps, kv_ps, o_ps = psum("proj_ps"), psum("kf_ps"), psum("kv_ps"), psum("o_ps")

        with nc.Block() as block:
            @block.sync
            def _(sp):
                sp.dma_start(wv[:], io["wv"]).then_inc(wv_loaded, 16)
                sp.dma_start(bv[:], io["bv"].partition_broadcast(P)).then_inc(wv_loaded, 16)
                for b in range(BATCH):
                    sp.dma_start(ctxT[:, :, b * CTX:(b + 1) * CTX], io["ctxT"][:, :, b * CTX:(b + 1) * CTX]).then_inc(
                        ctx_loaded, 16)
                    sp.wait_ge(ctx_loaded, 16 * (b + 1))

                def load_weights(f):
                    for to, of in ((wk, "wk"), (wq, "wq"), (bk, "bk"), (bq, "bq")):
                        sp.dma_start(to[:], io[of][bass.ds(f, 1)].rearrange("g p n -> p (g n)")).then_inc(w_loaded, 16)

                load_weights(0)
                sp.dma_start(mask[:], io["mask_f"]).then_inc(maps_loaded, 16)
                sp.wait_ge(cleared, 4)
                for h in range(HG):
                    for to, of in ((wqf, "wqf"), (wkf, "wkf")):
                        sp.dma_start(to[HD * h:HD * (h + 1), FD * h:FD * (h + 1)], io[of]).then_inc(maps_loaded, 16)
                with sp.Fori(1, FG) as f:
                    sp.wait_ge(proj_done, 2 + PRODUCTS * (f - 1) + K_PARTS + Q_PARTS)
                    load_weights(f)

            @block.tensor
            def _(pe):
                pe.wait_ge(wv_loaded, 32)
                for t in range(CT):
                    pe.wait_ge(ctx_loaded, 16 * (t // KT + 1))
                    if t >= 2:
                        pe.wait_ge(v_done, t - 1)
                    for i in range(DC):
                        last = nc.tensor.matmul(kf_ps[:, t % 2, :], ctxT[:, i, t * P:(t + 1) * P], wv[:, i, :],
                                                start=(i == 0), stop=(i == DC - 1))
                    last.then_inc(v_psum, 1)
                pe.wait_ge(v_done, CT)
                pe.wait_ge(maps_loaded, 16 * (2 * HG + 1))
                with pe.Fori(0, FG) as f:
                    def slot(i):
                        pe.wait_ge(proj_done, PRODUCTS * f + i + 1)
                        return proj_ps[:, i % 2, :]

                    pe.wait_ge(w_loaded, 64 * (f + 1))
                    for i in range(K_PARTS + Q_PARTS):
                        w, moving, n = (wk, ctxT, i) if i < K_PARTS else (wq, env.xT, i - K_PARTS)
                        to = slot(i)
                        for c in range(DC):
                            last = nc.tensor.matmul(to, w[:, c * P:(c + 1) * P], moving[:, c, n * HALF:(n + 1) * HALF],
                                                    start=(c == 0), stop=(c == DC - 1))
                        last.then_inc(proj_psum, 1)

                    def accumulate(t):
                        b = t // KT
                        pe.wait_ge(kf_done, CT * f + t + 1 + 2)
                        if t % KT == 0:
                            pe.wait_ge(kv_copied, 4 * BATCH * f + 4 * b + 4)
                        for j in range(2):
                            rhs = values[:, t, bass.ds(HG * f + 2 * j, 2), :].rearrange("p h e -> p (h e)")
                            last = nc.tensor.matmul(kv_ps[:, j, 0:PAIR], kf[:, t % 2, j * P:(j + 1) * P], rhs,
                                                    start=(t % KT == 0), stop=(t % KT == KT - 1))
                        last.then_inc(kv_step, 1)

                    pe.wait_ge(proj_done, 2 + PRODUCTS * f + K_PARTS)
                    for t in range(CT):
                        pe.wait_ge(kf_done, CT * f + t + 1)
                        nc.tensor.matmul(kf_ps[:, t % 2, 0:HG * FD], kT[:, t * P:(t + 1) * P], wkf[:],
                                         start=True, stop=True).then_inc(kf_psum, 1)
                        if t >= 1:
                            accumulate(t - 1)
                    accumulate(CT - 1)
                    pe.wait_ge(proj_done, 2 + PRODUCTS * f + K_PARTS + Q_PARTS)
                    for m in range(MAPPED):
                        b, j = m // 2, m % 2
                        nc.tensor.matmul(slot(K_PARTS + Q_PARTS + m), wqf[:, j * P:(j + 1) * P],
                                         qT[:, b * SEQ:(b + 1) * SEQ], start=True, stop=True).then_inc(proj_psum, 1)
                    pe.wait_ge(proj_done, 2 + PRODUCTS * (f + 1))
                    pe.wait_ge(kv_copied, 4 * BATCH * (f + 1) + 4)
                    for q in range(TILES):
                        pe.wait_ge(norm_done, TILES * f + q + 1)
                        b, at = q // QT, (q % QT) * P
                        for j in range(2):
                            last = nc.tensor.matmul(o_ps[:, q % 2, j * PAIR:(j + 1) * PAIR], qf[:, 2 * b + j, at:at + P],
                                                    kv[:, b, j, :], start=True, stop=True)
                        last.then_inc(o_done, 1)

            @block.scalar
            def _(act):
                act.sem_inc(proj_done, 2)
                with act.Fori(0, FG) as f:
                    act.wait_ge(kv_step, CT * f + 2)
                    act.wait_ge(norm_done, TILES * f + 2)
                    for i in range(PRODUCTS):
                        act.wait_ge(proj_psum, PRODUCTS * f + i + 1)
                        ps = proj_ps[:, i % 2, :]
                        if i < K_PARTS:
                            ins = nc.scalar.activation(kT[:, i * HALF:(i + 1) * HALF], ps, ACT.Identity, bias=bk[:])
                        elif i < K_PARTS + Q_PARTS:
                            n = i - K_PARTS
                            ins = nc.scalar.activation(qT[:, n * HALF:(n + 1) * HALF], ps, ACT.Identity, bias=bq[:])
                        else:
                            ins = nc.scalar.activation(qf[:, i - K_PARTS - Q_PARTS, :], ps, ACT.Relu)
                        ins.then_inc(proj_done, 1)

            @block.vector
            def _(dve):
                nc.vector.memset(wqf[:], 0.0).then_inc(cleared, 1)
                nc.vector.memset(wkf[:], 0.0).then_inc(cleared, 1)
                nc.vector.memset(kv[:], 0.0).then_inc(cleared, 1)
                nc.vector.memset(values[:, :, :, HD:VC], 1.0).then_inc(cleared, 1)
                dve.wait_ge(cleared, 4)
                dve.wait_ge(wv_loaded, 32)
                for t in range(CT):
                    dve.wait_ge(v_psum, t + 1)
                    nc.vector.tensor_tensor(values[:, t, :, 0:HD], kf_ps[:, t % 2, :].rearrange("p (h e) -> p h e", e=HD),
                                            bv[:].rearrange("p (h e) -> p h e", e=HD), ALU.add).then_inc(v_done, 1)
                dve.wait_ge(maps_loaded, 16 * (2 * HG + 1))
                dve.sem_inc(kf_done, 2)
                dve.sem_inc(kv_step, 2)
                dve.sem_inc(kv_copied, 4)
                dve.sem_inc(norm_done, 2)
                with dve.Fori(0, FG) as f:
                    for t in range(CT):
                        dve.wait_ge(kf_psum, CT * f + t + 1)
                        dve.wait_ge(kv_step, CT * f + t + 1)
                        nc.vector.tensor_scalar(kf[:, t % 2, :], kf_ps[:, t % 2, 0:HG * FD], 0.0, mask[:, t:t + 1],
                                                ALU.max, ALU.mult).then_inc(kf_done, 1)
                        if t % KT == KT - 1:
                            b = t // KT
                            dve.wait_ge(kv_step, CT * f + t + 1 + 2)
                            for j in range(2):
                                for half in range(2):
                                    rows, cols = slice(64 * half, 64 * half + 64), slice(VC * half, VC * (half + 1))
                                    nc.vector.tensor_copy(kv[rows, b, j, cols], kv_ps[rows, j, cols]).then_inc(kv_copied, 1)
                    for q in range(TILES):
                        o = o_ps[:, q % 2, 0:HG * VC].rearrange("p (h e) -> p h e", e=VC)
                        k = TILES * f + q
                        dve.wait_ge(o_done, k + 1)
                        nc.vector.tensor_scalar(inv[:, q % 2], o[:, :, HD:VC], EPS, None, ALU.add).then_inc(inv_step, 1)
                        dve.wait_ge(inv_step, 2 * k + 1)
                        nc.vector.reciprocal(inv[:, q % 2], inv[:, q % 2]).then_inc(inv_step, 1)
                        dve.wait_ge(inv_step, 2 * k + 2)
                        nc.vector.tensor_tensor(heads_out[:, q, bass.ds(P * f, P)].rearrange("p (h e) -> p h e", e=HD),
                                                o[:, :, 0:HD], inv[:, q % 2].to_broadcast([P, HG, HD]), ALU.mult).then_inc(
                                                    norm_done, 1)
                dve.wait_ge(norm_done, TILES * FG + 2)


def key_mask_block(env, name, keep_mask):
    nc, io = env.nc, env.io
    env.prefix = f"{name}_mask"
    loaded, step = env.sem("loaded"), env.sem("step")
    n = BATCH * CTX // P
    with ExitStack() as local:
        raw = local.enter_context(nc.sbuf_tensor(f"{name}_mask_raw", [P, n], I32))
        keep = local.enter_context(nc.sbuf_tensor(f"{name}_keep", [P, n], F32))
        with nc.Block() as block:
            @block.sync
            def _(sp):
                sp.dma_start(raw[:], io["mask"]).then_inc(loaded, 16)

            @block.vector
            def _(dve):
                dve.wait_ge(loaded, 16)
                nc.vector.tensor_scalar(keep[:], raw[:], 0.5, None, ALU.is_gt).then_inc(step, 1)
                dve.wait_ge(step, 1)
                nc.vector.tensor_scalar(keep_mask[:, 0, :], keep[:], 32 ** -0.5, None, ALU.mult).then_inc(step, 1)
                nc.vector.tensor_scalar(keep_mask[:, 1, :], keep[:], -1.0, 50.0, ALU.add, ALU.mult).then_inc(step, 1)
                dve.wait_ge(step, 3)


def quantise_rows(nc, link, src, dst, top, tmp):
    MAGIC = 1.5 * 2 ** 23
    s, inv = top[:, 0:1], top[:, 1:2]
    link(nc.vector.tensor_reduce(s, src, AX_X, ALU.max, apply_absolute_value=True))
    link(nc.vector.tensor_scalar(s, s, 1.0 / 127.0, 1e-8, ALU.mult, ALU.max))
    link(nc.vector.reciprocal(inv, s))
    link(nc.vector.tensor_scalar(tmp, src, inv, MAGIC, ALU.mult, ALU.add))
    link(nc.vector.tensor_scalar(tmp, tmp, MAGIC + 127.0, MAGIC - 127.0, ALU.min, ALU.max))
    link(nc.vector.tensor_scalar(dst, tmp, -MAGIC, s, ALU.add, ALU.mult))


def quantise_weights_block(env, name, wq_scratch, wp_scratch):
    nc, io = env.nc, env.io
    env.prefix = f"{name}_quant"
    FG = D // P
    loaded, ready, turned, copied, stored = (env.sem("loaded"), env.sem("ready"), env.sem("turned"), env.sem("copied"),
                                             env.sem("stored"))
    with ExitStack() as local:
        w = local.enter_context(nc.sbuf_tensor(f"{name}_w", [P, 2 * FG, D], F32))
        wT = local.enter_context(nc.sbuf_tensor(f"{name}_wT", [P, 2 * FG, DC, P], F32))
        tmp = local.enter_context(nc.sbuf_tensor(f"{name}_tmp", [P, D], F32))
        top = local.enter_context(nc.sbuf_tensor(f"{name}_top", [P, 2], F32))
        ps = local.enter_context(nc.psum_tensor(f"{name}_quant_ps", [P, 2, DC, P], F32))
        with nc.Block() as block:
            @block.sync
            def _(sp):
                sp.dma_start(w[:, 0:FG, :], io["wq_rows"].rearrange("(f p) n -> p f n", p=P)).then_inc(loaded, 16)
                sp.dma_start(w[:, FG:2 * FG, :], io["wp_rows"].rearrange("(f p) n -> p f n", p=P)).then_inc(loaded, 16)
                for g in range(FG):
                    sp.wait_ge(copied, g + 1)
                    sp.dma_start(wq_scratch[g], wT[:, g].rearrange("p c n -> p (c n)")).then_inc(stored, 16)
                sp.wait_ge(copied, 2 * FG)
                for g in range(FG):
                    sp.dma_start(wp_scratch[:, :, g * P:(g + 1) * P], wT[:, FG + g]).then_inc(stored, 16)
                sp.wait_ge(stored, 16 * 2 * FG)

            @block.vector
            def _(dve):
                links, count = env.sem("links"), [0]

                def link(ins):
                    count[0] += 1
                    ins.then_inc(links, 1)
                    dve.wait_ge(links, count[0])

                dve.wait_ge(loaded, 32)
                for g in range(2 * FG):
                    quantise_rows(nc, link, w[:, g, :], w[:, g, :], top, tmp[:])
                    dve.sem_inc(ready, 1)

            @block.tensor
            def _(pe):
                for g in range(2 * FG):
                    pe.wait_ge(ready, g + 1)
                    if g >= 2:
                        pe.wait_ge(copied, g - 1)
                    for c in range(DC):
                        last = nc.tensor.transpose(ps[:, g % 2, c, :], w[:, g, c * P:(c + 1) * P], env.ident[:])
                    last.then_inc(turned, 1)

            @block.scalar
            def _(act):
                for g in range(2 * FG):
                    act.wait_ge(turned, g + 1)
                    nc.scalar.copy(wT[:, g], ps[:, g % 2]).then_inc(copied, 1)


def output_block(env, name, heads_out, gate, wo_dram, quantised=False, after_norm=False):
    nc, io = env.nc, env.io
    env.prefix = f"{name}_out"
    loaded, ready, turned, copied = env.sem("loaded"), env.sem("ready"), env.sem("turned"), env.sem("copied")
    y_done, y_used, var_done, sd_done = env.sem("y_done"), env.sem("y_used"), env.sem("var_done"), env.sem("sd_done")
    LOADS = 16 * (5 if after_norm else 2)
    with ExitStack() as local:
        def sb(n, shape, dt=F32):
            return local.enter_context(nc.sbuf_tensor(f"{name}_{n}", shape, dt))

        wo, bo, aT = sb("wo", [P, DC, D]), sb("bo", [P, D]), sb("aT", [P, 2, DC, P])
        top, tmp, delta = sb("out_top", [P, 2]), sb("out_tmp", [P, D]), sb("delta", [P, 2, D])
        if after_norm:
            gamma, beta, rs = sb("gamma", [P, D]), sb("beta", [P, D]), sb("rs", [P, 1])
            stats, meanvar, sd = sb("out_stats", [P, 2, 6]), sb("out_meanvar", [P, 2, 2]), sb("out_sd", [P, 2, 2])
        t_ps = local.enter_context(nc.psum_tensor(f"{name}_turn_ps", [P, 2, DC, P], F32))
        y_ps = local.enter_context(nc.psum_tensor(f"{name}_out_ps", [P, 2, D], F32))
        with nc.Block() as block:
            @block.sync
            def _(sp):
                sp.dma_start(wo[:], wo_dram).then_inc(loaded, 16)
                sp.dma_start(bo[:], io["bo"].partition_broadcast(P)).then_inc(loaded, 16)
                if after_norm:
                    sp.dma_start(gamma[:], io["gamma"].partition_broadcast(P)).then_inc(loaded, 16)
                    sp.dma_start(beta[:], io["beta"].partition_broadcast(P)).then_inc(loaded, 16)
                    sp.dma_start(rs[:], io["rs"].partition_broadcast(P)).then_inc(loaded, 16)

            @block.tensor
            def _(pe):
                pe.wait_ge(loaded, LOADS)

                def product(t):
                    pe.wait_ge(copied, t + 1)
                    if t >= 2:
                        pe.wait_ge(y_used, t - 1)
                    for c in range(DC):
                        last = nc.tensor.matmul(y_ps[:, t % 2, :], aT[:, t % 2, c, :], wo[:, c, :],
                                                start=(c == 0), stop=(c == DC - 1))
                    last.then_inc(y_done, 1)

                for t in range(TILES):
                    if quantised:
                        pe.wait_ge(ready, t + 1)
                    if t >= 2:
                        pe.wait_ge(copied, t - 1)
                    for c in range(DC):
                        last = nc.tensor.transpose(t_ps[:, t % 2, c, :], heads_out[:, t, c * P:(c + 1) * P], env.ident[:])
                    last.then_inc(turned, 1)
                    if t >= 1:
                        product(t - 1)
                product(TILES - 1)

            @block.scalar
            def _(act):
                def root(act, t):
                    act.wait_ge(var_done, t + 1)
                    nc.scalar.activation(sd[:, t % 2, 0:1], meanvar[:, t % 2, 1:2], ACT.Sqrt,
                                         bias=env.eps_ln[:]).then_inc(sd_done, 1)

                for t in range(TILES):
                    act.wait_ge(turned, t + 1)
                    if t >= 2:
                        act.wait_ge(y_done, t - 1)
                    nc.scalar.copy(aT[:, t % 2], t_ps[:, t % 2]).then_inc(copied, 1)
                    if after_norm and t >= 2:
                        root(act, t - 2)
                if after_norm:
                    root(act, TILES - 2)
                    root(act, TILES - 1)

            @block.vector
            def _(dve):
                links, count = env.sem("links"), [0]

                def link(ins):
                    count[0] += 1
                    ins.then_inc(links, 1)
                    dve.wait_ge(links, count[0])

                if quantised:
                    for t in range(TILES):
                        quantise_rows(nc, link, heads_out[:, t, :], heads_out[:, t, :], top, tmp[:])
                        dve.sem_inc(ready, 1)
                dve.wait_ge(loaded, LOADS)
                if after_norm:
                    link(nc.vector.tensor_scalar(rs[:], rs[:], 0.0, 0.3, ALU.max, ALU.min))
                    link(nc.vector.tensor_scalar(gamma[:], gamma[:], gate, None, ALU.mult))
                    link(nc.vector.tensor_scalar(beta[:], beta[:], gate, None, ALU.mult))
                for t in range(TILES):
                    d = delta[:, t % 2, :]
                    dve.wait_ge(y_done, t + 1)
                    nc.vector.tensor_tensor(d, y_ps[:, t % 2, :], bo[:], ALU.add).then_inc(y_used, 1)
                    dve.wait_ge(y_used, t + 1)
                    if after_norm:
                        link(nc.vector.tensor_scalar(d, d, rs[:], None, ALU.mult))
                        link(nc.vector.bn_stats(stats[:, t % 2, :], d))
                        nc.vector.bn_aggr(meanvar[:, t % 2, :], stats[:, t % 2, :]).then_inc(var_done, 1)
                        dve.wait_ge(sd_done, t + 1)
                        link(nc.vector.reciprocal(sd[:, t % 2, 1:2], sd[:, t % 2, 0:1]))
                        link(nc.vector.tensor_scalar(d, d, meanvar[:, t % 2, 0:1], sd[:, t % 2, 1:2], ALU.subtract, ALU.mult))
                        link(nc.vector.tensor_tensor(d, d, gamma[:], ALU.mult))
                        link(nc.vector.tensor_tensor(d, d, beta[:], ALU.add))
                        link(nc.vector.tensor_tensor(env.x[:, t, :], env.x[:, t, :], d, ALU.add))
                    else:
                        link(nc.vector.scalar_tensor_tensor(env.x[:, t, :], d, gate, env.x[:, t, :], ALU.mult, ALU.add))


def build(nc, io, out, stages):
    with ExitStack() as stack:
        env = Env(nc, stack, io)
        env.x = stack.enter_context(nc.sbuf_tensor("x", [P, TILES, D], F32))
        env.xT = stack.enter_context(nc.sbuf_tensor("xT", [P, DC, TOK], F32))
        env.ident = stack.enter_context(nc.sbuf_tensor("ident", [P, P], F32))
        env.gates = stack.enter_context(nc.sbuf_tensor("gates", [P, 8], F32))
        env.tanh_gates = stack.enter_context(nc.sbuf_tensor("tanh_gates", [P, 8], F32))
        env.iota8 = stack.enter_context(nc.sbuf_tensor("iota8", [P, 8], F32))
        env.eps_ln = stack.enter_context(nc.sbuf_tensor("eps_ln", [P, 1], F32))
        setup_block(env)

        @contextmanager
        def sublayer():
            with nc.cleanup_on_exit(), ExitStack() as local:
                yield local

        def layer(prefix, *names):
            env.io = {n: io[f"{prefix}_{n}"] for n in names}

        def attention_layer(name, gate, **kinds):
            with sublayer() as local:
                sb = lambda n, s, d=F32: local.enter_context(nc.sbuf_tensor(n, s, d))
                layer(name, *[n[len(name) + 1:] for n in io if n.startswith(name)])
                env.io["ctxT"] = io["ctxT"]
                heads_out = sb(f"{name}_heads", [P, TILES, D])
                keep_mask = None
                quantised = kinds.get("quantised", False)
                if quantised:
                    wq_scratch = nc.dram_tensor("wq_scratch", (D // P, P, D), F32, kind="Internal").ap()
                    env.io["wq"] = wq_scratch
                    env.io["wo"] = nc.dram_tensor("wp_scratch", (P, DC, D), F32, kind="Internal").ap()
                    quantise_weights_block(env, name, wq_scratch, env.io["wo"])
                if kinds.get("masked"):
                    keep_mask = sb("keep_mask", [P, 2, BATCH * CTX // P])
                    env.io["mask"] = io["mask"]
                    key_mask_block(env, name, keep_mask)
                norm_block(env, name, quantised=quantised)
                if kinds.get("linear"):
                    env.io["mask_f"] = io["mask_f"]
                    linear_attention_block(env, name, heads_out)
                else:
                    softmax_attention_block(env, name, heads_out, keep_mask)
                output_block(env, name, heads_out, gate, env.io["wo"], quantised, kinds.get("after_norm", False))

        if "L0_attn" in stages:
            attention_layer("L0_attn", env.tanh_gates[:, 0:1], linear=True)
        if "L0_ffn" in stages:
            layer("L0_ffn", "w1", "w2", "w3")
            with sublayer() as local:
                sb = lambda n, s, d=F32: local.enter_context(nc.sbuf_tensor(n, s, d))
                scale, half, neg_half = sb("scale", [P, 3]), sb("half", [P, 3]), sb("neg_half", [P, 3])
                weight = sb("weight", [P, 1])
                ternary_scales(env, "L0_ffn", scale, half, neg_half, env.tanh_gates[:, 4:5], weight)
                xh, xl = sb("xh", [P, DC, TOK], F32R), sb("xl", [P, DC, TOK], F32R)
                norm_block(env, "L0_ffn", split=(xh, xl))
                ffn_block(env, "L0_ffn", [P, P], weight, ternary=(xh, xl, scale, half, neg_half))
        if "L1_attn" in stages:
            attention_layer("L1_attn", env.tanh_gates[:, 1:2], masked=True, after_norm=True)
        if "L1_ffn" in stages:
            with sublayer() as local:
                sb = lambda n, s, d=F32: local.enter_context(nc.sbuf_tensor(n, s, d))
                layer("L1_ffn", "w1", "w3", "wq", "keys")
                G = io["L1_ffn_w1"].shape[0]
                sims, bar = sb("sims", [P, TILES, PEER_HEADS, 2 * NK]), sb("bar", [P, TILES * PEER_HEADS])
                extra = sb("extra", [P, G, TILES])
                norm_block(env, "L1_ffn")
                product_keys_block(env, "L1_ffn", sims, bar, extra, G)
                ffn_block(env, "L1_ffn", [P] * 4, env.tanh_gates[:, 5:6], peer=(sims, bar, extra))
        if "L2_attn" in stages:
            attention_layer("L2_attn", env.tanh_gates[:, 2:3], quantised=True)
        if "L2_ffn" in stages:
            with sublayer() as local:
                layer("L2_ffn", "w1", "w2", "w3", "router")
                weight = local.enter_context(nc.sbuf_tensor("L2_weight", [P, TILES, 8], F32))
                norm_block(env, "L2_ffn")
                expert_weights_block(env, "L2_ffn", 8, 0, True, env.tanh_gates[:, 6:7], weight)
                ffn_block(env, "L2_ffn", [P, P], weight)
        if "L3_attn" in stages:
            attention_layer("L3_attn", env.tanh_gates[:, 3:4])
        if "L3_ffn" in stages:
            with sublayer() as local:
                layer("L3_ffn", "w1", "w2", "w3", "router")
                weight = local.enter_context(nc.sbuf_tensor("L3_weight", [P, TILES, 12], F32))
                norm_block(env, "L3_ffn")
                expert_weights_block(env, "L3_ffn", 12, 4, False, env.tanh_gates[:, 7:8], weight)
                ffn_block(env, "L3_ffn", [P, P, 96], weight)
        store_block(env, out)


def lay_out(inputs):
    import numpy as np

    def up(w, group):
        g = w.shape[0] // group
        return w.reshape(g, group, DC, P).transpose(0, 3, 2, 1).reshape(g, P, DC * group)

    def rows(w):
        return w.reshape(DC, P, w.shape[1]).transpose(1, 0, 2)

    i = {k: np.asarray(v) for k, v in inputs.items()}
    a = {k: i[k] for k in ("x", "g_xattn", "g_ffn")}
    a["L0_ffn_w1"], a["L0_ffn_w2"] = up(i["L0_ffn_W_up"], 256), up(i["L0_ffn_W_gate"], 256)
    a["L0_ffn_w3"] = i["L0_ffn_W_down"].T.reshape(8, 256, D)
    a["L1_ffn_w1"], a["L1_ffn_w3"] = up(i["L1_ffn_e_down"], 512), i["L1_ffn_e_up"].reshape(8, 512, D)
    a["L1_ffn_wq"] = rows(i["L1_ffn_Wq"])
    a["L1_ffn_keys"] = i["L1_ffn_keys"].transpose(3, 2, 0, 1)
    a["L2_ffn_w1"] = up(i["L2_ffn_wi_0"].transpose(0, 2, 1).reshape(-1, D), 256)
    a["L2_ffn_w2"] = up(i["L2_ffn_wi_1"].transpose(0, 2, 1).reshape(-1, D), 256)
    a["L2_ffn_w3"], a["L2_ffn_router"] = i["L2_ffn_wo"], rows(i["L2_ffn_w_gate"])
    s, w13 = i["L3_ffn_shared_gate_up_w"], i["L3_ffn_w13"]
    inter = w13.shape[1] // 2
    a["L3_ffn_w1"] = up(np.concatenate([s[:s.shape[0] // 2], w13[:, :inter].reshape(-1, D)]), inter)
    a["L3_ffn_w2"] = up(np.concatenate([s[s.shape[0] // 2:], w13[:, inter:].reshape(-1, D)]), inter)
    a["L3_ffn_w3"] = np.concatenate([i["L3_ffn_shared_down_w"].T.reshape(-1, inter, D),
                                     i["L3_ffn_w2"].transpose(0, 2, 1)])
    a["L3_ffn_router"] = rows(np.concatenate([i["L3_ffn_gate_w"], i["L3_ffn_shared_gate_w"]]).T)
    a["ctxT"] = rows(i["ctx_2048"].reshape(-1, D).T)
    a["mask"] = i["mask_BxS2_ik0"].reshape(-1, P).T

    def column(b):
        return b.reshape(DC, P, 1)

    for n in (0, 1, 3):
        for m in ("q", "k"):
            a[f"L{n}_attn_w{m}"] = up(i[f"L{n}_xattn_W{m}"], P)
            a[f"L{n}_attn_b{m}"] = column(i[f"L{n}_xattn_b{m}"])
        for m in ("v", "o"):
            a[f"L{n}_attn_w{m}"], a[f"L{n}_attn_b{m}"] = rows(i[f"L{n}_xattn_W{m}"].T), i[f"L{n}_xattn_b{m}"]
    a["L0_attn_wqf"], a["L0_attn_wkf"] = i["L0_xattn_Wqf"].T, i["L0_xattn_Wkf"].T
    a["mask_f"] = i["mask_BxS2_ff1"].reshape(-1, P).T
    a["L1_attn_gamma"], a["L1_attn_beta"] = i["L1_xattn_ln_gamma"], i["L1_xattn_ln_beta"]
    a["L1_attn_rs"] = i["L1_xattn_residual_scale"].reshape(1)
    a["L2_attn_wq_rows"], a["L2_attn_wp_rows"] = i["L2_xattn_wq"], i["L2_xattn_wp"]
    a["L2_attn_wk"], a["L2_attn_wv"] = up(i["L2_xattn_wkv"][:D], P), rows(i["L2_xattn_wkv"][D:].T)
    a["L2_attn_bq"], a["L2_attn_bk"] = column(i["L2_xattn_bq"]), column(i["L2_xattn_bkv"][:D])
    a["L2_attn_bv"], a["L2_attn_bo"] = i["L2_xattn_bkv"][D:], i["L2_xattn_bp"]
    return {k: np.ascontiguousarray(v) for k, v in a.items()}


STAGES = ("L0_attn", "L0_ffn", "L1_attn", "L1_ffn", "L2_attn", "L2_ffn", "L3_attn", "L3_ffn")


def kernel(**inputs):
    import concourse.bacc as bacc
    from concourse.bass_utils import run_bass_kernel_spmd

    nc = bacc.Bacc("TRN2", target_bir_lowering=False, num_devices=1)
    arrays, io = {}, {}
    for name, a in lay_out(inputs).items():
        arrays[f"in_{name}"] = a
        io[name] = nc.dram_tensor(f"in_{name}", a.shape, mybir.dt.from_np(a.dtype), kind="ExternalInput").ap()
    out = nc.dram_tensor("out_x", (BATCH, SEQ, D), F32, kind="ExternalOutput").ap()
    build(nc, io, out, STAGES)
    r = run_bass_kernel_spmd(nc, [arrays], core_ids=[0])
    return r.results[0]["out_x"]
```

```python
from contextlib import ExitStack, contextmanager

import concourse.bass as bass
from concourse import mybir

F32 = mybir.dt.float32
F32R = mybir.dt.float32r
U32 = mybir.dt.uint32
I32 = mybir.dt.int32
ALU = mybir.AluOpType
ACT = mybir.ActivationFunctionType
AX_X = mybir.AxisListType.X

P = 128
D = 512
DC = D // P
BATCH = 2
SEQ = 512
CTX = 1024
TOK = BATCH * SEQ
TILES = TOK // P
HALF = 512
HALVES = TOK // HALF
EPS_LN = 1e-5
EPS_TERNARY = 1e-8
NK = 128
PEER_HEADS = 4
KEY_ROWS = 32


class Env:

    def __init__(self, nc, stack, io):
        self.nc, self.stack, self.io = nc, stack, io
        self.prefix = ""

    def sem(self, name):
        return self.nc.alloc_semaphore(name=f"{self.prefix}_{name}")


def setup_block(env):
    nc, io = env.nc, env.io
    env.prefix = "setup"
    x_loaded, gates_loaded = env.sem("x_loaded"), env.sem("gates_loaded")
    zeroed, made, tanh_done = env.sem("zeroed"), env.sem("made"), env.sem("tanh_done")
    iota_done = env.sem("iota_done")
    iota = env.stack.enter_context(nc.sbuf_tensor("iota", [P, 8], I32))
    with nc.Block() as block:
        @block.sync
        def _(sp):
            sp.dma_start(env.x[:], io["x"].rearrange("b (t p) d -> p (b t) d", p=P)).then_inc(x_loaded, 16)
            sp.dma_start(env.gates[:, 0:4], io["g_xattn"].partition_broadcast(P)).then_inc(gates_loaded, 16)
            sp.dma_start(env.gates[:, 4:8], io["g_ffn"].partition_broadcast(P)).then_inc(gates_loaded, 16)
            sp.wait_ge(x_loaded, 16)

        @block.gpsimd
        def _(pool):
            nc.gpsimd.memset(env.ident[:], 0.0).then_inc(zeroed, 1)
            nc.gpsimd.memset(env.eps_ln[:], EPS_LN).then_inc(made, 1)
            nc.gpsimd.iota(iota[:], pattern=[[1, 8]], base=0, channel_multiplier=0).then_inc(iota_done, 1)
            pool.wait_ge(iota_done, 1)
            nc.gpsimd.tensor_copy(env.iota8[:], iota[:]).then_inc(made, 1)
            pool.wait_ge(zeroed, 1)
            nc.gpsimd.affine_select(out=env.ident[:], in_=env.ident[:], compare_op=ALU.not_equal, fill=1.0,
                                    base=0, pattern=[[-1, P]], channel_multiplier=1).then_inc(made, 1)
            pool.wait_ge(made, 3)

        @block.scalar
        def _(act):
            act.wait_ge(gates_loaded, 32)
            nc.scalar.activation(env.tanh_gates[:], env.gates[:], ACT.Tanh).then_inc(tanh_done, 1)
            act.wait_ge(tanh_done, 1)


def store_block(env, out):
    nc = env.nc
    env.prefix = "store"
    stored = env.sem("stored")
    with nc.Block() as block:
        @block.sync
        def _(sp):
            sp.dma_start(out.rearrange("b (t p) d -> p (b t) d", p=P), env.x[:]).then_inc(stored, 16)
            sp.wait_ge(stored, 16)


def norm_block(env, name, split=None, quantised=False):
    nc = env.nc
    env.prefix = f"{name}_norm"
    stats_done, var_done, sd_done = env.sem("stats_done"), env.sem("var_done"), env.sem("sd_done")
    rstd_done, xn_done, transposed = env.sem("rstd_done"), env.sem("xn_done"), env.sem("transposed")
    copied, high_done, low_done = env.sem("copied"), env.sem("high_done"), env.sem("low_done")
    with ExitStack() as local:
        stats = local.enter_context(nc.sbuf_tensor(f"{name}_stats", [P, TILES, 6], F32))
        meanvar = local.enter_context(nc.sbuf_tensor(f"{name}_meanvar", [P, TILES, 2], F32))
        sd = local.enter_context(nc.sbuf_tensor(f"{name}_sd", [P, TILES], F32))
        rstd = local.enter_context(nc.sbuf_tensor(f"{name}_rstd", [P, TILES], F32))
        xn = local.enter_context(nc.sbuf_tensor(f"{name}_xn", [P, 4, D], F32))
        top = local.enter_context(nc.sbuf_tensor(f"{name}_norm_top", [P, 2], F32))
        tmp = local.enter_context(nc.sbuf_tensor(f"{name}_norm_tmp", [P, D], F32))
        turned = local.enter_context(nc.psum_tensor(f"{name}_turned", [P, 4, DC, P], F32))
        with nc.Block() as block:
            @block.vector
            def _(dve):
                links, count = env.sem("links"), [0]

                def link(ins):
                    count[0] += 1
                    ins.then_inc(links, 1)
                    dve.wait_ge(links, count[0])

                for t in range(TILES):
                    nc.vector.bn_stats(stats[:, t, :], env.x[:, t, :]).then_inc(stats_done, 1)
                for t in range(TILES):
                    dve.wait_ge(stats_done, t + 1)
                    nc.vector.bn_aggr(meanvar[:, t, :], stats[:, t, :]).then_inc(var_done, 1)
                dve.wait_ge(sd_done, 1)
                nc.vector.reciprocal(rstd[:], sd[:]).then_inc(rstd_done, 1)
                dve.wait_ge(rstd_done, 1)
                for t in range(TILES):
                    if t >= 4:
                        dve.wait_ge(transposed, t - 3)
                    row = xn[:, t % 4, :]
                    last = nc.vector.tensor_scalar(row, env.x[:, t, :], meanvar[:, t, 0:1], rstd[:, t:t + 1],
                                                   ALU.subtract, ALU.mult)
                    if quantised:
                        link(last)
                        quantise_rows(nc, link, row, row, top, tmp[:])
                        dve.sem_inc(xn_done, 1)
                    else:
                        last.then_inc(xn_done, 1)
                if split:
                    high, low = split
                    for t in range(TILES):
                        cols = slice(t * P, (t + 1) * P)
                        dve.wait_ge(copied, t + 1)
                        dve.wait_ge(high_done, t + 1)
                        nc.vector.tensor_tensor(low[:, :, cols], env.xT[:, :, cols], high[:, :, cols].bitcast(F32),
                                                ALU.subtract).then_inc(low_done, 1)
                    dve.wait_ge(low_done, TILES)

            @block.tensor
            def _(pe):
                for t in range(TILES):
                    pe.wait_ge(xn_done, t + 1)
                    if t >= 4:
                        pe.wait_ge(copied, t - 3)
                    for c in range(DC):
                        last = nc.tensor.transpose(turned[:, t % 4, c, :], xn[:, t % 4, c * P:(c + 1) * P], env.ident[:])
                    last.then_inc(transposed, 1)

            @block.scalar
            def _(act):
                act.wait_ge(var_done, TILES)
                nc.scalar.activation(sd[:], meanvar[:, :, 1], ACT.Sqrt, bias=env.eps_ln[:]).then_inc(sd_done, 1)
                for t in range(TILES):
                    act.wait_ge(transposed, t + 1)
                    cols = slice(t * P, (t + 1) * P)
                    nc.scalar.copy(env.xT[:, :, cols], turned[:, t % 4]).then_inc(copied, 1)
                    if split:
                        act.wait_ge(copied, t + 1)
                        nc.scalar.copy(split[0][:, :, cols], env.xT[:, :, cols]).then_inc(high_done, 1)
                act.wait_ge(copied, TILES)


def ternary_scales(env, name, scale, half, neg_half, gate, weight):
    nc, io = env.nc, env.io
    env.prefix = f"{name}_scales"
    G, E = io["w1"].shape[0], io["w1"].shape[2] // DC
    elements = G * E * D
    loaded = [env.sem(f"loaded{s}") for s in range(3)]
    summed, total_done, used = env.sem("summed"), env.sem("total_done"), env.sem("used")
    ones_made, steps, scaled = env.sem("ones_made"), env.sem("steps"), env.sem("scaled")
    with ExitStack() as local:
        raw = local.enter_context(nc.sbuf_tensor(f"{name}_absw", [P, 3, G * E * D // P], F32))
        partial = local.enter_context(nc.sbuf_tensor(f"{name}_partial", [P, 3], F32))
        ones = local.enter_context(nc.sbuf_tensor(f"{name}_ones", [P, P], F32))
        total = local.enter_context(nc.psum_tensor(f"{name}_total", [P, 512], F32))
        with nc.Block() as block:
            @block.sync
            def _(sp):
                for m, w in enumerate(("w1", "w2")):
                    sp.dma_start(raw[:, m, :].rearrange("p (g n) -> p g n", g=G),
                                 io[w].rearrange("g p n -> p g n")).then_inc(loaded[m], 16)
                sp.dma_start(raw[:, 2, :].rearrange("p (r n) -> p r n", n=D),
                             io["w3"].rearrange("g (r p) n -> p (g r) n", p=P)).then_inc(loaded[2], 16)

            @block.vector
            def _(dve):
                nc.vector.memset(ones[:], 1.0).then_inc(ones_made, 1)
                for m in range(3):
                    dve.wait_ge(loaded[m], 16)
                    nc.vector.tensor_reduce(partial[:, m:m + 1], raw[:, m, :], AX_X, ALU.add,
                                            apply_absolute_value=True).then_inc(summed, 1)
                dve.wait_ge(total_done, 1)
                nc.vector.tensor_scalar(scale[:], total[:, 0:3], 1.0 / elements, EPS_TERNARY, ALU.mult,
                                        ALU.add).then_inc(scaled, 1)
                dve.wait_ge(scaled, 1)
                nc.vector.tensor_scalar(half[:], scale[:], 0.5, None, ALU.mult).then_inc(scaled, 1)
                nc.vector.tensor_scalar(neg_half[:], scale[:], -0.5, None, ALU.mult).then_inc(scaled, 1)
                dve.wait_ge(scaled, 3)
                nc.vector.tensor_scalar(weight[:], scale[:, 1:2], scale[:, 2:3], gate, ALU.mult, ALU.mult).then_inc(scaled, 1)
                dve.wait_ge(scaled, 4)

            @block.tensor
            def _(pe):
                pe.wait_ge(ones_made, 1)
                pe.wait_ge(summed, 3)
                nc.tensor.matmul(total[:, 0:3], ones[:], partial[:], start=True, stop=True).then_inc(total_done, 1)


def ffn_block(env, name, chunks, weight, x_parts, ternary=None, peer=None):
    nc, io = env.nc, env.io
    env.prefix = name
    w1, w2, w3 = io["w1"], io.get("w2"), io["w3"]
    G, E = w1.shape[0], w1.shape[2] // DC
    NCH = len(chunks)
    starts = [sum(chunks[:c]) for c in range(NCH)]
    FULL = E // P
    STEPS = NCH * HALVES
    PAIRS = 2
    YB = 4
    SIDES = 1 if peer else 2
    UP_INC, DOWN_INC = 16 * SIDES, 16 * (bool(FULL) + bool(E % P))
    ADDS = TILES * (PEER_HEADS - 1) + 1
    SPLIT_DOWN = not peer
    RAW = 1 if SPLIT_DOWN else 2
    assert G % 2 == 0
    after = [range(k * TILES // STEPS, (k + 1) * TILES // STEPS) for k in range(STEPS)]
    up_loaded, down_loaded = env.sem("up_loaded"), [env.sem(f"down_loaded{s}") for s in range(RAW)]
    hidden_psum, silu_done = env.sem("hidden_psum"), env.sem("silu_done")
    product_done = env.sem("product_done")
    hidden_done = env.sem("hidden_done") if SPLIT_DOWN else product_done
    high_done = env.sem("high_done")
    y_done = env.sem("y_done")
    y_used = env.sem("y_used")
    up_high, up_ready = env.sem("up_high"), env.sem("up_ready")
    down_high, down_ready = env.sem("down_high"), env.sem("down_ready")
    UP_READY = SIDES
    if peer:
        sums_done, added = env.sem("sums_done"), env.sem("added")
        kept_done = env.sem("kept_done")
    with ExitStack() as local:
        def sb(n, shape, dt=F32):
            return local.enter_context(nc.sbuf_tensor(f"{name}_{n}", shape, dt))

        up_in = sb("up_in", [P, SIDES, DC * E])
        down_in = sb("down_in", [P, RAW, NCH, D])
        NW = 1 if ternary else 2
        up_parts = [sb(f"up_{n}", [P, 2, SIDES, DC * E], F32R) for n in ("high", "low")[:NW]]
        if SPLIT_DOWN:
            down_parts = [sb(f"down_{n}", [P, 2, NCH, D], F32R) for n in ("high", "low")[:NW]]
            h_parts = [sb("h_high", [P, 2, NCH, TOK], F32R), sb("h_low", [P, 2, NCH, TOK], F32R)]
            product = sb("product", [P, PAIRS, HALF])
        else:
            down_parts, h_parts = [down_in], [sb("h", [P, 2, NCH, TOK])]
        if ternary:
            scale, half, neg_half = ternary
            low_sign = sb("low_sign", [P, DC * E])
        silu_sb = sb("silu", [P, PAIRS, HALF])
        if peer:
            sims, bar, extra = peer
            I1 = E // NK
            routes = sb("routes", [P, 2, TILES, E])
            sums = sb("sums", [P, 2, E])
            kept = sb("kept", [P, 2, E])
        hidden_ps = local.enter_context(nc.psum_tensor(f"{name}_hidden", [P, PAIRS, 2, HALF], F32))
        y_ps = local.enter_context(nc.psum_tensor(f"{name}_y", [P, YB, D], F32))

        def terms(a, b):
            return [(m, n) for m in range(len(a)) for n in range(len(b)) if m + n < 2]

        with nc.Block() as block:
            @block.sync
            def _(sp):
                def load_up(g):
                    for side, w in enumerate((w1, w2)[:SIDES]):
                        sp.dma_start(up_in[:, side, :], w[bass.ds(g, 1)].rearrange("g p n -> p (g n)")).then_inc(
                            up_loaded, 16)

                def load_down(g, s):
                    if FULL:
                        sp.dma_start(down_in[:, s, 0:FULL, :],
                                     w3[bass.ds(g, 1), 0:FULL * P, :].rearrange("g (c p) n -> p (g c) n", p=P)).then_inc(
                                         down_loaded[s], 16)
                    if E % P:
                        sp.dma_start(down_in[0:E % P, s, FULL, :],
                                     w3[bass.ds(g, 1), FULL * P:E, :].rearrange("g p n -> p (g n)")).then_inc(
                                         down_loaded[s], 16)

                load_up(0)
                load_down(0, 0)
                if RAW == 1:
                    with sp.Fori(1, G) as g:
                        sp.wait_ge(up_ready, UP_READY * g)
                        load_up(g)
                        sp.wait_ge(down_ready, g)
                        load_down(g, 0)
                else:
                    sp.wait_ge(up_ready, UP_READY)
                    load_up(1)
                    load_down(1, 1)
                    with sp.Fori(1, G // 2) as j:
                        for s in range(2):
                            g = 2 * j + s
                            sp.wait_ge(up_ready, UP_READY * g)
                            load_up(g)
                            sp.wait_ge(y_used, g * TILES)
                            load_down(g, s)

            @block.tensor
            def _(pe):
                up_pairs = [(i, m, n) for i in range(DC) for m, n in terms(up_parts, x_parts)]
                down_pairs = [(c, m, n) for c in range(NCH) for m, n in terms(h_parts, down_parts)]

                def up_step(g, s, k):
                    if k == 0:
                        pe.wait_ge(up_ready, UP_READY * (g + 1))
                        if peer:
                            pe.wait_ge(added, ADDS * (g + 1))
                    c, h, b = k // HALVES, k % HALVES, k % PAIRS
                    m, e0 = chunks[c], starts[c]
                    pe.wait_ge(product_done, g * STEPS + k + 1)
                    for side in range(SIDES):
                        for q, (i, wp, xp) in enumerate(up_pairs):
                            w = up_parts[wp][:, s, side].rearrange("p (c e) -> p c e", c=DC)
                            last = nc.tensor.matmul(hidden_ps[0:m, b, side, :], w[:, i, e0:e0 + m],
                                                    x_parts[xp][:, i, h * HALF:(h + 1) * HALF],
                                                    start=(q == 0), stop=(q == len(up_pairs) - 1))
                    if peer:
                        for t in range(HALF // P):
                            last = nc.tensor.transpose(hidden_ps[:, b, 1, t * P:(t + 1) * P],
                                                       routes[:, s, h * (HALF // P) + t, c * P:(c + 1) * P],
                                                       env.ident[:])
                    last.then_inc(hidden_psum, 1)

                def down_tile(g, s, t, loads):
                    if t == 0:
                        pe.wait_ge(hidden_done, PAIRS + (g + 1) * STEPS)
                        if SPLIT_DOWN:
                            pe.wait_ge(down_ready, g + 1)
                        else:
                            pe.wait_ge(down_loaded[s], DOWN_INC * loads)
                    pe.wait_ge(y_used, g * TILES + t + 1 + TILES - YB)
                    for q, (c, hp, wp) in enumerate(down_pairs):
                        m = chunks[c]
                        last = nc.tensor.matmul(y_ps[:, t % YB, :], h_parts[hp][0:m, s, c, t * P:(t + 1) * P],
                                                down_parts[wp][0:m, s, c, :], start=(q == 0), stop=(q == len(down_pairs) - 1))
                    last.then_inc(y_done, 1)

                def group(g, s, loads):
                    for k in range(STEPS):
                        up_step(g, s, k)
                        for t in after[k]:
                            down_tile(g - 1, 1 - s, t, loads)

                for k in range(STEPS):
                    up_step(0, 0, k)
                with pe.Fori(0, G // 2 - 1) as j:
                    group(2 * j + 1, 1, j + 1)
                    group(2 * j + 2, 0, j + 1)
                group(G - 1, 1, G // 2)
                for t in range(TILES):
                    down_tile(G - 1, 1, t, G // 2)

            @block.scalar
            def _(act):
                def high_up(g, s, side):
                    if side == 0:
                        act.wait_ge(up_loaded, UP_INC * (g + 1))
                    nc.scalar.copy(up_parts[0][:, s, side, :], up_in[:, side, :]).then_inc(up_high, 1)

                def high_down(g, s, c):
                    if c == 0:
                        act.wait_ge(down_loaded[0], DOWN_INC * (g + 1))
                        if not isinstance(g, int) or g >= 2:
                            act.wait_ge(y_used, g * TILES)
                    m = chunks[c]
                    nc.scalar.copy(down_parts[0][0:m, s, c, :], down_in[0:m, 0, c, :]).then_inc(down_high, 1)

                def silu(g, k):
                    m, b = chunks[k // HALVES], k % PAIRS
                    act.wait_ge(hidden_psum, g * STEPS + k + 1)
                    act.wait_ge(product_done, g * STEPS + k + 1)
                    nc.scalar.activation(silu_sb[0:m, b, :], hidden_ps[0:m, b, 0, :], ACT.Silu,
                                         scale=scale[0:m, 0:1] if ternary else 1.0).then_inc(silu_done, 1)

                def high_hidden(g, s, k):
                    c, h, b = k // HALVES, k % HALVES, k % PAIRS
                    m = chunks[c]
                    act.wait_ge(product_done, PAIRS + g * STEPS + k + 1)
                    nc.scalar.copy(h_parts[0][0:m, s, c, h * HALF:(h + 1) * HALF], product[0:m, b, :]).then_inc(high_done, 1)

                def group(g, s, last=False):
                    for k in range(STEPS + 1):
                        if k < STEPS:
                            silu(g, k)
                        if SPLIT_DOWN and k:
                            high_hidden(g, s, k - 1)
                        if not ternary:
                            if k < SIDES and not last:
                                high_up(g + 1, 1 - s, k)
                            if SPLIT_DOWN and 1 <= k <= NCH:
                                high_down(g, s, k - 1)

                if not ternary:
                    for side in range(SIDES):
                        high_up(0, 0, side)
                group(0, 0)
                with act.Fori(0, G // 2 - 1) as j:
                    group(2 * j + 1, 1)
                    group(2 * j + 2, 0)
                group(G - 1, 1, last=True)

            if not ternary:
                @block.gpsimd
                def _(pool):
                    def low_up(g, s):
                        for side in range(SIDES):
                            pool.wait_ge(up_high, SIDES * g + side + 1)
                            nc.gpsimd.tensor_tensor(up_parts[1][:, s, side, :], up_in[:, side, :],
                                                    up_parts[0][:, s, side, :].bitcast(F32), ALU.subtract).then_inc(up_ready, 1)

                    def low_down(g, s):
                        for c in range(NCH):
                            m = chunks[c]
                            pool.wait_ge(down_high, NCH * g + c + 1)
                            last = nc.gpsimd.tensor_tensor(down_parts[1][0:m, s, c, :], down_in[0:m, 0, c, :],
                                                           down_parts[0][0:m, s, c, :].bitcast(F32), ALU.subtract)
                            last.then_inc(*((down_ready, 1) if c == NCH - 1 else (down_part, 1)))

                    def pair_sums(g, tiles):
                        for t in tiles:
                            for h in range(PEER_HEADS):
                                n = t * PEER_HEADS + h
                                pool.wait_ge(kept_done, g * TILES * PEER_HEADS + n + 1)
                                first = sims[:, t, h, bass.ds(g * I1, I1)].unsqueeze(2).to_broadcast([P, I1, NK])
                                second = sims[:, t, h, KEY_ROWS:KEY_ROWS + NK].unsqueeze(1).to_broadcast([P, I1, NK])
                                nc.gpsimd.tensor_tensor(sums[:, n % 2, :].rearrange("p (a b) -> p a b", a=I1),
                                                        first, second, ALU.add).then_inc(sums_done, 1)

                    def group(g, s, last=False):
                        if peer and not last:
                            pair_sums(g + 1, range(TILES // 2))
                        if not last:
                            low_up(g + 1, 1 - s)
                        if SPLIT_DOWN:
                            low_down(g, s)
                        if peer and not last:
                            pair_sums(g + 1, range(TILES // 2, TILES))

                    down_part = env.sem("down_part")
                    low_up(0, 0)
                    if peer:
                        pair_sums(0, range(TILES))
                    group(0, 0)
                    with pool.Fori(0, G // 2 - 1) as j:
                        group(2 * j + 1, 1)
                        group(2 * j + 2, 0)
                    group(G - 1, 1, last=True)

            @block.vector
            def _(dve):
                def hidden_step(g, s, k):
                    if k < STEPS:
                        c, h, b = k // HALVES, k % HALVES, k % PAIRS
                        m, cols = chunks[c], slice(h * HALF, (h + 1) * HALF)
                        dve.wait_ge(silu_done, g * STEPS + k + 1)
                        if SPLIT_DOWN:
                            dve.wait_ge(hidden_done, g * STEPS + k + 1)
                        out = product[0:m, b, :] if SPLIT_DOWN else h_parts[0][0:m, s, c, cols]
                        nc.vector.tensor_tensor(out, silu_sb[0:m, b, :], hidden_ps[0:m, b, 1, :], ALU.mult).then_inc(
                            product_done, 1)
                    if SPLIT_DOWN and k:
                        c, h, b = (k - 1) // HALVES, (k - 1) % HALVES, (k - 1) % PAIRS
                        m, cols = chunks[c], slice(h * HALF, (h + 1) * HALF)
                        dve.wait_ge(high_done, g * STEPS + k)
                        nc.vector.tensor_tensor(h_parts[1][0:m, s, c, cols], product[0:m, b, :],
                                                h_parts[0][0:m, s, c, cols].bitcast(F32), ALU.subtract).then_inc(hidden_done, 1)

                def output(g, t):
                    w = weight[:, 0:1] if len(weight.shape) == 2 else weight[:, t, bass.ds(g, 1)]
                    dve.wait_ge(y_done, g * TILES + t + 1)
                    dve.wait_ge(y_used, g * TILES + t + 1)
                    nc.vector.scalar_tensor_tensor(env.x[:, t, :], y_ps[:, t % YB, :], w, env.x[:, t, :],
                                                   ALU.mult, ALU.add).then_inc(y_used, 1)

                def quantise_up(g, s, side):
                    dve.wait_ge(up_loaded, UP_INC * (g + 1))
                    nc.vector.tensor_scalar(low_sign[:], up_in[:, side, :], neg_half[:, side:side + 1], None,
                                            ALU.is_lt).then_inc(up_high, 1)
                    dve.wait_ge(up_high, SIDES * g + side + 1)
                    nc.vector.scalar_tensor_tensor(up_parts[0][:, s, side, :], up_in[:, side, :], half[:, side:side + 1],
                                                   low_sign[:], ALU.is_gt, ALU.subtract).then_inc(up_ready, 1)
                    dve.wait_ge(up_ready, SIDES * g + side + 1)

                def quantise_down(g, s):
                    dve.wait_ge(down_loaded[0], DOWN_INC * (g + 1))
                    src = down_in[:, 0].rearrange("p c e -> p (c e)")
                    nc.vector.tensor_scalar(low_sign[:], src, neg_half[:, 2:3], None, ALU.is_lt).then_inc(down_high, 1)
                    dve.wait_ge(down_high, g + 1)
                    nc.vector.scalar_tensor_tensor(down_parts[0][:, s].rearrange("p c e -> p (c e)"), src, half[:, 2:3],
                                                   low_sign[:], ALU.is_gt, ALU.subtract).then_inc(down_ready, 1)
                    dve.wait_ge(down_ready, g + 1)

                def routes_tile(g, s, t):
                    row = routes[:, s, t, :]
                    for h in range(PEER_HEADS):
                        n = t * PEER_HEADS + h
                        n_all = g * TILES * PEER_HEADS + n
                        b = bar[:, n:n + 1]
                        dve.wait_ge(sums_done, n_all + 1)
                        to = kept[:, n % 2, :] if h else row
                        nc.vector.scalar_tensor_tensor(to, sums[:, n % 2, :], b, sums[:, n % 2, :], ALU.is_ge,
                                                       ALU.mult).then_inc(kept_done, 1)
                        dve.wait_ge(kept_done, 2 + n_all + 1)
                        if h:
                            nc.vector.tensor_tensor(row, row, kept[:, n % 2, :], ALU.add).then_inc(added, 1)
                            dve.wait_ge(added, g * ADDS + t * (PEER_HEADS - 1) + h)

                def routes_end(g, s):
                    nc.vector.tensor_tensor(routes[:, s, :, E - 1], routes[:, s, :, E - 1],
                                            extra[:, bass.ds(g, 1), :].rearrange("p g t -> p (g t)"), ALU.add).then_inc(
                                                added, 1)

                def group(g, s, first=False, last=False):
                    for k in range(STEPS + SPLIT_DOWN):
                        hidden_step(g, s, k)
                        if peer and not last:
                            routes_tile(g + 1, 1 - s, k)
                        if k < STEPS and not first:
                            for t in after[k]:
                                output(g - 1, t)
                        if ternary:
                            if k < SIDES and not last:
                                quantise_up(g + 1, 1 - s, k)
                            if k == SIDES:
                                quantise_down(g, s)
                    if peer and not last:
                        routes_end(g + 1, 1 - s)

                dve.sem_inc(product_done, PAIRS)
                if SPLIT_DOWN:
                    dve.sem_inc(hidden_done, PAIRS)
                dve.sem_inc(y_used, TILES)
                if peer:
                    dve.sem_inc(kept_done, 2)
                    for t in range(TILES):
                        routes_tile(0, 0, t)
                    routes_end(0, 0)
                if ternary:
                    for side in range(SIDES):
                        quantise_up(0, 0, side)
                group(0, 0, first=True)
                with dve.Fori(0, G // 2 - 1) as j:
                    group(2 * j + 1, 1)
                    group(2 * j + 2, 0)
                group(G - 1, 1, last=True)
                for t in range(TILES):
                    output(G - 1, t)
                dve.wait_ge(y_used, TILES + G * TILES)


def expert_weights_block(env, name, G, shared, normalise, gate, weight):
    nc, io = env.nc, env.io
    env.prefix = f"{name}_experts"
    EX = 8
    N = EX + (1 if shared else 0)
    loaded, logits_done, step, exp_done = env.sem("loaded"), env.sem("logits_done"), env.sem("step"), env.sem("exp_done")
    with ExitStack() as local:
        def sb(n, shape, dt=F32):
            return local.enter_context(nc.sbuf_tensor(f"{name}_{n}", shape, dt))

        w = sb("router", [P, DC, N])
        logits, top, index = sb("logits", [P, TILES, N]), sb("top", [P, TILES, 8]), sb("index", [P, TILES, 8], U32)
        index_f, less_max, exps = sb("index_f", [P, TILES, 8]), sb("less_max", [P, TILES, 9]), sb("exps", [P, TILES, 9])
        total, inv, pick = sb("total", [P, TILES, 2]), sb("inv", [P, TILES, 2]), sb("pick", [P, 2, TILES, EX])
        ps = local.enter_context(nc.psum_tensor(f"{name}_router_ps", [P, TILES, 16], F32))
        with nc.Block() as block:
            @block.sync
            def _(sp):
                sp.dma_start(w[:], io["router"]).then_inc(loaded, 16)

            @block.tensor
            def _(pe):
                pe.wait_ge(loaded, 16)
                for t in range(TILES):
                    for i in range(DC):
                        last = nc.tensor.matmul(ps[:, t, 0:N], env.xT[:, i, t * P:(t + 1) * P], w[:, i, :],
                                                start=(i == 0), stop=(i == DC - 1))
                last.then_inc(logits_done, 1)

            @block.scalar
            def _(act):
                act.wait_ge(step, 1)
                nc.scalar.activation(exps[:, :, 0:N], less_max[:, :, 0:N], ACT.Exp).then_inc(exp_done, 1)

            @block.vector
            def _(dve):
                links = env.sem("links")
                count = [0]

                def link(ins):
                    count[0] += 1
                    ins.then_inc(links, 1)
                    dve.wait_ge(links, count[0])

                def spread(ap, n=EX):
                    return ap.to_broadcast([P, TILES, n])

                dve.wait_ge(logits_done, 1)
                link(nc.vector.tensor_copy(logits[:], ps[:, :, 0:N]))
                for t in range(TILES):
                    link(nc.vector.max(top[:, t, :], logits[:, t, 0:EX]))
                    link(nc.vector.max_index(index[:, t, :], top[:, t, :], logits[:, t, 0:EX]))
                link(nc.vector.tensor_copy(index_f[:], index[:]))
                link(nc.vector.tensor_tensor(less_max[:, :, 0:EX], top[:], spread(top[:, :, 0:1]), ALU.subtract))
                if shared:
                    link(nc.vector.tensor_scalar(less_max[:, :, EX:N], logits[:, :, EX:N], -1.0, None, ALU.mult))
                dve.sem_inc(step, 1)
                dve.wait_ge(exp_done, 1)
                link(nc.vector.tensor_reduce(total[:, :, 0], exps[:, :, 0:2 if normalise else EX], AX_X, ALU.add))
                if shared:
                    link(nc.vector.tensor_scalar(total[:, :, 1:2], exps[:, :, EX:N], 1.0, None, ALU.add))
                n = 2 if shared else 1
                link(nc.vector.reciprocal(inv[:, :, 0:n], total[:, :, 0:n]))
                for p in range(2):
                    link(nc.vector.tensor_tensor(pick[:, p], spread(index_f[:, :, p:p + 1]),
                                                 env.iota8[:].unsqueeze(1).to_broadcast([P, TILES, EX]), ALU.is_equal))
                    link(nc.vector.tensor_tensor(pick[:, p], pick[:, p], spread(exps[:, :, p:p + 1]), ALU.mult))
                link(nc.vector.tensor_tensor(pick[:, 0], pick[:, 0], pick[:, 1], ALU.add))
                link(nc.vector.tensor_tensor(pick[:, 1], pick[:, 0], spread(inv[:, :, 0:1]), ALU.mult))
                link(nc.vector.tensor_scalar(weight[:, :, shared:G], pick[:, 1], gate, None, ALU.mult))
                if shared:
                    link(nc.vector.tensor_scalar(weight[:, :, 0:shared], spread(inv[:, :, 1:2], shared), gate, None,
                                                 ALU.mult))


def product_keys_block(env, name, sims, bar, extra, G):
    nc, io = env.nc, env.io
    env.prefix = f"{name}_keys"
    H = PEER_HEADS
    wq_loaded, keys_loaded, keys_clear = env.sem("wq_loaded"), env.sem("keys_loaded"), env.sem("keys_clear")
    q_psum, q_done, sims_psum, sims_done = env.sem("q_psum"), env.sem("q_done"), env.sem("sims_psum"), env.sem("sims_done")
    kept_done, tile_done = env.sem("kept_done"), env.sem("tile_done")
    with ExitStack() as local:
        def sb(n, shape, dt=F32):
            return local.enter_context(nc.sbuf_tensor(f"{name}_{n}", shape, dt))

        wq, keys, qT = sb("wq", [P, DC, D]), sb("keys", [P, H, 2 * NK]), sb("qT", [P, H, TOK])
        full = sb("full", [P, 2, H, 2 * NK])
        best, index = sb("best", [P, 2, H, 2, 8]), sb("index", [P, 2, H, 8], U32)
        past, pairs, top = sb("past", [P, H, 8]), sb("pairs", [P, H, 8, 8]), sb("top", [P, H, 8])
        reach = sb("reach", [P, H, 8, 8])
        q_ps = local.enter_context(nc.psum_tensor(f"{name}_q_ps", [P, 4, HALF], F32))
        sims_ps = local.enter_context(nc.psum_tensor(f"{name}_sims_ps", [P, 2, H, 2 * NK], F32))
        with nc.Block() as block:
            @block.sync
            def _(sp):
                sp.dma_start(wq[:], io["wq"]).then_inc(wq_loaded, 16)
                sp.wait_ge(keys_clear, 1)
                for side in range(2):
                    sp.dma_start(keys[64 * side:64 * side + 64, :, side * NK:(side + 1) * NK],
                                 io["keys"][:, side]).then_inc(keys_loaded, 16)

            @block.tensor
            def _(pe):
                pe.wait_ge(wq_loaded, 16)
                for n in range(H * HALVES):
                    f, h = n // HALVES, n % HALVES
                    if n >= 4:
                        pe.wait_ge(q_done, n - 3)
                    for i in range(DC):
                        last = nc.tensor.matmul(q_ps[:, n % 4, :], wq[:, i, f * P:(f + 1) * P],
                                                env.xT[:, i, h * HALF:(h + 1) * HALF], start=(i == 0), stop=(i == DC - 1))
                    last.then_inc(q_psum, 1)
                pe.wait_ge(keys_loaded, 32)
                pe.wait_ge(q_done, H * HALVES)
                for t in range(TILES):
                    if t >= 2:
                        pe.wait_ge(sims_done, t - 1)
                    for f in range(H):
                        last = nc.tensor.matmul(sims_ps[:, t % 2, f, :], qT[:, f, t * P:(t + 1) * P], keys[:, f, :],
                                                start=True, stop=True)
                    last.then_inc(sims_psum, 1)

            @block.scalar
            def _(act):
                for n in range(H * HALVES):
                    f, h = n // HALVES, n % HALVES
                    act.wait_ge(q_psum, n + 1)
                    nc.scalar.copy(qT[:, f, h * HALF:(h + 1) * HALF], q_ps[:, n % 4, :]).then_inc(q_done, 1)
                for t in range(TILES):
                    act.wait_ge(sims_psum, t + 1)
                    if t >= 2:
                        act.wait_ge(tile_done, t - 1)
                    nc.scalar.copy(full[:, t % 2], sims_ps[:, t % 2]).then_inc(sims_done, 1)
                    act.wait_ge(sims_done, t + 1)
                    nc.scalar.copy(sims[:, t, :, 0:KEY_ROWS], full[:, t % 2, :, 0:KEY_ROWS]).then_inc(kept_done, 1)
                    nc.scalar.copy(sims[:, t, :, KEY_ROWS:], full[:, t % 2, :, NK:2 * NK]).then_inc(kept_done, 1)
                act.wait_ge(kept_done, 2 * TILES)

            @block.vector
            def _(dve):
                links = env.sem("links")
                count = [0]

                def link(ins, wait=True):
                    count[0] += 1
                    ins.then_inc(links, 1)
                    if wait:
                        dve.wait_ge(links, count[0])

                nc.vector.memset(keys[:], 0.0).then_inc(keys_clear, 1)
                link(nc.vector.memset(extra[:], 0.0))
                for t in range(TILES):
                    u = t % 2
                    dve.wait_ge(sims_done, t + 1)
                    for f in range(H):
                        for side in range(2):
                            link(nc.vector.max(best[:, u, f, side, :], full[:, u, f, side * NK:(side + 1) * NK]),
                                 wait=(f == H - 1 and side == 1))
                    for f in range(H):
                        link(nc.vector.max_index(index[:, u, f, :], best[:, u, f, 0, :], full[:, u, f, 0:NK]), wait=False)
                        link(nc.vector.tensor_tensor(pairs[:, f],
                                                     best[:, u, f, 0, :].unsqueeze(2).to_broadcast([P, 8, 8]),
                                                     best[:, u, f, 1, :].unsqueeze(1).to_broadcast([P, 8, 8]), ALU.add),
                             wait=(f == H - 1))
                    for f in range(H):
                        link(nc.vector.max(top[:, f, :], pairs[:, f].rearrange("p a b -> p (a b)")), wait=(f == H - 1))
                    link(nc.vector.tensor_scalar(bar[:, t * H:(t + 1) * H], top[:, :, 7], 0.0, None, ALU.max), wait=False)
                    link(nc.vector.tensor_scalar(past[:], index[:, u], KEY_ROWS - 0.5, None, ALU.is_gt))
                    for f in range(H):
                        b = bar[:, t * H + f:t * H + f + 1]
                        flat = pairs[:, f].rearrange("p a b -> p (a b)")
                        link(nc.vector.scalar_tensor_tensor(reach[:, f].rearrange("p a b -> p (a b)"), flat, b, flat,
                                                            ALU.is_ge, ALU.mult), wait=(f == H - 1))
                    link(nc.vector.tensor_tensor(reach[:].rearrange("p f a b -> p (f a) b"),
                                                 reach[:].rearrange("p f a b -> p (f a) b"),
                                                 past[:].rearrange("p f a -> p (f a)").unsqueeze(2).to_broadcast([P, H * 8, 8]),
                                                 ALU.mult))
                    link(nc.vector.tensor_reduce(extra[:, G - 1, t:t + 1], reach[:].rearrange("p f a b -> p (f a b)"),
                                                 AX_X, ALU.add))
                    dve.sem_inc(tile_done, 1)


def softmax_attention_block(env, name, heads_out, keep_mask=None):
    nc, io = env.nc, env.io
    env.prefix = f"{name}_attn"
    bounded = keep_mask is not None
    HEADS, HD = 16, 32
    FG, HG = 4, 4
    VC = HD + 1
    KT, QT = CTX // P, SEQ // P
    CT = BATCH * KT
    SCALE = HD ** -0.5
    BOUND = 50.0
    UNITS = HG * (KT if bounded else QT)
    PRODUCTS = CTX // HALF + 1
    S_SLOTS, O_SLOTS, P_SLOTS = (3, 4, 1) if bounded else (2, 2, 2)
    ctx_loaded, wv_loaded, w_loaded = (env.sem("ctx_loaded"), env.sem("wv_loaded"),
                                       env.sem("w_loaded"))
    ones_made, v_psum, v_done = env.sem("ones_made"), env.sem("v_psum"), env.sem("v_done")
    proj_psum, high_done, low_done = env.sem("proj_psum"), env.sem("high_done"), env.sem("low_done")
    k_stacked, q_stacked, group_done = env.sem("k_stacked"), env.sem("q_stacked"), env.sem("group_done")
    scores_done, exp_done = env.sem("scores_done"), env.sem("exp_done")
    pv_done, norm_done, inv_done = env.sem("pv_done"), env.sem("norm_done"), env.sem("inv_done")
    if bounded:
        clipped = env.sem("clipped")
    else:
        max_done, bias_done = env.sem("max_done"), env.sem("bias_done")
        turned = [env.sem(f"turned{i}") for i in range(2)]
        copied = [env.sem(f"copied{i}") for i in range(2)]
    with ExitStack() as local:
        def sb(n, shape, dt=F32):
            return local.enter_context(nc.sbuf_tensor(f"{name}_{n}", shape, dt))

        def psum(n, shape):
            return local.enter_context(nc.psum_tensor(f"{name}_{n}", shape, F32))

        ctxT = sb("ctxT", [P, DC, BATCH * CTX])
        values = sb("values", [P, CT, HEADS, VC])
        k_stack, q_stack = sb("k_stack", [P, 2, HG, CTX], F32R), sb("q_stack", [P, 2, HG, SEQ], F32R)
        kh, kl = sb("kh", [P, CTX], F32R), sb("kl", [P, CTX], F32R)
        qh, ql = sb("qh", [P, SEQ], F32R), sb("ql", [P, SEQ], F32R)
        wk, wq = sb("wk", [P, DC * P]), sb("wq", [P, DC * P])
        bk, bq = sb("bk", [P, 1]), sb("bq", [P, 1])
        probs, probsT = sb("probs", [P, 2, CTX]), sb("probsT", [P, 2, KT * P])
        wv = probs[:].rearrange("p a (b n) -> p (a b) n", n=D)
        bv = probsT[:, 0, 0:D]
        inv = sb("inv", [P, 2, HG, 1])
        small = sb("small", [P, 2, 2])
        o_ps = psum("o_ps", [P, O_SLOTS, HALF])
        s_ps = psum("s_ps", [P, S_SLOTS, HALF if bounded else CTX])
        t_ps = psum("t_ps", [P, P_SLOTS, HALF])

        pT4 = probsT[:].rearrange("p a (b n) -> p (a b) n", n=SEQ)

        with nc.Block() as block:
            @block.sync
            def _(sp):
                sp.dma_start(wv, io["wv"]).then_inc(wv_loaded, 16)
                sp.dma_start(bv, io["bv"].partition_broadcast(P)).then_inc(wv_loaded, 16)
                for b in range(BATCH):
                    sp.dma_start(ctxT[:, :, b * CTX:(b + 1) * CTX], io["ctxT"][:, :, b * CTX:(b + 1) * CTX]).then_inc(
                        ctx_loaded, 16)
                    sp.wait_ge(ctx_loaded, 16 * (b + 1))

                def load_weights(f):
                    for to, of in ((wk, "wk"), (wq, "wq"), (bk, "bk"), (bq, "bq")):
                        sp.dma_start(to[:], io[of][bass.ds(f, 1)].rearrange("g p n -> p (g n)")).then_inc(w_loaded, 16)

                def stack(n, s):
                    if not isinstance(n, int) or n >= 2:
                        sp.wait_ge(group_done, n - 1)
                    for what, (dst, halves, sem) in enumerate(((k_stack, (kh, kl, kh, kl), k_stacked),
                                                               (q_stack, (qh, qh, ql, ql), q_stacked))):
                        sp.wait_ge(low_done, P_SLOTS + PRODUCTS * n + (PRODUCTS - 1 if what == 0 else PRODUCTS))
                        for r in range(4):
                            for h in range(HG):
                                sp.dma_start(dst[32 * r:32 * r + 32, s, h, :].bitcast(F32),
                                             halves[r][32 * h:32 * h + 32, :].bitcast(F32)).then_inc(sem, 16)

                load_weights(0)
                stack(0, 0)
                with sp.Fori(0, FG - 1) as f:
                    stack(2 * f + 1, 1)
                    load_weights(f + 1)
                    stack(2 * f + 2, 0)
                stack(2 * FG - 1, 1)

            STACKS = 16 * 16

            @block.tensor
            def _(pe):
                pe.wait_ge(wv_loaded, 32)
                for t in range(CT):
                    pe.wait_ge(ctx_loaded, 16 * (t // KT + 1))
                    if t >= S_SLOTS:
                        pe.wait_ge(v_done, t - S_SLOTS + 1)
                    for i in range(DC):
                        last = nc.tensor.matmul(s_ps[:, t % S_SLOTS, 0:D], ctxT[:, i, t * P:(t + 1) * P], wv[:, i, :],
                                                start=(i == 0), stop=(i == DC - 1))
                    last.then_inc(v_psum, 1)

                def project(f, b):
                    n = 2 * f + b
                    pe.wait_ge(w_loaded, 64 * (f + 1))
                    for i in range(PRODUCTS):
                        w, moving = (wk, ctxT[:, :, b * CTX + i * HALF:b * CTX + (i + 1) * HALF]) if i < PRODUCTS - 1 \
                            else (wq, env.xT[:, :, b * SEQ:(b + 1) * SEQ])
                        pe.wait_ge(low_done, PRODUCTS * n + i + 1)
                        for c in range(DC):
                            last = nc.tensor.matmul(t_ps[:, (PRODUCTS * b + i) % P_SLOTS, :], w[:, c * P:(c + 1) * P], moving[:, c, :],
                                                    start=(c == 0), stop=(c == DC - 1))
                        last.then_inc(proj_psum, 1)

                def attend(f, b):
                    n = 2 * f + b
                    pe.wait_ge(k_stacked, STACKS * (n + 1))
                    pe.wait_ge(q_stacked, STACKS * (n + 1))
                    if not bounded:
                        ahead = n + 1 if isinstance(n, int) and n == 2 * FG - 1 else n + 2
                        pe.wait_ge(low_done, P_SLOTS + PRODUCTS * ahead)

                    def value(h, kt):
                        return values[:, b * KT + kt, bass.ds(HG * f + h, 1), :].rearrange("p a e -> p (a e)")

                    def bounded_scores(u):
                        h, kt = u // KT, u % KT
                        pe.wait_ge(clipped, UNITS * n + u + 1)
                        nc.tensor.matmul(s_ps[:, u % S_SLOTS, :], k_stack[:, b, h, kt * P:(kt + 1) * P], q_stack[:, b, h, :],
                                         start=True, stop=True).then_inc(scores_done, 1)

                    def bounded_pv(u):
                        h, kt = u // KT, u % KT
                        pe.wait_ge(exp_done, UNITS * n + u + 1 + 2)
                        if u == 0:
                            pe.wait_ge(norm_done, QT * (n + 1))
                        for q in range(QT):
                            last = nc.tensor.matmul(o_ps[:, q, h * VC:(h + 1) * VC],
                                                    pT4[:, u % 4, q * P:(q + 1) * P], value(h, kt),
                                                    start=(kt == 0), stop=(kt == KT - 1))
                        last.then_inc(pv_done, 1)

                    def scores(u):
                        q, h = u // HG, u % HG
                        pe.wait_ge(exp_done, UNITS * n + u + 1)
                        for i in range(CTX // HALF):
                            last = nc.tensor.matmul(s_ps[:, u % 2, i * HALF:(i + 1) * HALF],
                                                    q_stack[:, b, h, q * P:(q + 1) * P],
                                                    k_stack[:, b, h, i * HALF:(i + 1) * HALF], start=True, stop=True)
                        last.then_inc(scores_done, 1)

                    def turn(u):
                        pe.wait_ge(exp_done, UNITS * n + u + 1 + 2)
                        for i in range(2):
                            pe.wait_ge(copied[i], UNITS * n + u + 1)
                            for k in range(4):
                                kt = 4 * i + k
                                last = nc.tensor.transpose(t_ps[:, i, k * P:(k + 1) * P],
                                                           probs[:, u % 2, kt * P:(kt + 1) * P], env.ident[:])
                            last.then_inc(turned[i], 1)

                    def pv(u):
                        q, h = u // HG, u % HG
                        if h == 0:
                            pe.wait_ge(norm_done, QT * n + q + 1)
                        for i in range(2):
                            pe.wait_ge(copied[i], UNITS * n + u + 1 + 1)
                            for k in range(4):
                                kt = 4 * i + k
                                last = nc.tensor.matmul(o_ps[:, q % 2, h * VC:(h + 1) * VC], probsT[:, u % 2, kt * P:(kt + 1) * P],
                                                        value(h, kt), start=(kt == 0), stop=(kt == KT - 1))
                        last.then_inc(pv_done, 1)

                    if bounded:
                        LAG = 3
                        for u in range(UNITS + LAG):
                            if u < UNITS:
                                bounded_scores(u)
                            if u >= LAG:
                                bounded_pv(u - LAG)
                    else:
                        for u in range(UNITS + 2):
                            if u < UNITS:
                                scores(u)
                            if 1 <= u <= UNITS:
                                turn(u - 1)
                            if u >= 2:
                                pv(u - 2)
                    pe.drain().then_inc(group_done, 1)

                project(0, 0)
                with pe.Fori(0, FG - 1) as f:
                    project(f, 1)
                    attend(f, 0)
                    project(f + 1, 0)
                    attend(f, 1)
                project(FG - 1, 1)
                attend(FG - 1, 0)
                attend(FG - 1, 1)

            @block.scalar
            def _(act):

                def highs(f, b):
                    n = 2 * f + b
                    for i in range(PRODUCTS):
                        key = i < PRODUCTS - 1
                        if (i == 0 or not key) and (not isinstance(n, int) or n):
                            act.wait_ge(k_stacked if key else q_stacked, STACKS * n)
                        dst = kh[:, i * HALF:(i + 1) * HALF] if key else qh[:]
                        act.wait_ge(proj_psum, PRODUCTS * n + i + 1)
                        nc.scalar.activation(dst, t_ps[:, (PRODUCTS * b + i) % P_SLOTS, :], ACT.Identity,
                                             bias=(bk if key else bq)[:]).then_inc(high_done, 1)

                def attend(f, b):
                    n = 2 * f + b
                    if bounded:
                        for u in range(UNITS):
                            kt = u % KT
                            tile = b * KT + kt
                            act.wait_ge(clipped, UNITS * n + u + 1 + S_SLOTS)
                            act.wait_ge(pv_done, UNITS * n + u + 1)
                            nc.scalar.activation(pT4[:, u % 4, :], probs[:, 0, (u % 2) * HALF:(u % 2 + 1) * HALF], ACT.Exp,
                                                 bias=keep_mask[:, 1, tile:tile + 1],
                                                 scale=keep_mask[:, 0, tile:tile + 1]).then_inc(exp_done, 1)
                        return
                    for u in range(UNITS + 1):
                        if u < UNITS:
                            act.wait_ge(bias_done, UNITS * n + u + 1)
                            act.wait_ge(turned[1], UNITS * n + u + 1)
                            nc.scalar.activation(probs[:, u % 2, :], s_ps[:, u % 2, :], ACT.Exp,
                                                 bias=small[:, u % 2, 1:2], scale=SCALE).then_inc(exp_done, 1)
                        if u >= 1:
                            v = u - 1
                            act.wait_ge(turned[1], UNITS * n + v + 1 + 2)
                            act.wait_ge(pv_done, UNITS * n + v + 1)
                            nc.scalar.copy(probsT[:, v % 2, HALF:2 * HALF], t_ps[:, 1, :]).then_inc(copied[1], 1)

                act.sem_inc(exp_done, 2)
                if not bounded:
                    act.sem_inc(copied[1], 1)
                    act.sem_inc(turned[1], 2)
                highs(0, 0)
                with act.Fori(0, FG - 1) as f:
                    highs(f, 1)
                    attend(f, 0)
                    highs(f + 1, 0)
                    attend(f, 1)
                highs(FG - 1, 1)
                attend(FG - 1, 0)
                attend(FG - 1, 1)

            @block.vector
            def _(dve):
                nc.vector.memset(values[:, :, :, HD:VC], 1.0).then_inc(ones_made, 1)
                dve.wait_ge(ones_made, 1)
                dve.wait_ge(wv_loaded, 32)
                for t in range(CT):
                    dve.wait_ge(v_psum, t + 1)
                    nc.vector.tensor_tensor(values[:, t, :, 0:HD],
                                            s_ps[:, t % S_SLOTS, 0:D].rearrange("p (h e) -> p h e", e=HD),
                                            bv.rearrange("p (h e) -> p h e", e=HD), ALU.add).then_inc(v_done, 1)
                dve.wait_ge(v_done, CT)

                def lows(f, b):
                    n = 2 * f + b
                    for i in range(PRODUCTS):
                        key = i < PRODUCTS - 1
                        high = kh[:, i * HALF:(i + 1) * HALF] if key else qh[:]
                        low = kl[:, i * HALF:(i + 1) * HALF] if key else ql[:]
                        if (i == 0 or not key) and (not isinstance(n, int) or n):
                            dve.wait_ge(k_stacked if key else q_stacked, STACKS * n)
                        dve.wait_ge(high_done, PRODUCTS * n + i + 1)
                        nc.vector.scalar_tensor_tensor(low, t_ps[:, (PRODUCTS * b + i) % P_SLOTS, :], (bk if key else bq)[:],
                                                       high.bitcast(F32), ALU.add, ALU.subtract).then_inc(low_done, 1)

                def normalise(f, b, q):
                    k = (2 * f + b) * QT + q
                    o = o_ps[:, q % O_SLOTS, 0:HG * VC].rearrange("p (h e) -> p h e", e=VC)
                    nc.vector.reciprocal(inv[:, q % 2], o[:, :, HD:VC]).then_inc(inv_done, 1)
                    dve.wait_ge(inv_done, k + 1)
                    nc.vector.tensor_tensor(heads_out[:, b * QT + q, bass.ds(P * f, P)].rearrange("p (h e) -> p h e", e=HD),
                                            o[:, :, 0:HD], inv[:, q % 2].to_broadcast([P, HG, HD]), ALU.mult).then_inc(
                                                norm_done, 1)

                def attend(f, b):
                    n = 2 * f + b
                    if bounded:
                        for u in range(UNITS):
                            dve.wait_ge(scores_done, UNITS * n + u + 1)
                            dve.wait_ge(exp_done, UNITS * n + u + 1)
                            nc.vector.tensor_scalar(probs[:, 0, (u % 2) * HALF:(u % 2 + 1) * HALF], s_ps[:, u % S_SLOTS, :],
                                                    BOUND / SCALE, -BOUND / SCALE, ALU.min, ALU.max).then_inc(clipped, 1)
                        dve.wait_ge(pv_done, UNITS * (n + 1) + 4)
                        for q in range(QT):
                            normalise(f, b, q)
                        return
                    for u in range(UNITS + 3):
                        if u < UNITS:
                            dve.wait_ge(scores_done, UNITS * n + u + 1)
                            nc.vector.tensor_reduce(small[:, u % 2, 0:1], s_ps[:, u % 2, :], AX_X, ALU.max).then_inc(max_done, 1)
                            dve.wait_ge(max_done, UNITS * n + u + 1)
                            nc.vector.tensor_scalar(small[:, u % 2, 1:2], small[:, u % 2, 0:1], -SCALE, None,
                                                    ALU.mult).then_inc(bias_done, 1)
                        if 1 <= u <= UNITS:
                            v = u - 1
                            dve.wait_ge(turned[0], UNITS * n + v + 1)
                            dve.wait_ge(pv_done, UNITS * n + v + 1)
                            nc.vector.tensor_copy(probsT[:, v % 2, 0:HALF], t_ps[:, 0, :]).then_inc(copied[0], 1)
                        if u >= 6 and u % HG == 2:
                            q = (u - 6) // HG
                            dve.wait_ge(pv_done, UNITS * n + HG * (q + 1) + 2)
                            normalise(f, b, q)

                dve.sem_inc(low_done, P_SLOTS)
                dve.sem_inc(norm_done, QT if bounded else 2)
                dve.sem_inc(pv_done, 4 if bounded else 2)
                if bounded:
                    dve.sem_inc(clipped, S_SLOTS)
                else:
                    dve.sem_inc(copied[0], 1)
                lows(0, 0)
                with dve.Fori(0, FG - 1) as f:
                    lows(f, 1)
                    attend(f, 0)
                    lows(f + 1, 0)
                    attend(f, 1)
                lows(FG - 1, 1)
                attend(FG - 1, 0)
                attend(FG - 1, 1)
                dve.wait_ge(norm_done, QT * 2 * FG + (QT if bounded else 2))


def linear_attention_block(env, name, heads_out):
    nc, io = env.nc, env.io
    env.prefix = f"{name}_attn"
    HEADS, HD, FD = 16, 32, 64
    FG, HG = 4, 4
    VC = HD + 1
    KT, QT = CTX // P, SEQ // P
    CT = BATCH * KT
    PAIR = 2 * VC
    K_PARTS, Q_PARTS = BATCH * CTX // HALF, TOK // HALF
    MAPPED = BATCH * 2
    PRODUCTS = K_PARTS + Q_PARTS + MAPPED
    EPS = 1e-8
    ctx_loaded, wv_loaded, w_loaded, maps_loaded = (env.sem("ctx_loaded"), env.sem("wv_loaded"), env.sem("w_loaded"),
                                                    env.sem("maps_loaded"))
    cleared, v_psum, v_done = env.sem("cleared"), env.sem("v_psum"), env.sem("v_done")
    proj_psum, proj_done = env.sem("proj_psum"), env.sem("proj_done")
    kf_psum, kf_done = env.sem("kf_psum"), env.sem("kf_done")
    kv_step, kv_copied = env.sem("kv_step"), env.sem("kv_copied")
    o_done, norm_done, inv_step = env.sem("o_done"), env.sem("norm_done"), env.sem("inv_step")
    with ExitStack() as local:
        def sb(n, shape, dt=F32):
            return local.enter_context(nc.sbuf_tensor(f"{name}_{n}", shape, dt))

        def psum(n):
            return local.enter_context(nc.psum_tensor(f"{name}_{n}", [P, 2, HALF], F32))

        ctxT, values = sb("ctxT", [P, DC, BATCH * CTX]), sb("values", [P, CT, HEADS, VC])
        wv, bv, wk, wq = sb("wv", [P, DC, D]), sb("bv", [P, D]), sb("wk", [P, DC * P]), sb("wq", [P, DC * P])
        bk, bq, mask = sb("bk", [P, 1]), sb("bq", [P, 1]), sb("mask", [P, CT])
        wqf, wkf = sb("wqf", [P, HG * FD]), sb("wkf", [P, HG * FD])
        kT, qT = sb("kT", [P, BATCH * CTX]), sb("qT", [P, TOK])
        kf, qf = sb("kf", [P, 2, HG * FD]), sb("qf", [P, MAPPED, SEQ])
        kv = sb("kv", [P, BATCH, 2, PAIR])
        inv = sb("inv", [P, 2, HG, 1])
        proj_ps, kf_ps, kv_ps, o_ps = psum("proj_ps"), psum("kf_ps"), psum("kv_ps"), psum("o_ps")

        with nc.Block() as block:
            @block.sync
            def _(sp):
                sp.dma_start(wv[:], io["wv"]).then_inc(wv_loaded, 16)
                sp.dma_start(bv[:], io["bv"].partition_broadcast(P)).then_inc(wv_loaded, 16)
                for b in range(BATCH):
                    sp.dma_start(ctxT[:, :, b * CTX:(b + 1) * CTX], io["ctxT"][:, :, b * CTX:(b + 1) * CTX]).then_inc(
                        ctx_loaded, 16)
                    sp.wait_ge(ctx_loaded, 16 * (b + 1))

                def load_weights(f):
                    for to, of in ((wk, "wk"), (wq, "wq"), (bk, "bk"), (bq, "bq")):
                        sp.dma_start(to[:], io[of][bass.ds(f, 1)].rearrange("g p n -> p (g n)")).then_inc(w_loaded, 16)

                load_weights(0)
                sp.dma_start(mask[:], io["mask_f"]).then_inc(maps_loaded, 16)
                sp.wait_ge(cleared, 4)
                for h in range(HG):
                    for to, of in ((wqf, "wqf"), (wkf, "wkf")):
                        sp.dma_start(to[HD * h:HD * (h + 1), FD * h:FD * (h + 1)], io[of]).then_inc(maps_loaded, 16)
                with sp.Fori(1, FG) as f:
                    sp.wait_ge(proj_done, 2 + PRODUCTS * (f - 1) + K_PARTS + Q_PARTS)
                    load_weights(f)

            @block.tensor
            def _(pe):
                pe.wait_ge(wv_loaded, 32)
                for t in range(CT):
                    pe.wait_ge(ctx_loaded, 16 * (t // KT + 1))
                    if t >= 2:
                        pe.wait_ge(v_done, t - 1)
                    for i in range(DC):
                        last = nc.tensor.matmul(kf_ps[:, t % 2, :], ctxT[:, i, t * P:(t + 1) * P], wv[:, i, :],
                                                start=(i == 0), stop=(i == DC - 1))
                    last.then_inc(v_psum, 1)
                pe.wait_ge(v_done, CT)
                pe.wait_ge(maps_loaded, 16 * (2 * HG + 1))
                with pe.Fori(0, FG) as f:
                    def slot(i):
                        pe.wait_ge(proj_done, PRODUCTS * f + i + 1)
                        return proj_ps[:, i % 2, :]

                    pe.wait_ge(w_loaded, 64 * (f + 1))
                    for i in range(K_PARTS + Q_PARTS):
                        w, moving, n = (wk, ctxT, i) if i < K_PARTS else (wq, env.xT, i - K_PARTS)
                        to = slot(i)
                        for c in range(DC):
                            last = nc.tensor.matmul(to, w[:, c * P:(c + 1) * P], moving[:, c, n * HALF:(n + 1) * HALF],
                                                    start=(c == 0), stop=(c == DC - 1))
                        last.then_inc(proj_psum, 1)

                    def accumulate(t):
                        b = t // KT
                        pe.wait_ge(kf_done, CT * f + t + 1 + 2)
                        if t % KT == 0:
                            pe.wait_ge(kv_copied, 4 * BATCH * f + 4 * b + 4)
                        for j in range(2):
                            rhs = values[:, t, bass.ds(HG * f + 2 * j, 2), :].rearrange("p h e -> p (h e)")
                            last = nc.tensor.matmul(kv_ps[:, j, 0:PAIR], kf[:, t % 2, j * P:(j + 1) * P], rhs,
                                                    start=(t % KT == 0), stop=(t % KT == KT - 1))
                        last.then_inc(kv_step, 1)

                    pe.wait_ge(proj_done, 2 + PRODUCTS * f + K_PARTS)
                    for t in range(CT):
                        pe.wait_ge(kf_done, CT * f + t + 1)
                        nc.tensor.matmul(kf_ps[:, t % 2, 0:HG * FD], kT[:, t * P:(t + 1) * P], wkf[:],
                                         start=True, stop=True).then_inc(kf_psum, 1)
                        if t >= 1:
                            accumulate(t - 1)
                    accumulate(CT - 1)
                    pe.wait_ge(proj_done, 2 + PRODUCTS * f + K_PARTS + Q_PARTS)
                    for m in range(MAPPED):
                        b, j = m // 2, m % 2
                        nc.tensor.matmul(slot(K_PARTS + Q_PARTS + m), wqf[:, j * P:(j + 1) * P],
                                         qT[:, b * SEQ:(b + 1) * SEQ], start=True, stop=True).then_inc(proj_psum, 1)
                    pe.wait_ge(proj_done, 2 + PRODUCTS * (f + 1))
                    pe.wait_ge(kv_copied, 4 * BATCH * (f + 1) + 4)
                    for q in range(TILES):
                        pe.wait_ge(norm_done, TILES * f + q + 1)
                        b, at = q // QT, (q % QT) * P
                        for j in range(2):
                            last = nc.tensor.matmul(o_ps[:, q % 2, j * PAIR:(j + 1) * PAIR], qf[:, 2 * b + j, at:at + P],
                                                    kv[:, b, j, :], start=True, stop=True)
                        last.then_inc(o_done, 1)

            @block.scalar
            def _(act):
                act.sem_inc(proj_done, 2)
                with act.Fori(0, FG) as f:
                    act.wait_ge(kv_step, CT * f + 2)
                    act.wait_ge(norm_done, TILES * f + 2)
                    for i in range(PRODUCTS):
                        act.wait_ge(proj_psum, PRODUCTS * f + i + 1)
                        ps = proj_ps[:, i % 2, :]
                        if i < K_PARTS:
                            ins = nc.scalar.activation(kT[:, i * HALF:(i + 1) * HALF], ps, ACT.Identity, bias=bk[:])
                        elif i < K_PARTS + Q_PARTS:
                            n = i - K_PARTS
                            ins = nc.scalar.activation(qT[:, n * HALF:(n + 1) * HALF], ps, ACT.Identity, bias=bq[:])
                        else:
                            ins = nc.scalar.activation(qf[:, i - K_PARTS - Q_PARTS, :], ps, ACT.Relu)
                        ins.then_inc(proj_done, 1)

            @block.vector
            def _(dve):
                nc.vector.memset(wqf[:], 0.0).then_inc(cleared, 1)
                nc.vector.memset(wkf[:], 0.0).then_inc(cleared, 1)
                nc.vector.memset(kv[:], 0.0).then_inc(cleared, 1)
                nc.vector.memset(values[:, :, :, HD:VC], 1.0).then_inc(cleared, 1)
                dve.wait_ge(cleared, 4)
                dve.wait_ge(wv_loaded, 32)
                for t in range(CT):
                    dve.wait_ge(v_psum, t + 1)
                    nc.vector.tensor_tensor(values[:, t, :, 0:HD], kf_ps[:, t % 2, :].rearrange("p (h e) -> p h e", e=HD),
                                            bv[:].rearrange("p (h e) -> p h e", e=HD), ALU.add).then_inc(v_done, 1)
                dve.wait_ge(maps_loaded, 16 * (2 * HG + 1))
                dve.sem_inc(kf_done, 2)
                dve.sem_inc(kv_step, 2)
                dve.sem_inc(kv_copied, 4)
                dve.sem_inc(norm_done, 2)
                with dve.Fori(0, FG) as f:
                    for t in range(CT):
                        dve.wait_ge(kf_psum, CT * f + t + 1)
                        dve.wait_ge(kv_step, CT * f + t + 1)
                        nc.vector.tensor_scalar(kf[:, t % 2, :], kf_ps[:, t % 2, 0:HG * FD], 0.0, mask[:, t:t + 1],
                                                ALU.max, ALU.mult).then_inc(kf_done, 1)
                        if t % KT == KT - 1:
                            b = t // KT
                            dve.wait_ge(kv_step, CT * f + t + 1 + 2)
                            for j in range(2):
                                for half in range(2):
                                    rows, cols = slice(64 * half, 64 * half + 64), slice(VC * half, VC * (half + 1))
                                    nc.vector.tensor_copy(kv[rows, b, j, cols], kv_ps[rows, j, cols]).then_inc(kv_copied, 1)
                    for q in range(TILES):
                        o = o_ps[:, q % 2, 0:HG * VC].rearrange("p (h e) -> p h e", e=VC)
                        k = TILES * f + q
                        dve.wait_ge(o_done, k + 1)
                        nc.vector.tensor_scalar(inv[:, q % 2], o[:, :, HD:VC], EPS, None, ALU.add).then_inc(inv_step, 1)
                        dve.wait_ge(inv_step, 2 * k + 1)
                        nc.vector.reciprocal(inv[:, q % 2], inv[:, q % 2]).then_inc(inv_step, 1)
                        dve.wait_ge(inv_step, 2 * k + 2)
                        nc.vector.tensor_tensor(heads_out[:, q, bass.ds(P * f, P)].rearrange("p (h e) -> p h e", e=HD),
                                                o[:, :, 0:HD], inv[:, q % 2].to_broadcast([P, HG, HD]), ALU.mult).then_inc(
                                                    norm_done, 1)
                dve.wait_ge(norm_done, TILES * FG + 2)


def key_mask_block(env, name, keep_mask):
    nc, io = env.nc, env.io
    env.prefix = f"{name}_mask"
    loaded, step = env.sem("loaded"), env.sem("step")
    n = BATCH * CTX // P
    with ExitStack() as local:
        raw = local.enter_context(nc.sbuf_tensor(f"{name}_mask_raw", [P, n], I32))
        keep = local.enter_context(nc.sbuf_tensor(f"{name}_keep", [P, n], F32))
        with nc.Block() as block:
            @block.sync
            def _(sp):
                sp.dma_start(raw[:], io["mask"]).then_inc(loaded, 16)

            @block.vector
            def _(dve):
                dve.wait_ge(loaded, 16)
                nc.vector.tensor_scalar(keep[:], raw[:], 0.5, None, ALU.is_gt).then_inc(step, 1)
                dve.wait_ge(step, 1)
                nc.vector.tensor_scalar(keep_mask[:, 0, :], keep[:], 32 ** -0.5, None, ALU.mult).then_inc(step, 1)
                nc.vector.tensor_scalar(keep_mask[:, 1, :], keep[:], -1.0, 50.0, ALU.add, ALU.mult).then_inc(step, 1)
                dve.wait_ge(step, 3)


def quantise_rows(nc, link, src, dst, top, tmp):
    MAGIC = 1.5 * 2 ** 23
    s, inv = top[:, 0:1], top[:, 1:2]
    link(nc.vector.tensor_reduce(s, src, AX_X, ALU.max, apply_absolute_value=True))
    link(nc.vector.tensor_scalar(s, s, 1.0 / 127.0, 1e-8, ALU.mult, ALU.max))
    link(nc.vector.reciprocal(inv, s))
    link(nc.vector.tensor_scalar(tmp, src, inv, MAGIC, ALU.mult, ALU.add))
    link(nc.vector.tensor_scalar(tmp, tmp, MAGIC + 127.0, MAGIC - 127.0, ALU.min, ALU.max))
    link(nc.vector.tensor_scalar(dst, tmp, -MAGIC, s, ALU.add, ALU.mult))


def quantise_weights_block(env, name, wq_scratch, wp_scratch):
    nc, io = env.nc, env.io
    env.prefix = f"{name}_quant"
    FG = D // P
    loaded, ready, turned, copied, stored = (env.sem("loaded"), env.sem("ready"), env.sem("turned"), env.sem("copied"),
                                             env.sem("stored"))
    with ExitStack() as local:
        w = local.enter_context(nc.sbuf_tensor(f"{name}_w", [P, 2 * FG, D], F32))
        wT = local.enter_context(nc.sbuf_tensor(f"{name}_wT", [P, 2 * FG, DC, P], F32))
        tmp = local.enter_context(nc.sbuf_tensor(f"{name}_tmp", [P, D], F32))
        top = local.enter_context(nc.sbuf_tensor(f"{name}_top", [P, 2], F32))
        ps = local.enter_context(nc.psum_tensor(f"{name}_quant_ps", [P, 2, DC, P], F32))
        with nc.Block() as block:
            @block.sync
            def _(sp):
                sp.dma_start(w[:, 0:FG, :], io["wq_rows"].rearrange("(f p) n -> p f n", p=P)).then_inc(loaded, 16)
                sp.dma_start(w[:, FG:2 * FG, :], io["wp_rows"].rearrange("(f p) n -> p f n", p=P)).then_inc(loaded, 16)
                for g in range(FG):
                    sp.wait_ge(copied, g + 1)
                    sp.dma_start(wq_scratch[g], wT[:, g].rearrange("p c n -> p (c n)")).then_inc(stored, 16)
                sp.wait_ge(copied, 2 * FG)
                for g in range(FG):
                    sp.dma_start(wp_scratch[:, :, g * P:(g + 1) * P], wT[:, FG + g]).then_inc(stored, 16)
                sp.wait_ge(stored, 16 * 2 * FG)

            @block.vector
            def _(dve):
                links, count = env.sem("links"), [0]

                def link(ins):
                    count[0] += 1
                    ins.then_inc(links, 1)
                    dve.wait_ge(links, count[0])

                dve.wait_ge(loaded, 32)
                for g in range(2 * FG):
                    quantise_rows(nc, link, w[:, g, :], w[:, g, :], top, tmp[:])
                    dve.sem_inc(ready, 1)

            @block.tensor
            def _(pe):
                for g in range(2 * FG):
                    pe.wait_ge(ready, g + 1)
                    if g >= 2:
                        pe.wait_ge(copied, g - 1)
                    for c in range(DC):
                        last = nc.tensor.transpose(ps[:, g % 2, c, :], w[:, g, c * P:(c + 1) * P], env.ident[:])
                    last.then_inc(turned, 1)

            @block.scalar
            def _(act):
                for g in range(2 * FG):
                    act.wait_ge(turned, g + 1)
                    nc.scalar.copy(wT[:, g], ps[:, g % 2]).then_inc(copied, 1)


def output_block(env, name, heads_out, gate, wo_dram, quantised=False, after_norm=False):
    nc, io = env.nc, env.io
    env.prefix = f"{name}_out"
    loaded, ready, turned, copied = env.sem("loaded"), env.sem("ready"), env.sem("turned"), env.sem("copied")
    y_done, y_used, var_done, sd_done = env.sem("y_done"), env.sem("y_used"), env.sem("var_done"), env.sem("sd_done")
    LOADS = 16 * (5 if after_norm else 2)
    with ExitStack() as local:
        def sb(n, shape, dt=F32):
            return local.enter_context(nc.sbuf_tensor(f"{name}_{n}", shape, dt))

        wo, bo, aT = sb("wo", [P, DC, D]), sb("bo", [P, D]), sb("aT", [P, 2, DC, P])
        top, tmp, delta = sb("out_top", [P, 2]), sb("out_tmp", [P, D]), sb("delta", [P, 2, D])
        if after_norm:
            gamma, beta, rs = sb("gamma", [P, D]), sb("beta", [P, D]), sb("rs", [P, 1])
            stats, meanvar, sd = sb("out_stats", [P, 2, 6]), sb("out_meanvar", [P, 2, 2]), sb("out_sd", [P, 2, 2])
        t_ps = local.enter_context(nc.psum_tensor(f"{name}_turn_ps", [P, 2, DC, P], F32))
        y_ps = local.enter_context(nc.psum_tensor(f"{name}_out_ps", [P, 2, D], F32))
        with nc.Block() as block:
            @block.sync
            def _(sp):
                sp.dma_start(wo[:], wo_dram).then_inc(loaded, 16)
                sp.dma_start(bo[:], io["bo"].partition_broadcast(P)).then_inc(loaded, 16)
                if after_norm:
                    sp.dma_start(gamma[:], io["gamma"].partition_broadcast(P)).then_inc(loaded, 16)
                    sp.dma_start(beta[:], io["beta"].partition_broadcast(P)).then_inc(loaded, 16)
                    sp.dma_start(rs[:], io["rs"].partition_broadcast(P)).then_inc(loaded, 16)

            @block.tensor
            def _(pe):
                pe.wait_ge(loaded, LOADS)

                def product(t):
                    pe.wait_ge(copied, t + 1)
                    if t >= 2:
                        pe.wait_ge(y_used, t - 1)
                    for c in range(DC):
                        last = nc.tensor.matmul(y_ps[:, t % 2, :], aT[:, t % 2, c, :], wo[:, c, :],
                                                start=(c == 0), stop=(c == DC - 1))
                    last.then_inc(y_done, 1)

                for t in range(TILES):
                    if quantised:
                        pe.wait_ge(ready, t + 1)
                    if t >= 2:
                        pe.wait_ge(copied, t - 1)
                    for c in range(DC):
                        last = nc.tensor.transpose(t_ps[:, t % 2, c, :], heads_out[:, t, c * P:(c + 1) * P], env.ident[:])
                    last.then_inc(turned, 1)
                    if t >= 1:
                        product(t - 1)
                product(TILES - 1)

            @block.scalar
            def _(act):
                def root(act, t):
                    act.wait_ge(var_done, t + 1)
                    nc.scalar.activation(sd[:, t % 2, 0:1], meanvar[:, t % 2, 1:2], ACT.Sqrt,
                                         bias=env.eps_ln[:]).then_inc(sd_done, 1)

                for t in range(TILES):
                    act.wait_ge(turned, t + 1)
                    if t >= 2:
                        act.wait_ge(y_done, t - 1)
                    nc.scalar.copy(aT[:, t % 2], t_ps[:, t % 2]).then_inc(copied, 1)
                    if after_norm and t >= 2:
                        root(act, t - 2)
                if after_norm:
                    root(act, TILES - 2)
                    root(act, TILES - 1)

            @block.vector
            def _(dve):
                links, count = env.sem("links"), [0]

                def link(ins):
                    count[0] += 1
                    ins.then_inc(links, 1)
                    dve.wait_ge(links, count[0])

                if quantised:
                    for t in range(TILES):
                        quantise_rows(nc, link, heads_out[:, t, :], heads_out[:, t, :], top, tmp[:])
                        dve.sem_inc(ready, 1)
                dve.wait_ge(loaded, LOADS)
                if after_norm:
                    link(nc.vector.tensor_scalar(rs[:], rs[:], 0.0, 0.3, ALU.max, ALU.min))
                    link(nc.vector.tensor_scalar(gamma[:], gamma[:], gate, None, ALU.mult))
                    link(nc.vector.tensor_scalar(beta[:], beta[:], gate, None, ALU.mult))
                for t in range(TILES):
                    d = delta[:, t % 2, :]
                    dve.wait_ge(y_done, t + 1)
                    nc.vector.tensor_tensor(d, y_ps[:, t % 2, :], bo[:], ALU.add).then_inc(y_used, 1)
                    dve.wait_ge(y_used, t + 1)
                    if after_norm:
                        link(nc.vector.tensor_scalar(d, d, rs[:], None, ALU.mult))
                        link(nc.vector.bn_stats(stats[:, t % 2, :], d))
                        nc.vector.bn_aggr(meanvar[:, t % 2, :], stats[:, t % 2, :]).then_inc(var_done, 1)
                        dve.wait_ge(sd_done, t + 1)
                        link(nc.vector.reciprocal(sd[:, t % 2, 1:2], sd[:, t % 2, 0:1]))
                        link(nc.vector.tensor_scalar(d, d, meanvar[:, t % 2, 0:1], sd[:, t % 2, 1:2], ALU.subtract, ALU.mult))
                        link(nc.vector.tensor_tensor(d, d, gamma[:], ALU.mult))
                        link(nc.vector.tensor_tensor(d, d, beta[:], ALU.add))
                        link(nc.vector.tensor_tensor(env.x[:, t, :], env.x[:, t, :], d, ALU.add))
                    else:
                        link(nc.vector.scalar_tensor_tensor(env.x[:, t, :], d, gate, env.x[:, t, :], ALU.mult, ALU.add))


def build(nc, io, out, stages):
    with ExitStack() as stack:
        env = Env(nc, stack, io)
        env.x = stack.enter_context(nc.sbuf_tensor("x", [P, TILES, D], F32))
        env.ident = stack.enter_context(nc.sbuf_tensor("ident", [P, P], F32))
        env.gates = stack.enter_context(nc.sbuf_tensor("gates", [P, 8], F32))
        env.tanh_gates = stack.enter_context(nc.sbuf_tensor("tanh_gates", [P, 8], F32))
        env.iota8 = stack.enter_context(nc.sbuf_tensor("iota8", [P, 8], F32))
        env.eps_ln = stack.enter_context(nc.sbuf_tensor("eps_ln", [P, 1], F32))
        setup_block(env)

        @contextmanager
        def sublayer():
            with nc.cleanup_on_exit(), ExitStack() as local:
                yield local

        def layer(prefix, *names):
            env.io = {n: io[f"{prefix}_{n}"] for n in names}

        def attention_layer(name, gate, **kinds):
            with sublayer() as local:
                sb = lambda n, s, d=F32: local.enter_context(nc.sbuf_tensor(n, s, d))
                layer(name, *[n[len(name) + 1:] for n in io if n.startswith(name)])
                env.io["ctxT"] = io["ctxT"]
                env.xT = sb(f"{name}_xT", [P, DC, TOK])
                heads_out = sb(f"{name}_heads", [P, TILES, D])
                keep_mask = None
                quantised = kinds.get("quantised", False)
                if quantised:
                    wq_scratch = nc.dram_tensor("wq_scratch", (D // P, P, D), F32, kind="Internal").ap()
                    env.io["wq"] = wq_scratch
                    env.io["wo"] = nc.dram_tensor("wp_scratch", (P, DC, D), F32, kind="Internal").ap()
                    quantise_weights_block(env, name, wq_scratch, env.io["wo"])
                if kinds.get("masked"):
                    keep_mask = sb("keep_mask", [P, 2, BATCH * CTX // P])
                    env.io["mask"] = io["mask"]
                    key_mask_block(env, name, keep_mask)
                norm_block(env, name, quantised=quantised)
                if kinds.get("linear"):
                    env.io["mask_f"] = io["mask_f"]
                    linear_attention_block(env, name, heads_out)
                else:
                    softmax_attention_block(env, name, heads_out, keep_mask)
                output_block(env, name, heads_out, gate, env.io["wo"], quantised, kinds.get("after_norm", False))

        if "L0_attn" in stages:
            attention_layer("L0_attn", env.tanh_gates[:, 0:1], linear=True)
        def x_halves(name, local):
            return [local.enter_context(nc.sbuf_tensor(f"{name}_x_{n}", [P, DC, TOK], F32R)) for n in ("high", "low")]

        @contextmanager
        def x_hat(name, x_parts):
            with nc.sbuf_tensor(f"{name}_xT", [P, DC, TOK], F32) as env.xT:
                norm_block(env, name, split=x_parts)
                yield

        if "L0_ffn" in stages:
            layer("L0_ffn", "w1", "w2", "w3")
            with sublayer() as local:
                sb = lambda n, s, d=F32: local.enter_context(nc.sbuf_tensor(n, s, d))
                scale, half, neg_half = sb("scale", [P, 3]), sb("half", [P, 3]), sb("neg_half", [P, 3])
                weight = sb("weight", [P, 1])
                ternary_scales(env, "L0_ffn", scale, half, neg_half, env.tanh_gates[:, 4:5], weight)
                x_parts = x_halves("L0_ffn", local)
                with x_hat("L0_ffn", x_parts):
                    pass
                ffn_block(env, "L0_ffn", [P, P], weight, x_parts, ternary=(scale, half, neg_half))
        if "L1_attn" in stages:
            attention_layer("L1_attn", env.tanh_gates[:, 1:2], masked=True, after_norm=True)
        if "L1_ffn" in stages:
            with sublayer() as local:
                sb = lambda n, s, d=F32: local.enter_context(nc.sbuf_tensor(n, s, d))
                layer("L1_ffn", "w1", "w3", "wq", "keys")
                G = io["L1_ffn_w1"].shape[0]
                sims, bar = sb("sims", [P, TILES, PEER_HEADS, KEY_ROWS + NK]), sb("bar", [P, TILES * PEER_HEADS])
                extra = sb("extra", [P, G, TILES])
                x_parts = x_halves("L1_ffn", local)
                with x_hat("L1_ffn", x_parts):
                    product_keys_block(env, "L1_ffn", sims, bar, extra, G)
                ffn_block(env, "L1_ffn", [P] * 4, env.tanh_gates[:, 5:6], x_parts, peer=(sims, bar, extra))
        if "L2_attn" in stages:
            attention_layer("L2_attn", env.tanh_gates[:, 2:3], quantised=True)
        if "L2_ffn" in stages:
            with sublayer() as local:
                layer("L2_ffn", "w1", "w2", "w3", "router")
                weight = local.enter_context(nc.sbuf_tensor("L2_weight", [P, TILES, 8], F32))
                x_parts = x_halves("L2_ffn", local)
                with x_hat("L2_ffn", x_parts):
                    expert_weights_block(env, "L2_ffn", 8, 0, True, env.tanh_gates[:, 6:7], weight)
                ffn_block(env, "L2_ffn", [P, P], weight, x_parts)
        if "L3_attn" in stages:
            attention_layer("L3_attn", env.tanh_gates[:, 3:4])
        if "L3_ffn" in stages:
            with sublayer() as local:
                layer("L3_ffn", "w1", "w2", "w3", "router")
                weight = local.enter_context(nc.sbuf_tensor("L3_weight", [P, TILES, 12], F32))
                x_parts = x_halves("L3_ffn", local)
                with x_hat("L3_ffn", x_parts):
                    expert_weights_block(env, "L3_ffn", 12, 4, False, env.tanh_gates[:, 7:8], weight)
                ffn_block(env, "L3_ffn", [P, P, 96], weight, x_parts)
        store_block(env, out)


def lay_out(inputs):
    import numpy as np

    def up(w, group):
        g = w.shape[0] // group
        return w.reshape(g, group, DC, P).transpose(0, 3, 2, 1).reshape(g, P, DC * group)

    def rows(w):
        return w.reshape(DC, P, w.shape[1]).transpose(1, 0, 2)

    i = {k: np.asarray(v) for k, v in inputs.items()}
    a = {k: i[k] for k in ("x", "g_xattn", "g_ffn")}
    a["L0_ffn_w1"], a["L0_ffn_w2"] = up(i["L0_ffn_W_up"], 256), up(i["L0_ffn_W_gate"], 256)
    a["L0_ffn_w3"] = i["L0_ffn_W_down"].T.reshape(8, 256, D)
    a["L1_ffn_w1"], a["L1_ffn_w3"] = up(i["L1_ffn_e_down"], 512), i["L1_ffn_e_up"].reshape(8, 512, D)
    a["L1_ffn_wq"] = rows(i["L1_ffn_Wq"])
    a["L1_ffn_keys"] = i["L1_ffn_keys"].transpose(3, 2, 0, 1)
    a["L2_ffn_w1"] = up(i["L2_ffn_wi_0"].transpose(0, 2, 1).reshape(-1, D), 256)
    a["L2_ffn_w2"] = up(i["L2_ffn_wi_1"].transpose(0, 2, 1).reshape(-1, D), 256)
    a["L2_ffn_w3"], a["L2_ffn_router"] = i["L2_ffn_wo"], rows(i["L2_ffn_w_gate"])
    s, w13 = i["L3_ffn_shared_gate_up_w"], i["L3_ffn_w13"]
    inter = w13.shape[1] // 2
    a["L3_ffn_w1"] = up(np.concatenate([s[:s.shape[0] // 2], w13[:, :inter].reshape(-1, D)]), inter)
    a["L3_ffn_w2"] = up(np.concatenate([s[s.shape[0] // 2:], w13[:, inter:].reshape(-1, D)]), inter)
    a["L3_ffn_w3"] = np.concatenate([i["L3_ffn_shared_down_w"].T.reshape(-1, inter, D),
                                     i["L3_ffn_w2"].transpose(0, 2, 1)])
    a["L3_ffn_router"] = rows(np.concatenate([i["L3_ffn_gate_w"], i["L3_ffn_shared_gate_w"]]).T)
    a["ctxT"] = rows(i["ctx_2048"].reshape(-1, D).T)
    a["mask"] = i["mask_BxS2_ik0"].reshape(-1, P).T

    def column(b):
        return b.reshape(DC, P, 1)

    for n in (0, 1, 3):
        for m in ("q", "k"):
            a[f"L{n}_attn_w{m}"] = up(i[f"L{n}_xattn_W{m}"], P)
            a[f"L{n}_attn_b{m}"] = column(i[f"L{n}_xattn_b{m}"])
        for m in ("v", "o"):
            a[f"L{n}_attn_w{m}"], a[f"L{n}_attn_b{m}"] = rows(i[f"L{n}_xattn_W{m}"].T), i[f"L{n}_xattn_b{m}"]
    a["L0_attn_wqf"], a["L0_attn_wkf"] = i["L0_xattn_Wqf"].T, i["L0_xattn_Wkf"].T
    a["mask_f"] = i["mask_BxS2_ff1"].reshape(-1, P).T
    a["L1_attn_gamma"], a["L1_attn_beta"] = i["L1_xattn_ln_gamma"], i["L1_xattn_ln_beta"]
    a["L1_attn_rs"] = i["L1_xattn_residual_scale"].reshape(1)
    a["L2_attn_wq_rows"], a["L2_attn_wp_rows"] = i["L2_xattn_wq"], i["L2_xattn_wp"]
    a["L2_attn_wk"], a["L2_attn_wv"] = up(i["L2_xattn_wkv"][:D], P), rows(i["L2_xattn_wkv"][D:].T)
    a["L2_attn_bq"], a["L2_attn_bk"] = column(i["L2_xattn_bq"]), column(i["L2_xattn_bkv"][:D])
    a["L2_attn_bv"], a["L2_attn_bo"] = i["L2_xattn_bkv"][D:], i["L2_xattn_bp"]
    return {k: np.ascontiguousarray(v) for k, v in a.items()}


STAGES = ("L0_attn", "L0_ffn", "L1_attn", "L1_ffn", "L2_attn", "L2_ffn", "L3_attn", "L3_ffn")


def kernel(**inputs):
    import concourse.bacc as bacc
    from concourse.bass_utils import run_bass_kernel_spmd

    nc = bacc.Bacc("TRN2", target_bir_lowering=False, num_devices=1)
    arrays, io = {}, {}
    for name, a in lay_out(inputs).items():
        arrays[f"in_{name}"] = a
        io[name] = nc.dram_tensor(f"in_{name}", a.shape, mybir.dt.from_np(a.dtype), kind="ExternalInput").ap()
    out = nc.dram_tensor("out_x", (BATCH, SEQ, D), F32, kind="ExternalOutput").ap()
    build(nc, io, out, STAGES)
    r = run_bass_kernel_spmd(nc, [arrays], core_ids=[0])
    return r.results[0]["out_x"]
```

```python
from contextlib import ExitStack, contextmanager

import concourse.bass as bass
from concourse import mybir

F32 = mybir.dt.float32
F32R = mybir.dt.float32r
U32 = mybir.dt.uint32
I32 = mybir.dt.int32
ALU = mybir.AluOpType
ACT = mybir.ActivationFunctionType
AX_X = mybir.AxisListType.X

P = 128
D = 512
DC = D // P
BATCH = 2
SEQ = 512
CTX = 1024
TOK = BATCH * SEQ
TILES = TOK // P
HALF = 512
HALVES = TOK // HALF
EPS_LN = 1e-5
EPS_TERNARY = 1e-8
NK = 128
PEER_HEADS = 4
KEY_ROWS = 32


class Env:

    def __init__(self, nc, stack, io):
        self.nc, self.stack, self.io = nc, stack, io
        self.prefix = ""

    def sem(self, name):
        return self.nc.alloc_semaphore(name=f"{self.prefix}_{name}")


def setup_block(env):
    nc, io = env.nc, env.io
    env.prefix = "setup"
    x_loaded, gates_loaded = env.sem("x_loaded"), env.sem("gates_loaded")
    zeroed, made, tanh_done = env.sem("zeroed"), env.sem("made"), env.sem("tanh_done")
    iota_done = env.sem("iota_done")
    iota = env.stack.enter_context(nc.sbuf_tensor("iota", [P, 8], I32))
    with nc.Block() as block:
        @block.sync
        def _(sp):
            sp.dma_start(env.x[:], io["x"].rearrange("b (t p) d -> p (b t) d", p=P)).then_inc(x_loaded, 16)
            sp.dma_start(env.gates[:, 0:4], io["g_xattn"].partition_broadcast(P)).then_inc(gates_loaded, 16)
            sp.dma_start(env.gates[:, 4:8], io["g_ffn"].partition_broadcast(P)).then_inc(gates_loaded, 16)
            sp.wait_ge(x_loaded, 16)

        @block.gpsimd
        def _(pool):
            nc.gpsimd.memset(env.ident[:], 0.0).then_inc(zeroed, 1)
            nc.gpsimd.memset(env.eps_ln[:], EPS_LN).then_inc(made, 1)
            nc.gpsimd.iota(iota[:], pattern=[[1, 8]], base=0, channel_multiplier=0).then_inc(iota_done, 1)
            pool.wait_ge(iota_done, 1)
            nc.gpsimd.tensor_copy(env.iota8[:], iota[:]).then_inc(made, 1)
            pool.wait_ge(zeroed, 1)
            nc.gpsimd.affine_select(out=env.ident[:], in_=env.ident[:], compare_op=ALU.not_equal, fill=1.0,
                                    base=0, pattern=[[-1, P]], channel_multiplier=1).then_inc(made, 1)
            pool.wait_ge(made, 3)

        @block.scalar
        def _(act):
            act.wait_ge(gates_loaded, 32)
            nc.scalar.activation(env.tanh_gates[:], env.gates[:], ACT.Tanh).then_inc(tanh_done, 1)
            act.wait_ge(tanh_done, 1)


def store_block(env, out):
    nc = env.nc
    env.prefix = "store"
    stored = env.sem("stored")
    with nc.Block() as block:
        @block.sync
        def _(sp):
            sp.dma_start(out.rearrange("b (t p) d -> p (b t) d", p=P), env.x[:]).then_inc(stored, 16)
            sp.wait_ge(stored, 16)


def norm_block(env, name, split=None, quantised=False, load_context=False):
    nc = env.nc
    env.prefix = f"{name}_norm"
    stats_done, var_done, sd_done = env.sem("stats_done"), env.sem("var_done"), env.sem("sd_done")
    rstd_done, xn_done, transposed = env.sem("rstd_done"), env.sem("xn_done"), env.sem("transposed")
    copied, high_done, low_done = env.sem("copied"), env.sem("high_done"), env.sem("low_done")
    with ExitStack() as local:
        stats = local.enter_context(nc.sbuf_tensor(f"{name}_stats", [P, TILES, 6], F32))
        meanvar = local.enter_context(nc.sbuf_tensor(f"{name}_meanvar", [P, TILES, 2], F32))
        sd = local.enter_context(nc.sbuf_tensor(f"{name}_sd", [P, TILES], F32))
        rstd = local.enter_context(nc.sbuf_tensor(f"{name}_rstd", [P, TILES], F32))
        xn = local.enter_context(nc.sbuf_tensor(f"{name}_xn", [P, 4, D], F32))
        top = local.enter_context(nc.sbuf_tensor(f"{name}_norm_top", [P, 2], F32))
        tmp = local.enter_context(nc.sbuf_tensor(f"{name}_norm_tmp", [P, D], F32))
        turned = local.enter_context(nc.psum_tensor(f"{name}_turned", [P, 4, DC, P], F32))
        with nc.Block() as block:
            if load_context:
                @block.sync
                def _(sp):
                    for b in range(BATCH):
                        sp.dma_start(env.ctxT[:, :, b * CTX:(b + 1) * CTX],
                                     env.io["ctxT"][:, :, b * CTX:(b + 1) * CTX]).then_inc(env.ctx_loaded, 16)
                        sp.wait_ge(env.ctx_loaded, 16 * (b + 1))

            @block.vector
            def _(dve):
                links, count = env.sem("links"), [0]

                def link(ins):
                    count[0] += 1
                    ins.then_inc(links, 1)
                    dve.wait_ge(links, count[0])

                for t in range(TILES):
                    nc.vector.bn_stats(stats[:, t, :], env.x[:, t, :]).then_inc(stats_done, 1)
                for t in range(TILES):
                    dve.wait_ge(stats_done, t + 1)
                    nc.vector.bn_aggr(meanvar[:, t, :], stats[:, t, :]).then_inc(var_done, 1)
                dve.wait_ge(sd_done, 1)
                nc.vector.reciprocal(rstd[:], sd[:]).then_inc(rstd_done, 1)
                dve.wait_ge(rstd_done, 1)
                for t in range(TILES):
                    if t >= 4:
                        dve.wait_ge(transposed, t - 3)
                    row = xn[:, t % 4, :]
                    last = nc.vector.tensor_scalar(row, env.x[:, t, :], meanvar[:, t, 0:1], rstd[:, t:t + 1],
                                                   ALU.subtract, ALU.mult)
                    if quantised:
                        link(last)
                        quantise_rows(nc, link, row, row, top, tmp[:])
                        dve.sem_inc(xn_done, 1)
                    else:
                        last.then_inc(xn_done, 1)
                if split:
                    high, low = split
                    for t in range(TILES):
                        cols = slice(t * P, (t + 1) * P)
                        dve.wait_ge(copied, t + 1)
                        dve.wait_ge(high_done, t + 1)
                        nc.vector.tensor_tensor(low[:, :, cols], env.xT[:, :, cols], high[:, :, cols].bitcast(F32),
                                                ALU.subtract).then_inc(low_done, 1)
                    dve.wait_ge(low_done, TILES)

            @block.tensor
            def _(pe):
                for t in range(TILES):
                    pe.wait_ge(xn_done, t + 1)
                    if t >= 4:
                        pe.wait_ge(copied, t - 3)
                    for c in range(DC):
                        last = nc.tensor.transpose(turned[:, t % 4, c, :], xn[:, t % 4, c * P:(c + 1) * P], env.ident[:])
                    last.then_inc(transposed, 1)

            @block.scalar
            def _(act):
                act.wait_ge(var_done, TILES)
                nc.scalar.activation(sd[:], meanvar[:, :, 1], ACT.Sqrt, bias=env.eps_ln[:]).then_inc(sd_done, 1)
                for t in range(TILES):
                    act.wait_ge(transposed, t + 1)
                    cols = slice(t * P, (t + 1) * P)
                    nc.scalar.copy(env.xT[:, :, cols], turned[:, t % 4]).then_inc(copied, 1)
                    if split:
                        act.wait_ge(copied, t + 1)
                        nc.scalar.copy(split[0][:, :, cols], env.xT[:, :, cols]).then_inc(high_done, 1)
                act.wait_ge(copied, TILES)


def ternary_scales(env, name, scale, half, neg_half, gate, weight):
    nc, io = env.nc, env.io
    env.prefix = f"{name}_scales"
    G, E = io["w1"].shape[0], io["w1"].shape[2] // DC
    elements = G * E * D
    loaded = [env.sem(f"loaded{s}") for s in range(3)]
    summed, total_done = env.sem("summed"), env.sem("total_done")
    ones_made, scaled = env.sem("ones_made"), env.sem("scaled")
    with ExitStack() as local:
        raw = local.enter_context(nc.sbuf_tensor(f"{name}_absw", [P, 3, G * E * D // P], F32))
        partial = local.enter_context(nc.sbuf_tensor(f"{name}_partial", [P, 3], F32))
        ones = local.enter_context(nc.sbuf_tensor(f"{name}_ones", [P, P], F32))
        total = local.enter_context(nc.psum_tensor(f"{name}_total", [P, 512], F32))
        with nc.Block() as block:
            @block.sync
            def _(sp):
                for m, w in enumerate(("w1", "w2")):
                    sp.dma_start(raw[:, m, :].rearrange("p (g n) -> p g n", g=G),
                                 io[w].rearrange("g p n -> p g n")).then_inc(loaded[m], 16)
                sp.dma_start(raw[:, 2, :].rearrange("p (r n) -> p r n", n=D),
                             io["w3"].rearrange("g (r p) n -> p (g r) n", p=P)).then_inc(loaded[2], 16)

            @block.vector
            def _(dve):
                nc.vector.memset(ones[:], 1.0).then_inc(ones_made, 1)
                for m in range(3):
                    dve.wait_ge(loaded[m], 16)
                    nc.vector.tensor_reduce(partial[:, m:m + 1], raw[:, m, :], AX_X, ALU.add,
                                            apply_absolute_value=True).then_inc(summed, 1)
                dve.wait_ge(total_done, 1)
                nc.vector.tensor_scalar(scale[:], total[:, 0:3], 1.0 / elements, EPS_TERNARY, ALU.mult,
                                        ALU.add).then_inc(scaled, 1)
                dve.wait_ge(scaled, 1)
                nc.vector.tensor_scalar(half[:], scale[:], 0.5, None, ALU.mult).then_inc(scaled, 1)
                nc.vector.tensor_scalar(neg_half[:], scale[:], -0.5, None, ALU.mult).then_inc(scaled, 1)
                dve.wait_ge(scaled, 3)
                nc.vector.tensor_scalar(weight[:], scale[:, 1:2], scale[:, 2:3], gate, ALU.mult, ALU.mult).then_inc(scaled, 1)
                dve.wait_ge(scaled, 4)

            @block.tensor
            def _(pe):
                pe.wait_ge(ones_made, 1)
                pe.wait_ge(summed, 3)
                nc.tensor.matmul(total[:, 0:3], ones[:], partial[:], start=True, stop=True).then_inc(total_done, 1)


def ffn_block(env, name, chunks, weight, x_parts, ternary=None, peer=None, meanwhile=None):
    nc, io = env.nc, env.io
    env.prefix = name
    w1, w2, w3 = io["w1"], io.get("w2"), io["w3"]
    G, E = w1.shape[0], w1.shape[2] // DC
    NCH = len(chunks)
    starts = [sum(chunks[:c]) for c in range(NCH)]
    FULL = E // P
    STEPS = NCH * HALVES
    PAIRS = 2
    YB = 4
    SIDES = 1 if peer else 2
    UP_INC, DOWN_INC = 16 * SIDES, 16 * (bool(FULL) + bool(E % P))
    ADDS = TILES * (PEER_HEADS - 1) + 1
    SPLIT_DOWN = not peer
    RAW = 1 if SPLIT_DOWN else 2
    assert G % 2 == 0
    after = [range(k * TILES // STEPS, (k + 1) * TILES // STEPS) for k in range(STEPS)]
    up_loaded, down_loaded = env.sem("up_loaded"), [env.sem(f"down_loaded{s}") for s in range(RAW)]
    hidden_psum, silu_done = env.sem("hidden_psum"), env.sem("silu_done")
    product_done = env.sem("product_done")
    hidden_done = env.sem("hidden_done") if SPLIT_DOWN else product_done
    high_done = env.sem("high_done")
    y_done = env.sem("y_done")
    y_used = env.sem("y_used")
    up_high, up_ready = env.sem("up_high"), env.sem("up_ready")
    down_high, down_ready = env.sem("down_high"), env.sem("down_ready")
    UP_READY = SIDES
    if peer:
        sums_done, added = env.sem("sums_done"), env.sem("added")
        kept_done = env.sem("kept_done")
    with ExitStack() as local:
        def sb(n, shape, dt=F32):
            return local.enter_context(nc.sbuf_tensor(f"{name}_{n}", shape, dt))

        up_in = sb("up_in", [P, SIDES, DC * E])
        NW = 1 if ternary else 2
        up_parts = [sb(f"up_{n}", [P, 2, SIDES, DC * E], F32R) for n in ("high", "low")[:NW]]

        def load_up(sp, g):
            for side, w in enumerate((w1, w2)[:SIDES]):
                sp.dma_start(up_in[:, side, :], w[bass.ds(g, 1)].rearrange("g p n -> p (g n)")).then_inc(up_loaded, 16)

        def high_up(act, g, s, side):
            if side == 0:
                act.wait_ge(up_loaded, UP_INC * (g + 1))
            nc.scalar.copy(up_parts[0][:, s, side, :], up_in[:, side, :]).then_inc(up_high, 1)

        def low_up(pool, g, s):
            for side in range(SIDES):
                pool.wait_ge(up_high, SIDES * g + side + 1)
                nc.gpsimd.tensor_tensor(up_parts[1][:, s, side, :], up_in[:, side, :],
                                        up_parts[0][:, s, side, :].bitcast(F32), ALU.subtract).then_inc(up_ready, 1)

        if meanwhile:
            meanwhile({"sync": lambda sp: load_up(sp, 0),
                       "scalar": lambda act: [high_up(act, 0, 0, side) for side in range(SIDES)],
                       "gpsimd": lambda pool: low_up(pool, 0, 0)})
            env.prefix = name

        down_in = sb("down_in", [P, RAW, NCH, D])
        if SPLIT_DOWN:
            down_parts = [sb(f"down_{n}", [P, 2, NCH, D], F32R) for n in ("high", "low")[:NW]]
            h_parts = [sb("h_high", [P, 2, NCH, TOK], F32R), sb("h_low", [P, 2, NCH, TOK], F32R)]
            product = sb("product", [P, PAIRS, HALF])
        else:
            down_parts, h_parts = [down_in], [sb("h", [P, 2, NCH, TOK])]
        if ternary:
            scale, half, neg_half = ternary
            low_sign = sb("low_sign", [P, DC * E])
        silu_sb = sb("silu", [P, PAIRS, HALF])
        if peer:
            sims, bar, extra = peer
            I1 = E // NK
            routes = sb("routes", [P, 2, TILES, E])
            sums = sb("sums", [P, 2, E])
            kept = sb("kept", [P, 2, E])
        hidden_ps = local.enter_context(nc.psum_tensor(f"{name}_hidden", [P, PAIRS, 2, HALF], F32))
        y_ps = local.enter_context(nc.psum_tensor(f"{name}_y", [P, YB, D], F32))

        def terms(a, b):
            return [(m, n) for m in range(len(a)) for n in range(len(b)) if m + n < 2]

        with nc.Block() as block:
            @block.sync
            def _(sp):
                def load_down(g, s):
                    if FULL:
                        sp.dma_start(down_in[:, s, 0:FULL, :],
                                     w3[bass.ds(g, 1), 0:FULL * P, :].rearrange("g (c p) n -> p (g c) n", p=P)).then_inc(
                                         down_loaded[s], 16)
                    if E % P:
                        sp.dma_start(down_in[0:E % P, s, FULL, :],
                                     w3[bass.ds(g, 1), FULL * P:E, :].rearrange("g p n -> p (g n)")).then_inc(
                                         down_loaded[s], 16)

                if not meanwhile:
                    load_up(sp, 0)
                load_down(0, 0)
                if RAW == 1:
                    with sp.Fori(1, G) as g:
                        sp.wait_ge(up_ready, UP_READY * g)
                        load_up(sp, g)
                        sp.wait_ge(down_ready, g)
                        load_down(g, 0)
                else:
                    sp.wait_ge(up_ready, UP_READY)
                    load_up(sp, 1)
                    load_down(1, 1)
                    with sp.Fori(1, G // 2) as j:
                        for s in range(2):
                            g = 2 * j + s
                            sp.wait_ge(up_ready, UP_READY * g)
                            load_up(sp, g)
                            sp.wait_ge(y_used, g * TILES)
                            load_down(g, s)

            @block.tensor
            def _(pe):
                up_pairs = [(i, m, n) for i in range(DC) for m, n in terms(up_parts, x_parts)]
                down_pairs = [(c, m, n) for c in range(NCH) for m, n in terms(h_parts, down_parts)]

                def up_step(g, s, k):
                    if k == 0:
                        pe.wait_ge(up_ready, UP_READY * (g + 1))
                        if peer:
                            pe.wait_ge(added, ADDS * (g + 1))
                    c, h, b = k // HALVES, k % HALVES, k % PAIRS
                    m, e0 = chunks[c], starts[c]
                    pe.wait_ge(product_done, g * STEPS + k + 1)
                    for side in range(SIDES):
                        for q, (i, wp, xp) in enumerate(up_pairs):
                            w = up_parts[wp][:, s, side].rearrange("p (c e) -> p c e", c=DC)
                            last = nc.tensor.matmul(hidden_ps[0:m, b, side, :], w[:, i, e0:e0 + m],
                                                    x_parts[xp][:, i, h * HALF:(h + 1) * HALF],
                                                    start=(q == 0), stop=(q == len(up_pairs) - 1))
                    if peer:
                        for t in range(HALF // P):
                            last = nc.tensor.transpose(hidden_ps[:, b, 1, t * P:(t + 1) * P],
                                                       routes[:, s, h * (HALF // P) + t, c * P:(c + 1) * P],
                                                       env.ident[:])
                    last.then_inc(hidden_psum, 1)

                def down_tile(g, s, t, loads):
                    if t == 0:
                        pe.wait_ge(hidden_done, PAIRS + (g + 1) * STEPS)
                        if SPLIT_DOWN:
                            pe.wait_ge(down_ready, g + 1)
                        else:
                            pe.wait_ge(down_loaded[s], DOWN_INC * loads)
                    pe.wait_ge(y_used, g * TILES + t + 1 + TILES - YB)
                    for q, (c, hp, wp) in enumerate(down_pairs):
                        m = chunks[c]
                        last = nc.tensor.matmul(y_ps[:, t % YB, :], h_parts[hp][0:m, s, c, t * P:(t + 1) * P],
                                                down_parts[wp][0:m, s, c, :], start=(q == 0), stop=(q == len(down_pairs) - 1))
                    last.then_inc(y_done, 1)

                def group(g, s, loads):
                    for k in range(STEPS):
                        up_step(g, s, k)
                        for t in after[k]:
                            down_tile(g - 1, 1 - s, t, loads)

                for k in range(STEPS):
                    up_step(0, 0, k)
                with pe.Fori(0, G // 2 - 1) as j:
                    group(2 * j + 1, 1, j + 1)
                    group(2 * j + 2, 0, j + 1)
                group(G - 1, 1, G // 2)
                for t in range(TILES):
                    down_tile(G - 1, 1, t, G // 2)

            @block.scalar
            def _(act):
                def high_down(g, s, c):
                    if c == 0:
                        act.wait_ge(down_loaded[0], DOWN_INC * (g + 1))
                        if not isinstance(g, int) or g >= 2:
                            act.wait_ge(y_used, g * TILES)
                    m = chunks[c]
                    nc.scalar.copy(down_parts[0][0:m, s, c, :], down_in[0:m, 0, c, :]).then_inc(down_high, 1)

                def silu(g, k):
                    m, b = chunks[k // HALVES], k % PAIRS
                    act.wait_ge(hidden_psum, g * STEPS + k + 1)
                    act.wait_ge(product_done, g * STEPS + k + 1)
                    nc.scalar.activation(silu_sb[0:m, b, :], hidden_ps[0:m, b, 0, :], ACT.Silu,
                                         scale=scale[0:m, 0:1] if ternary else 1.0).then_inc(silu_done, 1)

                def high_hidden(g, s, k):
                    c, h, b = k // HALVES, k % HALVES, k % PAIRS
                    m = chunks[c]
                    act.wait_ge(product_done, PAIRS + g * STEPS + k + 1)
                    nc.scalar.copy(h_parts[0][0:m, s, c, h * HALF:(h + 1) * HALF], product[0:m, b, :]).then_inc(high_done, 1)

                def group(g, s, last=False):
                    for k in range(STEPS + 1):
                        if k < STEPS:
                            silu(g, k)
                        if SPLIT_DOWN and k:
                            high_hidden(g, s, k - 1)
                        if not ternary:
                            if k < SIDES and not last:
                                high_up(act, g + 1, 1 - s, k)
                            if SPLIT_DOWN and 1 <= k <= NCH:
                                high_down(g, s, k - 1)

                group(0, 0)
                with act.Fori(0, G // 2 - 1) as j:
                    group(2 * j + 1, 1)
                    group(2 * j + 2, 0)
                group(G - 1, 1, last=True)

            if not ternary:
                @block.gpsimd
                def _(pool):
                    def low_down(g, s):
                        for c in range(NCH):
                            m = chunks[c]
                            pool.wait_ge(down_high, NCH * g + c + 1)
                            last = nc.gpsimd.tensor_tensor(down_parts[1][0:m, s, c, :], down_in[0:m, 0, c, :],
                                                           down_parts[0][0:m, s, c, :].bitcast(F32), ALU.subtract)
                            last.then_inc(*((down_ready, 1) if c == NCH - 1 else (down_part, 1)))

                    def pair_sums(g, tiles):
                        for t in tiles:
                            for h in range(PEER_HEADS):
                                n = t * PEER_HEADS + h
                                pool.wait_ge(kept_done, g * TILES * PEER_HEADS + n + 1)
                                first = sims[:, t, h, bass.ds(g * I1, I1)].unsqueeze(2).to_broadcast([P, I1, NK])
                                second = sims[:, t, h, KEY_ROWS:KEY_ROWS + NK].unsqueeze(1).to_broadcast([P, I1, NK])
                                nc.gpsimd.tensor_tensor(sums[:, n % 2, :].rearrange("p (a b) -> p a b", a=I1),
                                                        first, second, ALU.add).then_inc(sums_done, 1)

                    def group(g, s, last=False):
                        if peer and not last:
                            pair_sums(g + 1, range(TILES // 2))
                        if not last:
                            low_up(pool, g + 1, 1 - s)
                        if SPLIT_DOWN:
                            low_down(g, s)
                        if peer and not last:
                            pair_sums(g + 1, range(TILES // 2, TILES))

                    down_part = env.sem("down_part")
                    if peer:
                        pair_sums(0, range(TILES))
                    group(0, 0)
                    with pool.Fori(0, G // 2 - 1) as j:
                        group(2 * j + 1, 1)
                        group(2 * j + 2, 0)
                    group(G - 1, 1, last=True)

            @block.vector
            def _(dve):
                def hidden_step(g, s, k):
                    if k < STEPS:
                        c, h, b = k // HALVES, k % HALVES, k % PAIRS
                        m, cols = chunks[c], slice(h * HALF, (h + 1) * HALF)
                        dve.wait_ge(silu_done, g * STEPS + k + 1)
                        if SPLIT_DOWN:
                            dve.wait_ge(hidden_done, g * STEPS + k + 1)
                        out = product[0:m, b, :] if SPLIT_DOWN else h_parts[0][0:m, s, c, cols]
                        nc.vector.tensor_tensor(out, silu_sb[0:m, b, :], hidden_ps[0:m, b, 1, :], ALU.mult).then_inc(
                            product_done, 1)
                    if SPLIT_DOWN and k:
                        c, h, b = (k - 1) // HALVES, (k - 1) % HALVES, (k - 1) % PAIRS
                        m, cols = chunks[c], slice(h * HALF, (h + 1) * HALF)
                        dve.wait_ge(high_done, g * STEPS + k)
                        nc.vector.tensor_tensor(h_parts[1][0:m, s, c, cols], product[0:m, b, :],
                                                h_parts[0][0:m, s, c, cols].bitcast(F32), ALU.subtract).then_inc(hidden_done, 1)

                def output(g, t):
                    w = weight[:, 0:1] if len(weight.shape) == 2 else weight[:, t, bass.ds(g, 1)]
                    dve.wait_ge(y_done, g * TILES + t + 1)
                    dve.wait_ge(y_used, g * TILES + t + 1)
                    nc.vector.scalar_tensor_tensor(env.x[:, t, :], y_ps[:, t % YB, :], w, env.x[:, t, :],
                                                   ALU.mult, ALU.add).then_inc(y_used, 1)

                def quantise_up(g, s, side):
                    dve.wait_ge(up_loaded, UP_INC * (g + 1))
                    nc.vector.tensor_scalar(low_sign[:], up_in[:, side, :], neg_half[:, side:side + 1], None,
                                            ALU.is_lt).then_inc(up_high, 1)
                    dve.wait_ge(up_high, SIDES * g + side + 1)
                    nc.vector.scalar_tensor_tensor(up_parts[0][:, s, side, :], up_in[:, side, :], half[:, side:side + 1],
                                                   low_sign[:], ALU.is_gt, ALU.subtract).then_inc(up_ready, 1)
                    dve.wait_ge(up_ready, SIDES * g + side + 1)

                def quantise_down(g, s):
                    dve.wait_ge(down_loaded[0], DOWN_INC * (g + 1))
                    src = down_in[:, 0].rearrange("p c e -> p (c e)")
                    nc.vector.tensor_scalar(low_sign[:], src, neg_half[:, 2:3], None, ALU.is_lt).then_inc(down_high, 1)
                    dve.wait_ge(down_high, g + 1)
                    nc.vector.scalar_tensor_tensor(down_parts[0][:, s].rearrange("p c e -> p (c e)"), src, half[:, 2:3],
                                                   low_sign[:], ALU.is_gt, ALU.subtract).then_inc(down_ready, 1)
                    dve.wait_ge(down_ready, g + 1)

                def routes_tile(g, s, t):
                    row = routes[:, s, t, :]
                    for h in range(PEER_HEADS):
                        n = t * PEER_HEADS + h
                        n_all = g * TILES * PEER_HEADS + n
                        b = bar[:, n:n + 1]
                        dve.wait_ge(sums_done, n_all + 1)
                        to = kept[:, n % 2, :] if h else row
                        nc.vector.scalar_tensor_tensor(to, sums[:, n % 2, :], b, sums[:, n % 2, :], ALU.is_ge,
                                                       ALU.mult).then_inc(kept_done, 1)
                        dve.wait_ge(kept_done, 2 + n_all + 1)
                        if h:
                            nc.vector.tensor_tensor(row, row, kept[:, n % 2, :], ALU.add).then_inc(added, 1)
                            dve.wait_ge(added, g * ADDS + t * (PEER_HEADS - 1) + h)

                def routes_end(g, s):
                    nc.vector.tensor_tensor(routes[:, s, :, E - 1], routes[:, s, :, E - 1],
                                            extra[:, bass.ds(g, 1), :].rearrange("p g t -> p (g t)"), ALU.add).then_inc(
                                                added, 1)

                def group(g, s, first=False, last=False):
                    for k in range(STEPS + SPLIT_DOWN):
                        hidden_step(g, s, k)
                        if peer and not last:
                            routes_tile(g + 1, 1 - s, k)
                        if k < STEPS and not first:
                            for t in after[k]:
                                output(g - 1, t)
                        if ternary:
                            if k < SIDES and not last:
                                quantise_up(g + 1, 1 - s, k)
                            if k == SIDES:
                                quantise_down(g, s)
                    if peer and not last:
                        routes_end(g + 1, 1 - s)

                dve.sem_inc(product_done, PAIRS)
                if SPLIT_DOWN:
                    dve.sem_inc(hidden_done, PAIRS)
                dve.sem_inc(y_used, TILES)
                if peer:
                    dve.sem_inc(kept_done, 2)
                    for t in range(TILES):
                        routes_tile(0, 0, t)
                    routes_end(0, 0)
                if ternary:
                    for side in range(SIDES):
                        quantise_up(0, 0, side)
                group(0, 0, first=True)
                with dve.Fori(0, G // 2 - 1) as j:
                    group(2 * j + 1, 1)
                    group(2 * j + 2, 0)
                group(G - 1, 1, last=True)
                for t in range(TILES):
                    output(G - 1, t)
                dve.wait_ge(y_used, TILES + G * TILES)


def expert_weights_block(env, name, G, shared, normalise, gate, weight, first):
    nc, io = env.nc, env.io
    env.prefix = f"{name}_experts"
    EX = 8
    N = EX + (1 if shared else 0)
    loaded, logits_done, step, exp_done = env.sem("loaded"), env.sem("logits_done"), env.sem("step"), env.sem("exp_done")
    with ExitStack() as local:
        def sb(n, shape, dt=F32):
            return local.enter_context(nc.sbuf_tensor(f"{name}_{n}", shape, dt))

        w = sb("router", [P, DC, N])
        logits, top, index = sb("logits", [P, TILES, N]), sb("top", [P, TILES, 8]), sb("index", [P, TILES, 8], U32)
        index_f, less_max, exps = sb("index_f", [P, TILES, 8]), sb("less_max", [P, TILES, 9]), sb("exps", [P, TILES, 9])
        total, inv, pick = sb("total", [P, TILES, 2]), sb("inv", [P, TILES, 2]), sb("pick", [P, 2, TILES, EX])
        ps = local.enter_context(nc.psum_tensor(f"{name}_router_ps", [P, TILES, 16], F32))
        with nc.Block() as block:
            @block.sync
            def _(sp):
                sp.dma_start(w[:], io["router"]).then_inc(loaded, 16)
                first["sync"](sp)

            @block.tensor
            def _(pe):
                pe.wait_ge(loaded, 16)
                for t in range(TILES):
                    for i in range(DC):
                        last = nc.tensor.matmul(ps[:, t, 0:N], env.xT[:, i, t * P:(t + 1) * P], w[:, i, :],
                                                start=(i == 0), stop=(i == DC - 1))
                last.then_inc(logits_done, 1)

            @block.gpsimd
            def _(pool):
                first["gpsimd"](pool)

            @block.scalar
            def _(act):
                first["scalar"](act)
                act.wait_ge(step, 1)
                nc.scalar.activation(exps[:, :, 0:N], less_max[:, :, 0:N], ACT.Exp).then_inc(exp_done, 1)

            @block.vector
            def _(dve):
                links = env.sem("links")
                count = [0]

                def link(ins, wait=True):
                    count[0] += 1
                    ins.then_inc(links, 1)
                    if wait:
                        dve.wait_ge(links, count[0])

                def spread(ap, n=EX):
                    return ap.to_broadcast([P, TILES, n])

                dve.wait_ge(logits_done, 1)
                link(nc.vector.tensor_copy(logits[:], ps[:, :, 0:N]))
                for t in range(TILES):
                    link(nc.vector.max(top[:, t, :], logits[:, t, 0:EX]), wait=(t == TILES - 1))
                for t in range(TILES):
                    link(nc.vector.max_index(index[:, t, :], top[:, t, :], logits[:, t, 0:EX]), wait=(t == TILES - 1))
                link(nc.vector.tensor_copy(index_f[:], index[:]))
                link(nc.vector.tensor_tensor(less_max[:, :, 0:EX], top[:], spread(top[:, :, 0:1]), ALU.subtract))
                if shared:
                    link(nc.vector.tensor_scalar(less_max[:, :, EX:N], logits[:, :, EX:N], -1.0, None, ALU.mult))
                dve.sem_inc(step, 1)
                dve.wait_ge(exp_done, 1)
                link(nc.vector.tensor_reduce(total[:, :, 0], exps[:, :, 0:2 if normalise else EX], AX_X, ALU.add))
                if shared:
                    link(nc.vector.tensor_scalar(total[:, :, 1:2], exps[:, :, EX:N], 1.0, None, ALU.add))
                n = 2 if shared else 1
                link(nc.vector.reciprocal(inv[:, :, 0:n], total[:, :, 0:n]))
                for p in range(2):
                    link(nc.vector.tensor_tensor(pick[:, p], spread(index_f[:, :, p:p + 1]),
                                                 env.iota8[:].unsqueeze(1).to_broadcast([P, TILES, EX]), ALU.is_equal))
                    link(nc.vector.tensor_tensor(pick[:, p], pick[:, p], spread(exps[:, :, p:p + 1]), ALU.mult))
                link(nc.vector.tensor_tensor(pick[:, 0], pick[:, 0], pick[:, 1], ALU.add))
                link(nc.vector.tensor_tensor(pick[:, 1], pick[:, 0], spread(inv[:, :, 0:1]), ALU.mult))
                link(nc.vector.tensor_scalar(weight[:, :, shared:G], pick[:, 1], gate, None, ALU.mult))
                if shared:
                    link(nc.vector.tensor_scalar(weight[:, :, 0:shared], spread(inv[:, :, 1:2], shared), gate, None,
                                                 ALU.mult))


def product_keys_block(env, name, sims, bar, extra, G, first):
    nc, io = env.nc, env.io
    env.prefix = f"{name}_keys"
    H = PEER_HEADS
    wq_loaded, keys_loaded, keys_clear = env.sem("wq_loaded"), env.sem("keys_loaded"), env.sem("keys_clear")
    q_psum, q_done, sims_psum, sims_done = env.sem("q_psum"), env.sem("q_done"), env.sem("sims_psum"), env.sem("sims_done")
    kept_done, tile_done = env.sem("kept_done"), env.sem("tile_done")
    with ExitStack() as local:
        def sb(n, shape, dt=F32):
            return local.enter_context(nc.sbuf_tensor(f"{name}_{n}", shape, dt))

        wq, keys, qT = sb("wq", [P, DC, D]), sb("keys", [P, H, 2 * NK]), sb("qT", [P, H, TOK])
        full = sb("full", [P, 2, H, 2 * NK])
        best, index = sb("best", [P, 2, H, 2, 8]), sb("index", [P, 2, H, 8], U32)
        past, pairs, top = sb("past", [P, H, 8]), sb("pairs", [P, H, 8, 8]), sb("top", [P, H, 8])
        reach = sb("reach", [P, H, 8, 8])
        q_ps = local.enter_context(nc.psum_tensor(f"{name}_q_ps", [P, 4, HALF], F32))
        sims_ps = local.enter_context(nc.psum_tensor(f"{name}_sims_ps", [P, 2, H, 2 * NK], F32))
        with nc.Block() as block:
            @block.sync
            def _(sp):
                sp.dma_start(wq[:], io["wq"]).then_inc(wq_loaded, 16)
                sp.wait_ge(keys_clear, 1)
                for side in range(2):
                    sp.dma_start(keys[64 * side:64 * side + 64, :, side * NK:(side + 1) * NK],
                                 io["keys"][:, side]).then_inc(keys_loaded, 16)
                first["sync"](sp)

            @block.tensor
            def _(pe):
                pe.wait_ge(wq_loaded, 16)
                for n in range(H * HALVES):
                    f, h = n // HALVES, n % HALVES
                    if n >= 4:
                        pe.wait_ge(q_done, n - 3)
                    for i in range(DC):
                        last = nc.tensor.matmul(q_ps[:, n % 4, :], wq[:, i, f * P:(f + 1) * P],
                                                env.xT[:, i, h * HALF:(h + 1) * HALF], start=(i == 0), stop=(i == DC - 1))
                    last.then_inc(q_psum, 1)
                pe.wait_ge(keys_loaded, 32)
                pe.wait_ge(q_done, H * HALVES)
                for t in range(TILES):
                    if t >= 2:
                        pe.wait_ge(sims_done, t - 1)
                    for f in range(H):
                        last = nc.tensor.matmul(sims_ps[:, t % 2, f, :], qT[:, f, t * P:(t + 1) * P], keys[:, f, :],
                                                start=True, stop=True)
                    last.then_inc(sims_psum, 1)

            @block.scalar
            def _(act):
                for n in range(H * HALVES):
                    f, h = n // HALVES, n % HALVES
                    act.wait_ge(q_psum, n + 1)
                    nc.scalar.copy(qT[:, f, h * HALF:(h + 1) * HALF], q_ps[:, n % 4, :]).then_inc(q_done, 1)
                for t in range(TILES):
                    act.wait_ge(sims_psum, t + 1)
                    if t >= 2:
                        act.wait_ge(tile_done, t - 1)
                    nc.scalar.copy(full[:, t % 2], sims_ps[:, t % 2]).then_inc(sims_done, 1)
                    act.wait_ge(sims_done, t + 1)
                    nc.scalar.copy(sims[:, t, :, 0:KEY_ROWS], full[:, t % 2, :, 0:KEY_ROWS]).then_inc(kept_done, 1)
                    nc.scalar.copy(sims[:, t, :, KEY_ROWS:], full[:, t % 2, :, NK:2 * NK]).then_inc(kept_done, 1)
                first["scalar"](act)
                act.wait_ge(kept_done, 2 * TILES)

            @block.gpsimd
            def _(pool):
                first["gpsimd"](pool)

            @block.vector
            def _(dve):
                links = env.sem("links")
                count = [0]

                def link(ins, wait=True):
                    count[0] += 1
                    ins.then_inc(links, 1)
                    if wait:
                        dve.wait_ge(links, count[0])

                nc.vector.memset(keys[:], 0.0).then_inc(keys_clear, 1)
                link(nc.vector.memset(extra[:], 0.0))
                for t in range(TILES):
                    u = t % 2
                    dve.wait_ge(sims_done, t + 1)
                    for f in range(H):
                        for side in range(2):
                            link(nc.vector.max(best[:, u, f, side, :], full[:, u, f, side * NK:(side + 1) * NK]),
                                 wait=(f == H - 1 and side == 1))
                    for f in range(H):
                        link(nc.vector.max_index(index[:, u, f, :], best[:, u, f, 0, :], full[:, u, f, 0:NK]), wait=False)
                        link(nc.vector.tensor_tensor(pairs[:, f],
                                                     best[:, u, f, 0, :].unsqueeze(2).to_broadcast([P, 8, 8]),
                                                     best[:, u, f, 1, :].unsqueeze(1).to_broadcast([P, 8, 8]), ALU.add),
                             wait=(f == H - 1))
                    for f in range(H):
                        link(nc.vector.max(top[:, f, :], pairs[:, f].rearrange("p a b -> p (a b)")), wait=(f == H - 1))
                    link(nc.vector.tensor_scalar(bar[:, t * H:(t + 1) * H], top[:, :, 7], 0.0, None, ALU.max), wait=False)
                    link(nc.vector.tensor_scalar(past[:], index[:, u], KEY_ROWS - 0.5, None, ALU.is_gt))
                    for f in range(H):
                        b = bar[:, t * H + f:t * H + f + 1]
                        flat = pairs[:, f].rearrange("p a b -> p (a b)")
                        link(nc.vector.scalar_tensor_tensor(reach[:, f].rearrange("p a b -> p (a b)"), flat, b, flat,
                                                            ALU.is_ge, ALU.mult), wait=(f == H - 1))
                    link(nc.vector.tensor_tensor(reach[:].rearrange("p f a b -> p (f a) b"),
                                                 reach[:].rearrange("p f a b -> p (f a) b"),
                                                 past[:].rearrange("p f a -> p (f a)").unsqueeze(2).to_broadcast([P, H * 8, 8]),
                                                 ALU.mult))
                    link(nc.vector.tensor_reduce(extra[:, G - 1, t:t + 1], reach[:].rearrange("p f a b -> p (f a b)"),
                                                 AX_X, ALU.add))
                    dve.sem_inc(tile_done, 1)


def masked_attention_block(env, name, aT, keep_mask):
    nc, io = env.nc, env.io
    env.prefix = f"{name}_attn"
    HD = 32
    FG, HG = 4, 4
    ONES, LOW = HD, 2 * HD
    KT = CTX // P
    SCALE = HD ** -0.5
    BOUND = 50.0
    SETS = FG * BATCH
    UNITS = HG * KT
    LAG = 5
    S_SLOTS, PT_SLOTS = 3, 4
    KEYS, QUERIES = range(0, 2), 2
    PRODUCTS = 5
    PRODUCT_AT = {3: 0, 8: 1, 12: 2, 18: 3, 24: 4}
    INV_PARTS = SEQ // P
    STACKS = 16 * 16
    LOADS = 16 * 6
    ctx_loaded, w_loaded, ones_made = env.ctx_loaded, env.sem("w_loaded"), env.sem("ones_made")
    product_psum, high_done = env.sem("product_psum"), env.sem("high_done")
    product_used = env.sem("product_used")
    k_stacked, q_stacked = env.sem("k_stacked"), env.sem("q_stacked")
    scores_done, clipped = env.sem("scores_done"), env.sem("clipped")
    exp_done, pv_done = env.sem("exp_done"), env.sem("pv_done")

    def earlier(this, before, u):
        if u >= 0:
            return this, u
        return before, u + UNITS

    def head_steps(this, before, w):
        head, step = w // KT - 1, w % KT
        if head >= 0:
            return (*this, head), step
        return (before is not None and (*before, head + HG)), step

    probs_high, probs_low = env.sem("probs_high"), env.sem("probs_low")
    inv_done, norm_done = env.sem("inv_done"), env.sem("norm_done")
    from_low, joined = env.sem("from_low"), env.sem("joined")
    v_high, v_low = env.sem("v_high"), env.sem("v_low")
    with ExitStack() as local:
        def sb(n, shape, dt=F32):
            return local.enter_context(nc.sbuf_tensor(f"{name}_{n}", shape, dt))

        def psum(n, shape):
            return local.enter_context(nc.psum_tensor(f"{name}_{n}", shape, F32))

        ctxT = env.ctxT
        values = sb("values", [P, 2, KT, HG, 3, HD], F32R)
        k_stack, q_stack = sb("k_stack", [P, 2, HG, CTX], F32R), sb("q_stack", [P, 2, HG, SEQ], F32R)
        kh, kl = sb("kh", [P, CTX], F32R), sb("kl", [P, CTX], F32R)
        qh, ql = sb("qh", [P, SEQ], F32R), sb("ql", [P, SEQ], F32R)
        wk, wq, wv = sb("wk", [P, DC * P]), sb("wq", [P, DC * P]), sb("wv", [P, DC * P])
        bk, bq, bv = sb("bk", [P, 1]), sb("bq", [P, 1]), sb("bv", [P, P])
        within, probs = sb("within", [P, 2, SEQ]), sb("probs", [P, PT_SLOTS, SEQ])
        p_high, p_low = sb("p_high", [P, PT_SLOTS, SEQ], F32R), sb("p_low", [P, PT_SLOTS, SEQ], F32R)
        inv, result, v_sum = sb("inv", [HD, SEQ]), sb("result", [HD, SEQ]), sb("v_sum", [P, HALF])
        s_ps, o_ps = psum("s_ps", [P, S_SLOTS, SEQ]), psum("o_ps", [P, HG, SEQ])
        product_ps = psum("product_ps", [P, HALF])

        def values_of(slot, i, part):
            t0 = (i - QUERIES - 1) * (KT // 2)
            return values[:, slot, t0:t0 + KT // 2, :, part, :].rearrange("p t h e -> p (t h) e")

        with nc.Block() as block:
            @block.sync
            def _(sp):
                def load_weights(f):
                    for to, of in ((wk, "wk"), (bk, "bk"), (wq, "wq"), (bq, "bq"), (wv, "wv")):
                        sp.dma_start(to[:], io[of][bass.ds(f, 1)].rearrange("g p n -> p (g n)")).then_inc(w_loaded, 16)
                    sp.dma_start(bv[:], io["bv"][bass.ds(f, 1)].rearrange("g n -> (g n)").partition_broadcast(P)).then_inc(
                        w_loaded, 16)

                def stack(n, s):
                    if not isinstance(n, int) or n >= 2:
                        sp.wait_ge(scores_done, UNITS * (n - 1))
                    for dst, halves, sem, last in ((k_stack, (kh, kl, kh, kl), k_stacked, max(KEYS)),
                                                   (q_stack, (qh, qh, ql, ql), q_stacked, QUERIES)):
                        sp.wait_ge(product_used, 1 + PRODUCTS * n + last + 1)
                        for h in range(HG):
                            for r in range(4):
                                sp.dma_start(dst[32 * r:32 * r + 32, s, h, :].bitcast(F32),
                                             halves[r][32 * h:32 * h + 32, :].bitcast(F32)).then_inc(sem, 16)

                load_weights(0)
                stack(0, 0)
                with sp.Fori(1, FG) as f:
                    stack(2 * f - 1, 1)
                    sp.wait_ge(product_used, 1 + PRODUCTS * 2 * f)
                    load_weights(f)
                    stack(2 * f, 0)
                stack(SETS - 1, 1)

            @block.tensor
            def _(pe):
                def product(n, s, f, i):
                    b = s
                    if i == 0:
                        pe.wait_ge(w_loaded, LOADS * (f + 1))
                    pe.wait_ge(product_used, PRODUCTS * n + i + 1)
                    if i <= QUERIES:
                        w, moving = (wk, ctxT[:, :, b * CTX + i * HALF:b * CTX + (i + 1) * HALF]) if i in KEYS \
                            else (wq, env.xT[:, :, b * SEQ:(b + 1) * SEQ])
                        for c in range(DC):
                            last = nc.tensor.matmul(product_ps[:], w[:, c * P:(c + 1) * P], moving[:, c, :],
                                                    start=(c == 0), stop=(c == DC - 1))
                    else:
                        for j in range(KT // 2):
                            t = b * KT + (i - QUERIES - 1) * (KT // 2) + j
                            for c in range(DC):
                                last = nc.tensor.matmul(product_ps[:, j * P:(j + 1) * P], ctxT[:, c, t * P:(t + 1) * P],
                                                        wv[:, c * P:(c + 1) * P], start=(c == 0), stop=(c == DC - 1))
                    last.then_inc(product_psum, 1)

                def pv(n, s, v):
                    h, kt = v // KT, v % KT
                    pe.wait_ge(probs_low, PT_SLOTS + UNITS * n + v + 1)
                    if kt == 0:
                        pe.wait_ge(norm_done, HG * n + h + 1)
                    stationary = values[:, s, kt, h].rearrange("p a e -> p (a e)")
                    nc.tensor.matmul(o_ps[0:3 * HD, h, :], stationary, p_high[:, v % PT_SLOTS, :],
                                     start=(kt == 0), stop=False)
                    nc.tensor.matmul(o_ps[0:3 * HD, h, :], stationary, p_low[:, v % PT_SLOTS, :],
                                     start=False, stop=(kt == KT - 1)).then_inc(pv_done, 1)

                def attend(this, following, before):
                    n, s = this
                    pe.wait_ge(k_stacked, STACKS * (n + 1))
                    pe.wait_ge(q_stacked, STACKS * (n + 1))
                    pe.wait_ge(v_low, 2 * (n + 1))
                    for u in range(UNITS):
                        h, kt = u // KT, u % KT
                        pe.wait_ge(clipped, UNITS * n + u + 1 + (u < UNITS % S_SLOTS))
                        nc.tensor.matmul(s_ps[:, u % S_SLOTS, :], k_stack[:, s, h, kt * P:(kt + 1) * P],
                                         q_stack[:, s, h, :], start=True, stop=True).then_inc(scores_done, 1)
                        if following and u in PRODUCT_AT:
                            product(*following, PRODUCT_AT[u])
                        of, v = earlier(this, before, u - LAG)
                        if of:
                            pv(*of, v)

                pe.wait_ge(ones_made, 1)
                pe.wait_ge(ctx_loaded, 16 * BATCH)
                for i in range(PRODUCTS):
                    product(0, 0, 0, i)
                attend((0, 0), (1, 1, 0), None)
                with pe.Fori(0, FG - 1) as f:
                    attend((2 * f + 1, 1), (2 * f + 2, 0, f + 1), (2 * f, 0))
                    attend((2 * f + 2, 0), (2 * f + 3, 1, f + 1), (2 * f + 1, 1))
                attend((SETS - 1, 1), None, (SETS - 2, 0))
                for v in range(UNITS - LAG, UNITS):
                    pv(SETS - 1, 1, v)

            @block.scalar
            def _(act):
                def high(n, s, i):
                    if i > QUERIES:
                        act.wait_ge(product_used, 1 + PRODUCTS * n + i + 1)
                        nc.scalar.copy(values_of(s, i, 0), v_sum[:].rearrange("p (n e) -> p n e", e=HD)).then_inc(v_high, 1)
                        return
                    key = i in KEYS
                    if i in (0, QUERIES) and (not isinstance(n, int) or n):
                        act.wait_ge(k_stacked if key else q_stacked, STACKS * n)
                    dst = kh[:, i * HALF:(i + 1) * HALF] if key else qh[:]
                    act.wait_ge(product_psum, PRODUCTS * n + i + 1)
                    nc.scalar.activation(dst, product_ps[:], ACT.Identity, bias=(bk if key else bq)[:]).then_inc(high_done, 1)

                def high_probs(n, u):
                    act.wait_ge(exp_done, 2 + UNITS * n + u + 1)
                    act.wait_ge(pv_done, UNITS * n + u + 1)
                    nc.scalar.copy(p_high[:, u % PT_SLOTS, :], probs[:, u % PT_SLOTS, :]).then_inc(probs_high, 1)

                def low_result(n, h):
                    act.wait_ge(pv_done, PT_SLOTS + UNITS * n + KT * (h + 1))
                    act.wait_ge(norm_done, HG + HG * n + h)
                    nc.scalar.copy(result[:], o_ps[LOW:LOW + HD, h, :]).then_inc(from_low, 1)

                def attend(this, following, before):
                    n, s = this
                    for u in range(UNITS):
                        tile = s * KT + u % KT
                        act.wait_ge(clipped, UNITS * n + u + 1 + S_SLOTS)
                        act.wait_ge(probs_low, UNITS * n + u + 1)
                        nc.scalar.activation(probs[:, u % PT_SLOTS, :], within[:, u % 2, :], ACT.Exp,
                                             bias=keep_mask[:, 1, tile:tile + 1],
                                             scale=keep_mask[:, 0, tile:tile + 1]).then_inc(exp_done, 1)
                        if u:
                            high_probs(n, u - 1)
                        elif before:
                            high_probs(before[0], UNITS - 1)
                        of, step = head_steps(this, before, u - LAG)
                        if of and step == 0:
                            low_result(of[0], of[2])
                        if following and u in PRODUCT_AT:
                            high(*following, PRODUCT_AT[u])

                act.sem_inc(exp_done, 2)
                for i in range(PRODUCTS):
                    high(0, 0, i)
                attend((0, 0), (1, 1), None)
                with act.Fori(0, FG - 1) as f:
                    attend((2 * f + 1, 1), (2 * f + 2, 0), (2 * f, 0))
                    attend((2 * f + 2, 0), (2 * f + 3, 1), (2 * f + 1, 1))
                attend((SETS - 1, 1), None, (SETS - 2, 0))
                high_probs(SETS - 1, UNITS - 1)
                low_result(SETS - 1, HG - 1)

            @block.gpsimd
            def _(pool):
                with pool.Fori(0, SETS * UNITS // PT_SLOTS) as g:
                    for k in range(PT_SLOTS):
                        pool.wait_ge(probs_high, PT_SLOTS * g + k + 1)
                        nc.gpsimd.tensor_tensor(p_low[:, k, :], probs[:, k, :], p_high[:, k, :].bitcast(F32),
                                                ALU.subtract).then_inc(probs_low, 1)

            @block.vector
            def _(dve):
                def low(n, s, i):
                    key = i in KEYS
                    if i > QUERIES:
                        dve.wait_ge(product_psum, PRODUCTS * n + i + 1)
                        if i > QUERIES + 1 or not isinstance(n, int) or n:
                            dve.wait_ge(v_low, 2 * n + i - QUERIES - 1)
                        nc.vector.tensor_tensor(v_sum[:].rearrange("p (t e) -> p t e", e=P),
                                                product_ps[:].rearrange("p (t e) -> p t e", e=P),
                                                bv[:].unsqueeze(1).to_broadcast([P, KT // 2, P]), ALU.add).then_inc(
                                                    product_used, 1)
                        return
                    halves = slice(i * HALF, (i + 1) * HALF) if key else slice(0, SEQ)
                    high, to = (kh, kl) if key else (qh, ql)
                    if i in (0, QUERIES) and (not isinstance(n, int) or n):
                        dve.wait_ge(k_stacked if key else q_stacked, STACKS * n)
                    dve.wait_ge(high_done, (QUERIES + 1) * n + i + 1)
                    nc.vector.scalar_tensor_tensor(to[:, halves], product_ps[:], (bk if key else bq)[:],
                                                   high[:, halves].bitcast(F32), ALU.add, ALU.subtract).then_inc(
                                                       product_used, 1)

                def low_values(n, s, i):
                    dve.wait_ge(v_high, 2 * n + i - QUERIES)
                    nc.vector.tensor_tensor(values_of(s, i, 2), v_sum[:].rearrange("p (n e) -> p n e", e=HD),
                                            values_of(s, i, 0).bitcast(F32), ALU.subtract).then_inc(v_low, 1)

                def invert(n, s, f, h, part):
                    cols = slice(part * P, (part + 1) * P)
                    dve.wait_ge(pv_done, PT_SLOTS + UNITS * n + KT * (h + 1))
                    dve.wait_ge(norm_done, HG + HG * n + h)
                    nc.vector.reciprocal(inv[:, cols], o_ps[ONES:ONES + HD, h, cols]).then_inc(inv_done, 1)

                def join(n, s, f, h):
                    dve.wait_ge(from_low, HG * n + h + 1)
                    nc.vector.tensor_tensor(result[:], o_ps[0:HD, h, :], result[:], ALU.add).then_inc(joined, 1)

                def head_step(head, step):
                    if head and step < INV_PARTS:
                        invert(*head, step)
                    if head and step == INV_PARTS:
                        join(*head)
                    if head and step == INV_PARTS + 1:
                        normalise(*head)

                def normalise(n, s, f, h):
                    dve.wait_ge(inv_done, INV_PARTS * (HG * n + h + 1))
                    dve.wait_ge(joined, HG * n + h + 1)
                    nc.vector.tensor_tensor(
                        aT[HD * h:HD * (h + 1), bass.ds(f, 1), s * SEQ:(s + 1) * SEQ].rearrange("p c n -> p (c n)"),
                        result[:], inv[:], ALU.mult).then_inc(norm_done, 1)

                def attend(this, following, before):
                    n, s, f = this
                    for u in range(UNITS):
                        dve.wait_ge(scores_done, UNITS * n + u + 1)
                        dve.wait_ge(exp_done, UNITS * n + u + 1)
                        nc.vector.tensor_scalar(within[:, u % 2, :], s_ps[:, u % S_SLOTS, :],
                                                BOUND / SCALE, -BOUND / SCALE, ALU.min, ALU.max).then_inc(clipped, 1)
                        head_step(*head_steps(this, before, u - LAG))
                        if following and u - 2 in PRODUCT_AT and PRODUCT_AT[u - 2] > QUERIES:
                            low_values(*following, PRODUCT_AT[u - 2])
                        if following and u in PRODUCT_AT:
                            low(*following, PRODUCT_AT[u])

                nc.vector.memset(values[:, :, :, :, 1, :].bitcast(F32), 1.0).then_inc(ones_made, 1)
                dve.sem_inc(product_used, 1)
                dve.sem_inc(norm_done, HG)
                dve.sem_inc(pv_done, PT_SLOTS)
                dve.sem_inc(probs_low, PT_SLOTS)
                dve.sem_inc(clipped, S_SLOTS)
                for i in range(PRODUCTS):
                    low(0, 0, i)
                    if i > QUERIES:
                        low_values(0, 0, i)
                attend((0, 0, 0), (1, 1), None)
                with dve.Fori(0, FG - 1) as f:
                    attend((2 * f + 1, 1, f), (2 * f + 2, 0), (2 * f, 0, f))
                    attend((2 * f + 2, 0, f + 1), (2 * f + 3, 1), (2 * f + 1, 1, f))
                attend((SETS - 1, 1, FG - 1), None, (SETS - 2, 0, FG - 1))
                for w in range(UNITS - LAG, UNITS + KT):
                    head_step(*head_steps((SETS - 1, 1, FG - 1), None, w))
                dve.wait_ge(norm_done, HG * SETS + HG)


def softmax_attention_block(env, name, aT):
    nc, io = env.nc, env.io
    env.prefix = f"{name}_attn"
    HD = 32
    FG, HG = 4, 4
    KT, QT = CTX // P, SEQ // P
    SCALE = HD ** -0.5
    SETS = FG * BATCH
    UNITS = HG * QT
    BANKS = 2
    PAIR = 2 * P
    KEYS, QUERIES = range(0, 2), 2
    PRODUCTS = 5
    BEHIND = {2: 0, 4: 1, 6: 2, 9: 3, 12: 4}
    TURN_LAG, PV_LAG, SUM_LAG = 2, 4, 9
    PROBS = 4
    STACKS = 8 * 16
    LOADS = 16 * 5
    assert PRODUCTS % 2 == 1 and UNITS % 2 == 0
    ctx_loaded, bv_loaded, w_loaded = env.ctx_loaded, env.sem("bv_loaded"), env.sem("w_loaded")
    product_psum, product_high = env.sem("product_psum"), env.sem("product_high")
    product_used = env.sem("product_used")
    stacked = [env.sem(f"stacked{h}") for h in range(HG)]
    wq_scaled, scores_done, max_done = env.sem("wq_scaled"), env.sem("scores_done"), env.sem("max_done")
    exp_done, inv_done, scaled = env.sem("exp_done"), env.sem("inv_done"), env.sem("scaled")
    turned = [env.sem(f"turned{i}") for i in range(BANKS)]
    high_done = [env.sem(f"high_done{i}") for i in range(BANKS)]
    low_done = [env.sem(f"low_done{i}") for i in range(BANKS)]
    pv_done = env.sem("pv_done")
    from_low, head_done = env.sem("from_low"), env.sem("head_done")

    def rotation(following):
        order = []
        for u in range(UNITS):
            order.append((u, None))
            if following is not None and u in BEHIND:
                order.append((None, BEHIND[u]))
        return order

    def earlier(this, before, u):
        if u >= 0:
            return this, u
        return before, u + UNITS

    with ExitStack() as local:
        def sb(n, shape, dt=F32):
            return local.enter_context(nc.sbuf_tensor(f"{name}_{n}", shape, dt))

        def psum(n, shape):
            return local.enter_context(nc.psum_tensor(f"{name}_{n}", shape, F32))

        ctxT = env.ctxT
        values = sb("values", [P, 2, KT, HG, 2, HD], F32R)
        k_stack, q_stack = sb("k_stack", [P, HG, CTX], F32R), sb("q_stack", [P, HG, SEQ], F32R)
        kh, kl = sb("kh", [P, CTX], F32R), sb("kl", [P, CTX], F32R)
        qh, ql = sb("qh", [P, SEQ], F32R), sb("ql", [P, SEQ], F32R)
        wk, wq, wv = sb("wk", [P, DC * P]), sb("wq", [P, DC * P]), sb("wv", [P, DC * P])
        bk, bq, bv = sb("bk", [P, 1]), sb("bq", [P, 1]), sb("bv", [HD, FG * HG])
        probs = sb("probs", [P, PROBS, CTX])
        pT_high, pT_low = sb("pT_high", [P, 2, KT, PAIR], F32R), sb("pT_low", [P, 2, KT, PAIR], F32R)
        less_max = sb("less_max", [P, 2, 1])
        sums = sb("sums", [P, PROBS, 2])
        of_low = sb("of_low", [HD, 2, SEQ])
        o_ps, s_ps, t_ps = psum("o_ps", [P, 2, SEQ]), psum("s_ps", [P, 2, CTX]), psum("t_ps", [P, BANKS, HALF])

        def product_parts(i, b):
            if i > QUERIES:
                t0 = (i - QUERIES - 1) * (KT // 2)
                return [values[:, b, t0:t0 + KT // 2, :, part, :].rearrange("p t h e -> p (t h) e")
                        for part in range(2)] + [None]
            if i == QUERIES:
                return qh[:], ql[:], bq
            cols = slice(i * HALF, (i + 1) * HALF)
            return kh[:, cols], kl[:, cols], bk

        def product_psum_of(i, slot):
            ps = s_ps[:, slot, 0:HALF]
            return ps.rearrange("p (n e) -> p n e", e=HD) if i > QUERIES else ps

        def pT(halves, u, i):
            return halves[:, (u // 2) % 2, i * (KT // BANKS):(i + 1) * (KT // BANKS), (u % 2) * P:(u % 2 + 1) * P]

        def bank(i):
            return t_ps[:, i, :].rearrange("p (k q) -> p k q", q=P)

        with nc.Block() as block:
            @block.sync
            def _(sp):
                def load_weights(f):
                    for to, of in ((wk, "wk"), (bk, "bk"), (wq, "wq"), (bq, "bq"), (wv, "wv")):
                        sp.dma_start(to[:], io[of][bass.ds(f, 1)].rearrange("g p n -> p (g n)")).then_inc(w_loaded, 16)

                def stack(n):
                    sp.wait_ge(product_used, PRODUCTS * n + QUERIES + 1)
                    for h in range(HG):
                        if not isinstance(n, int) or n:
                            sp.wait_ge(scores_done, UNITS * (n - 1) + QT * (h + 1))
                        for dst, halves in ((k_stack, (kh, kl, kh, kl)), (q_stack, (qh, qh, ql, ql))):
                            for r in range(4):
                                sp.dma_start(dst[32 * r:32 * r + 32, h, :].bitcast(F32),
                                             halves[r][32 * h:32 * h + 32, :].bitcast(F32)).then_inc(stacked[h], 16)

                load_weights(0)
                sp.dma_start(bv[:], io["bv"]).then_inc(bv_loaded, 16)
                stack(0)
                with sp.Fori(1, FG) as f:
                    stack(2 * f - 1)
                    sp.wait_ge(product_used, PRODUCTS * 2 * f)
                    load_weights(f)
                    stack(2 * f)
                stack(SETS - 1)

            @block.tensor
            def _(pe):
                def product(n, b, f, i, slot):
                    if i == 0:
                        pe.wait_ge(w_loaded, LOADS * (f + 1))
                    if i == QUERIES:
                        pe.wait_ge(wq_scaled, 2 * (f + 1))
                    if i <= QUERIES:
                        at = b * CTX + i * HALF
                        w, moving = (wk, ctxT[:, :, at:at + HALF]) if i in KEYS else (wq, env.xT[:, :, b * SEQ:(b + 1) * SEQ])
                        for c in range(DC):
                            last = nc.tensor.matmul(s_ps[:, slot, 0:HALF], w[:, c * P:(c + 1) * P], moving[:, c, :],
                                                    start=(c == 0), stop=(c == DC - 1))
                    else:
                        for t in range(KT // 2):
                            at = b * CTX + ((i - QUERIES - 1) * (KT // 2) + t) * P
                            for c in range(DC):
                                last = nc.tensor.matmul(s_ps[:, slot, t * P:(t + 1) * P], ctxT[:, c, at:at + P],
                                                        wv[:, c * P:(c + 1) * P], start=(c == 0), stop=(c == DC - 1))
                    last.then_inc(product_psum, 1)

                def scores(n, b, f, u, slot):
                    h, q = u // QT, u % QT
                    if q == 0:
                        pe.wait_ge(stacked[h], STACKS * (n + 1))
                    for i in range(CTX // HALF):
                        last = nc.tensor.matmul(s_ps[:, slot, i * HALF:(i + 1) * HALF], q_stack[:, h, q * P:(q + 1) * P],
                                                k_stack[:, h, i * HALF:(i + 1) * HALF], start=True, stop=True)
                    last.then_inc(scores_done, 1)

                def turn(n, b, f, u):
                    pe.wait_ge(scaled, UNITS * n + u + 1)
                    for i in range(BANKS):
                        pe.wait_ge(low_done[i], UNITS * n + u + 1)
                        for k in range(KT // BANKS):
                            kt = i * (KT // BANKS) + k
                            last = nc.tensor.transpose(t_ps[:, i, k * P:(k + 1) * P], probs[:, u % PROBS, kt * P:(kt + 1) * P],
                                                       env.ident[:])
                        last.then_inc(turned[i], 1)

                def pv(n, b, f, v):
                    h, q, i, first = v // QT, v // 2 * 2 % QT, v % 2, v // 2 * 2
                    if v % QT == 0:
                        pe.wait_ge(head_done, HG * n + h + 1)
                    pe.wait_ge(low_done[i], 1 + UNITS * n + first + 2)
                    for k in range(KT // BANKS):
                        kt = i * (KT // BANKS) + k
                        for part in (pT_high, pT_low):
                            last = nc.tensor.matmul(o_ps[0:2 * HD, h % 2, q * P:q * P + PAIR],
                                                    values[:, b, kt, h].rearrange("p a e -> p (a e)"),
                                                    part[:, (v // 2) % 2, kt, :],
                                                    start=(kt == 0 and part is pT_high), stop=(kt == KT - 1 and part is pT_low))
                    last.then_inc(pv_done, 1)

                def attend(this, following, before):
                    n, b, f = this
                    pe.wait_ge(product_used, PRODUCTS * (n + 1))
                    order = rotation(following)
                    for r, (u, i) in enumerate(order):
                        held_by, held_for = order[r - 2] if r >= 2 else (r - 2, None)
                        if held_for is None:
                            pe.wait_ge(exp_done, 2 + UNITS * n + held_by + 1)
                        else:
                            pe.wait_ge(product_used, PRODUCTS * (n + 1) + held_for + 1)
                        if u is None:
                            product(*following, i, (r + b) % 2)
                            continue
                        scores(*this, u, (r + b) % 2)
                        for lag, step in ((TURN_LAG, turn), (PV_LAG, pv)):
                            of, v = earlier(this, before, u - lag)
                            if of:
                                step(*of, v)

                pe.wait_ge(ctx_loaded, 16 * BATCH)
                for i in range(PRODUCTS):
                    if i >= 2:
                        pe.wait_ge(product_used, i - 1)
                    product(0, 0, 0, i, i % 2)
                attend((0, 0, 0), (1, 1, 0), None)
                with pe.Fori(0, FG - 1) as f:
                    attend((2 * f + 1, 1, f), (2 * f + 2, 0, f + 1), (2 * f, 0, f))
                    attend((2 * f + 2, 0, f + 1), (2 * f + 3, 1, f + 1), (2 * f + 1, 1, f))
                final = (SETS - 1, 1, FG - 1)
                attend(final, None, (SETS - 2, 0, FG - 1))
                for u in range(UNITS, UNITS + PV_LAG):
                    if u - TURN_LAG < UNITS:
                        turn(*final, u - TURN_LAG)
                    pv(*final, u - PV_LAG)

            @block.scalar
            def _(act):
                def scale_queries(f):
                    act.wait_ge(w_loaded, LOADS * (f + 1))
                    nc.scalar.activation(wq[:], wq[:], ACT.Copy, scale=SCALE).then_inc(wq_scaled, 1)
                    nc.scalar.activation(bq[:], bq[:], ACT.Copy, scale=SCALE).then_inc(wq_scaled, 1)

                def high_product(n, b, f, i, slot):
                    if i == 0 and b == 0:
                        scale_queries(f)
                    if i == QUERIES:
                        act.wait_ge(wq_scaled, 2 * (f + 1))
                    if i in (0, QUERIES) and (not isinstance(n, int) or n):
                        for h in range(HG):
                            act.wait_ge(stacked[h], STACKS * n)
                    act.wait_ge(product_psum, PRODUCTS * n + i + 1)
                    dst, _, bias = product_parts(i, b)
                    nc.scalar.activation(dst, product_psum_of(i, slot), ACT.Identity, bias=bias[:] if bias else 0.0).then_inc(
                        product_high, 1)

                def high(n, u):
                    act.wait_ge(pv_done, UNITS * n + u // 2 * 2 + 1)
                    for i in range(BANKS):
                        act.wait_ge(turned[i], UNITS * n + u + 1 + i * PROBS)
                        nc.scalar.copy(pT(pT_high, u, i), bank(i)).then_inc(high_done[i], 1)

                def low_values(n, h):
                    act.wait_ge(pv_done, 3 + UNITS * n + QT * (h + 1))
                    act.wait_ge(head_done, HG * n + h + 1)
                    nc.scalar.copy(of_low[:, h % 2, :], o_ps[HD:2 * HD, h % 2, :]).then_inc(from_low, 1)

                def attend(this, following, before):
                    n, b = this
                    for r, (u, i) in enumerate(rotation(following)):
                        if u is None:
                            high_product(*following, i, (r + b) % 2)
                            continue
                        of, v = earlier(this, before, u - TURN_LAG)
                        if of:
                            high(of[0], v)
                        act.wait_ge(max_done, UNITS * n + u + 1)
                        act.wait_ge(turned[1], UNITS * n + u + 1)
                        nc.scalar.activation(probs[:, u % PROBS, :], s_ps[:, (r + b) % 2, :], ACT.Exp,
                                             bias=less_max[:, u % 2, :], accum_out=sums[:, u % PROBS, 0:1]).then_inc(exp_done, 1)
                        of, v = earlier(this, before, u - SUM_LAG)
                        if of and v % QT == 0:
                            low_values(of[0], v // QT)

                act.sem_inc(exp_done, 2)
                act.sem_inc(turned[1], PROBS)
                for i in range(PRODUCTS):
                    high_product(0, 0, 0, i, i % 2)
                attend((0, 0), (1, 1, 0), None)
                with act.Fori(0, FG - 1) as f:
                    attend((2 * f + 1, 1), (2 * f + 2, 0, f + 1), (2 * f, 0))
                    attend((2 * f + 2, 0), (2 * f + 3, 1, f + 1), (2 * f + 1, 1))
                attend((SETS - 1, 1), None, (SETS - 2, 0))
                for u in range(UNITS - TURN_LAG, UNITS):
                    high(SETS - 1, u)
                for h in range(HG - 2, HG):
                    low_values(SETS - 1, h)

            @block.gpsimd
            def _(pool):
                def scale(g):
                    for u in range(PROBS):
                        pool.wait_ge(inv_done, PROBS * g + u + 1)
                        nc.gpsimd.tensor_tensor(probs[:, u, :], probs[:, u, :], sums[:, u, 1:2].to_broadcast([P, CTX]),
                                                ALU.mult).then_inc(scaled, 1)

                with pool.Fori(0, SETS * UNITS // PROBS) as g:
                    scale(g)

            @block.vector
            def _(dve):
                def low_product(n, b, i, slot):
                    if i in (0, QUERIES) and (not isinstance(n, int) or n):
                        for h in range(HG):
                            dve.wait_ge(stacked[h], STACKS * n)
                    dve.wait_ge(product_high, PRODUCTS * n + i + 1)
                    high, dst, bias = product_parts(i, b)
                    nc.vector.scalar_tensor_tensor(dst, product_psum_of(i, slot), bias[:] if bias else 0.0, high.bitcast(F32),
                                                   ALU.add, ALU.subtract).then_inc(product_used, 1)

                def invert(n, u):
                    dve.wait_ge(exp_done, 2 + UNITS * n + u + 1)
                    nc.vector.reciprocal(sums[:, u % PROBS, 1:2], sums[:, u % PROBS, 0:1]).then_inc(inv_done, 1)

                def low(n, u):
                    for i in range(BANKS):
                        dve.wait_ge(high_done[i], UNITS * n + u + 1)
                        nc.vector.tensor_tensor(pT(pT_low, u, i), bank(i), pT(pT_high, u, i).bitcast(F32),
                                                ALU.subtract).then_inc(low_done[i], 1)

                def finish(n, b, f, h):
                    dve.wait_ge(from_low, HG * n + h + 1)
                    nc.vector.scalar_tensor_tensor(
                        aT[HD * h:HD * (h + 1), bass.ds(f, 1), b * SEQ:(b + 1) * SEQ].rearrange("p c n -> p (c n)"),
                        o_ps[0:HD, h % 2, :], bv[:, bass.ds(HG * f + h, 1)], of_low[:, h % 2, :], ALU.add, ALU.add).then_inc(
                            head_done, 1)

                def attend(this, following, before):
                    n, b, f = this
                    for r, (u, i) in enumerate(rotation(following)):
                        if u is None:
                            low_product(*following, i, (r + b) % 2)
                            continue
                        of, v = earlier(this, before, u - 1)
                        if of:
                            invert(of[0], v)
                        dve.wait_ge(scores_done, UNITS * n + u + 1)
                        nc.vector.tensor_reduce(less_max[:, u % 2, :], s_ps[:, (r + b) % 2, :], AX_X, ALU.max,
                                                negate=True).then_inc(max_done, 1)
                        of, v = earlier(this, before, u - TURN_LAG)
                        if of:
                            low(of[0], v)
                        of, v = earlier(this, before, u - SUM_LAG)
                        if of and v % QT == 0:
                            finish(*of, v // QT)

                dve.sem_inc(head_done, 2)
                dve.sem_inc(pv_done, 3)
                for i in range(BANKS):
                    dve.sem_inc(low_done[i], 1)
                dve.wait_ge(bv_loaded, 16)
                for i in range(PRODUCTS):
                    low_product(0, 0, i, i % 2)
                attend((0, 0, 0), (1, 1), None)
                with dve.Fori(0, FG - 1) as f:
                    attend((2 * f + 1, 1, f), (2 * f + 2, 0), (2 * f, 0, f))
                    attend((2 * f + 2, 0, f + 1), (2 * f + 3, 1), (2 * f + 1, 1, f))
                final = (SETS - 1, 1, FG - 1)
                attend(final, None, (SETS - 2, 0, FG - 1))
                invert(SETS - 1, UNITS - 1)
                for u in range(UNITS - TURN_LAG, UNITS):
                    low(SETS - 1, u)
                for h in range(HG - 2, HG):
                    finish(*final, h)
                dve.wait_ge(head_done, HG * SETS + 2)


def token_major_block(env, name, aT, heads_out):
    nc = env.nc
    env.prefix = f"{name}_back"
    turned, copied = env.sem("turned"), env.sem("copied")
    with nc.psum_tensor(f"{name}_back_ps", [P, 4, DC, P], F32) as ps, nc.Block() as block:
        @block.tensor
        def _(pe):
            for t in range(TILES):
                if t >= 4:
                    pe.wait_ge(copied, t - 3)
                for c in range(DC):
                    last = nc.tensor.transpose(ps[:, t % 4, c, :], aT[:, c, t * P:(t + 1) * P], env.ident[:])
                last.then_inc(turned, 1)

        @block.scalar
        def _(act):
            for t in range(TILES):
                act.wait_ge(turned, t + 1)
                nc.scalar.copy(heads_out[:, t, :], ps[:, t % 4].rearrange("p c n -> p (c n)")).then_inc(copied, 1)
            act.wait_ge(copied, TILES)


def linear_attention_block(env, name, heads_out):
    nc, io = env.nc, env.io
    env.prefix = f"{name}_attn"
    HEADS, HD, FD = 16, 32, 64
    FG, HG = 4, 4
    VC = HD + 1
    KT, QT = CTX // P, SEQ // P
    CT = BATCH * KT
    PAIR = 2 * VC
    K_PARTS, Q_PARTS = BATCH * CTX // HALF, TOK // HALF
    MAPPED = BATCH * 2
    PRODUCTS = K_PARTS + Q_PARTS + MAPPED
    EPS = 1e-8
    ctx_loaded, wv_loaded, w_loaded, maps_loaded = (env.ctx_loaded, env.sem("wv_loaded"), env.sem("w_loaded"),
                                                    env.sem("maps_loaded"))
    cleared, v_psum, v_done = env.sem("cleared"), env.sem("v_psum"), env.sem("v_done")
    proj_psum, proj_done = env.sem("proj_psum"), env.sem("proj_done")
    kf_psum, kf_done = env.sem("kf_psum"), env.sem("kf_done")
    kv_step, kv_copied = env.sem("kv_step"), env.sem("kv_copied")
    o_done, norm_done, inv_step = env.sem("o_done"), env.sem("norm_done"), env.sem("inv_step")
    with ExitStack() as local:
        def sb(n, shape, dt=F32):
            return local.enter_context(nc.sbuf_tensor(f"{name}_{n}", shape, dt))

        def psum(n):
            return local.enter_context(nc.psum_tensor(f"{name}_{n}", [P, 2, HALF], F32))

        ctxT, values = env.ctxT, sb("values", [P, CT, HEADS, VC])
        wv, bv, wk, wq = sb("wv", [P, DC, D]), sb("bv", [P, D]), sb("wk", [P, DC * P]), sb("wq", [P, DC * P])
        bk, bq, mask = sb("bk", [P, 1]), sb("bq", [P, 1]), sb("mask", [P, CT])
        wqf, wkf = sb("wqf", [P, HG * FD]), sb("wkf", [P, HG * FD])
        kT, qT = sb("kT", [P, BATCH * CTX]), sb("qT", [P, TOK])
        kf, qf = sb("kf", [P, 2, HG * FD]), sb("qf", [P, MAPPED, SEQ])
        kv = sb("kv", [P, BATCH, 2, PAIR])
        inv = sb("inv", [P, 2, HG, 1])
        proj_ps, kf_ps, kv_ps, o_ps = psum("proj_ps"), psum("kf_ps"), psum("kv_ps"), psum("o_ps")

        with nc.Block() as block:
            @block.sync
            def _(sp):
                sp.dma_start(wv[:], io["wv"]).then_inc(wv_loaded, 16)
                sp.dma_start(bv[:], io["bv"].partition_broadcast(P)).then_inc(wv_loaded, 16)

                def load_weights(f):
                    for to, of in ((wk, "wk"), (wq, "wq"), (bk, "bk"), (bq, "bq")):
                        sp.dma_start(to[:], io[of][bass.ds(f, 1)].rearrange("g p n -> p (g n)")).then_inc(w_loaded, 16)

                load_weights(0)
                sp.dma_start(mask[:], io["mask_f"]).then_inc(maps_loaded, 16)
                sp.wait_ge(cleared, 4)
                for h in range(HG):
                    for to, of in ((wqf, "wqf"), (wkf, "wkf")):
                        sp.dma_start(to[HD * h:HD * (h + 1), FD * h:FD * (h + 1)], io[of]).then_inc(maps_loaded, 16)
                with sp.Fori(1, FG) as f:
                    sp.wait_ge(proj_done, 2 + PRODUCTS * (f - 1) + K_PARTS + Q_PARTS)
                    load_weights(f)

            @block.tensor
            def _(pe):
                pe.wait_ge(ctx_loaded, 16 * BATCH)
                pe.wait_ge(wv_loaded, 32)
                for t in range(CT):
                    if t >= 2:
                        pe.wait_ge(v_done, t - 1)
                    for i in range(DC):
                        last = nc.tensor.matmul(kf_ps[:, t % 2, :], ctxT[:, i, t * P:(t + 1) * P], wv[:, i, :],
                                                start=(i == 0), stop=(i == DC - 1))
                    last.then_inc(v_psum, 1)
                pe.wait_ge(v_done, CT)
                pe.wait_ge(maps_loaded, 16 * (2 * HG + 1))
                with pe.Fori(0, FG) as f:
                    def slot(i):
                        pe.wait_ge(proj_done, PRODUCTS * f + i + 1)
                        return proj_ps[:, i % 2, :]

                    pe.wait_ge(w_loaded, 64 * (f + 1))
                    for i in range(K_PARTS + Q_PARTS):
                        w, moving, n = (wk, ctxT, i) if i < K_PARTS else (wq, env.xT, i - K_PARTS)
                        to = slot(i)
                        for c in range(DC):
                            last = nc.tensor.matmul(to, w[:, c * P:(c + 1) * P], moving[:, c, n * HALF:(n + 1) * HALF],
                                                    start=(c == 0), stop=(c == DC - 1))
                        last.then_inc(proj_psum, 1)

                    def accumulate(t):
                        b = t // KT
                        pe.wait_ge(kf_done, CT * f + t + 1 + 2)
                        if t % KT == 0:
                            pe.wait_ge(kv_copied, 4 * BATCH * f + 4 * b + 4)
                        for j in range(2):
                            rhs = values[:, t, bass.ds(HG * f + 2 * j, 2), :].rearrange("p h e -> p (h e)")
                            last = nc.tensor.matmul(kv_ps[:, j, 0:PAIR], kf[:, t % 2, j * P:(j + 1) * P], rhs,
                                                    start=(t % KT == 0), stop=(t % KT == KT - 1))
                        last.then_inc(kv_step, 1)

                    pe.wait_ge(proj_done, 2 + PRODUCTS * f + K_PARTS)
                    for t in range(CT):
                        pe.wait_ge(kf_done, CT * f + t + 1)
                        nc.tensor.matmul(kf_ps[:, t % 2, 0:HG * FD], kT[:, t * P:(t + 1) * P], wkf[:],
                                         start=True, stop=True).then_inc(kf_psum, 1)
                        if t >= 1:
                            accumulate(t - 1)
                    accumulate(CT - 1)
                    pe.wait_ge(proj_done, 2 + PRODUCTS * f + K_PARTS + Q_PARTS)
                    for m in range(MAPPED):
                        b, j = m // 2, m % 2
                        nc.tensor.matmul(slot(K_PARTS + Q_PARTS + m), wqf[:, j * P:(j + 1) * P],
                                         qT[:, b * SEQ:(b + 1) * SEQ], start=True, stop=True).then_inc(proj_psum, 1)
                    pe.wait_ge(proj_done, 2 + PRODUCTS * (f + 1))
                    pe.wait_ge(kv_copied, 4 * BATCH * (f + 1) + 4)
                    for q in range(TILES):
                        pe.wait_ge(norm_done, TILES * f + q + 1)
                        b, at = q // QT, (q % QT) * P
                        for j in range(2):
                            last = nc.tensor.matmul(o_ps[:, q % 2, j * PAIR:(j + 1) * PAIR], qf[:, 2 * b + j, at:at + P],
                                                    kv[:, b, j, :], start=True, stop=True)
                        last.then_inc(o_done, 1)

            @block.scalar
            def _(act):
                act.sem_inc(proj_done, 2)
                with act.Fori(0, FG) as f:
                    act.wait_ge(kv_step, CT * f + 2)
                    act.wait_ge(norm_done, TILES * f + 2)
                    for i in range(PRODUCTS):
                        act.wait_ge(proj_psum, PRODUCTS * f + i + 1)
                        ps = proj_ps[:, i % 2, :]
                        if i < K_PARTS:
                            ins = nc.scalar.activation(kT[:, i * HALF:(i + 1) * HALF], ps, ACT.Identity, bias=bk[:])
                        elif i < K_PARTS + Q_PARTS:
                            n = i - K_PARTS
                            ins = nc.scalar.activation(qT[:, n * HALF:(n + 1) * HALF], ps, ACT.Identity, bias=bq[:])
                        else:
                            ins = nc.scalar.activation(qf[:, i - K_PARTS - Q_PARTS, :], ps, ACT.Relu)
                        ins.then_inc(proj_done, 1)

            @block.vector
            def _(dve):
                nc.vector.memset(wqf[:], 0.0).then_inc(cleared, 1)
                nc.vector.memset(wkf[:], 0.0).then_inc(cleared, 1)
                nc.vector.memset(kv[:], 0.0).then_inc(cleared, 1)
                nc.vector.memset(values[:, :, :, HD:VC], 1.0).then_inc(cleared, 1)
                dve.wait_ge(cleared, 4)
                dve.wait_ge(wv_loaded, 32)
                for t in range(CT):
                    dve.wait_ge(v_psum, t + 1)
                    nc.vector.tensor_tensor(values[:, t, :, 0:HD], kf_ps[:, t % 2, :].rearrange("p (h e) -> p h e", e=HD),
                                            bv[:].rearrange("p (h e) -> p h e", e=HD), ALU.add).then_inc(v_done, 1)
                dve.wait_ge(maps_loaded, 16 * (2 * HG + 1))
                dve.sem_inc(kf_done, 2)
                dve.sem_inc(kv_step, 2)
                dve.sem_inc(kv_copied, 4)
                dve.sem_inc(norm_done, 2)
                with dve.Fori(0, FG) as f:
                    for t in range(CT):
                        dve.wait_ge(kf_psum, CT * f + t + 1)
                        dve.wait_ge(kv_step, CT * f + t + 1)
                        nc.vector.tensor_scalar(kf[:, t % 2, :], kf_ps[:, t % 2, 0:HG * FD], 0.0, mask[:, t:t + 1],
                                                ALU.max, ALU.mult).then_inc(kf_done, 1)
                        if t % KT == KT - 1:
                            b = t // KT
                            dve.wait_ge(kv_step, CT * f + t + 1 + 2)
                            for j in range(2):
                                for half in range(2):
                                    rows, cols = slice(64 * half, 64 * half + 64), slice(VC * half, VC * (half + 1))
                                    nc.vector.tensor_copy(kv[rows, b, j, cols], kv_ps[rows, j, cols]).then_inc(kv_copied, 1)
                    for q in range(TILES):
                        o = o_ps[:, q % 2, 0:HG * VC].rearrange("p (h e) -> p h e", e=VC)
                        k = TILES * f + q
                        dve.wait_ge(o_done, k + 1)
                        nc.vector.tensor_scalar(inv[:, q % 2], o[:, :, HD:VC], EPS, None, ALU.add).then_inc(inv_step, 1)
                        dve.wait_ge(inv_step, 2 * k + 1)
                        nc.vector.reciprocal(inv[:, q % 2], inv[:, q % 2]).then_inc(inv_step, 1)
                        dve.wait_ge(inv_step, 2 * k + 2)
                        nc.vector.tensor_tensor(heads_out[:, q, bass.ds(P * f, P)].rearrange("p (h e) -> p h e", e=HD),
                                                o[:, :, 0:HD], inv[:, q % 2].to_broadcast([P, HG, HD]), ALU.mult).then_inc(
                                                    norm_done, 1)
                dve.wait_ge(norm_done, TILES * FG + 2)


def key_mask_block(env, name, keep_mask):
    nc, io = env.nc, env.io
    env.prefix = f"{name}_mask"
    loaded, step = env.sem("loaded"), env.sem("step")
    n = BATCH * CTX // P
    with ExitStack() as local:
        raw = local.enter_context(nc.sbuf_tensor(f"{name}_mask_raw", [P, n], I32))
        keep = local.enter_context(nc.sbuf_tensor(f"{name}_keep", [P, n], F32))
        with nc.Block() as block:
            @block.sync
            def _(sp):
                sp.dma_start(raw[:], io["mask"]).then_inc(loaded, 16)

            @block.vector
            def _(dve):
                dve.wait_ge(loaded, 16)
                nc.vector.tensor_scalar(keep[:], raw[:], 0.5, None, ALU.is_gt).then_inc(step, 1)
                dve.wait_ge(step, 1)
                nc.vector.tensor_scalar(keep_mask[:, 0, :], keep[:], 32 ** -0.5, None, ALU.mult).then_inc(step, 1)
                nc.vector.tensor_scalar(keep_mask[:, 1, :], keep[:], -1.0, 50.0, ALU.add, ALU.mult).then_inc(step, 1)
                dve.wait_ge(step, 3)


def quantise_rows(nc, link, src, dst, top, tmp):
    MAGIC = 1.5 * 2 ** 23
    s, inv = top[:, 0:1], top[:, 1:2]
    link(nc.vector.tensor_reduce(s, src, AX_X, ALU.max, apply_absolute_value=True))
    link(nc.vector.tensor_scalar(s, s, 1.0 / 127.0, 1e-8, ALU.mult, ALU.max))
    link(nc.vector.reciprocal(inv, s))
    link(nc.vector.tensor_scalar(tmp, src, inv, MAGIC, ALU.mult, ALU.add))
    link(nc.vector.tensor_scalar(tmp, tmp, MAGIC + 127.0, MAGIC - 127.0, ALU.min, ALU.max))
    link(nc.vector.tensor_scalar(dst, tmp, -MAGIC, s, ALU.add, ALU.mult))


def quantise_weights_block(env, name, wq_scratch, wp_scratch):
    nc, io = env.nc, env.io
    env.prefix = f"{name}_quant"
    FG = D // P
    loaded, ready, turned, copied, stored = (env.sem("loaded"), env.sem("ready"), env.sem("turned"), env.sem("copied"),
                                             env.sem("stored"))
    with ExitStack() as local:
        w = local.enter_context(nc.sbuf_tensor(f"{name}_w", [P, 2 * FG, D], F32))
        wT = local.enter_context(nc.sbuf_tensor(f"{name}_wT", [P, 2 * FG, DC, P], F32))
        tmp = local.enter_context(nc.sbuf_tensor(f"{name}_tmp", [P, D], F32))
        top = local.enter_context(nc.sbuf_tensor(f"{name}_top", [P, 2], F32))
        ps = local.enter_context(nc.psum_tensor(f"{name}_quant_ps", [P, 2, DC, P], F32))
        with nc.Block() as block:
            @block.sync
            def _(sp):
                sp.dma_start(w[:, 0:FG, :], io["wq_rows"].rearrange("(f p) n -> p f n", p=P)).then_inc(loaded, 16)
                sp.dma_start(w[:, FG:2 * FG, :], io["wp_rows"].rearrange("(f p) n -> p f n", p=P)).then_inc(loaded, 16)
                for g in range(FG):
                    sp.wait_ge(copied, g + 1)
                    sp.dma_start(wq_scratch[g], wT[:, g].rearrange("p c n -> p (c n)")).then_inc(stored, 16)
                sp.wait_ge(copied, 2 * FG)
                for g in range(FG):
                    sp.dma_start(wp_scratch[:, :, g * P:(g + 1) * P], wT[:, FG + g]).then_inc(stored, 16)
                sp.wait_ge(stored, 16 * 2 * FG)

            @block.vector
            def _(dve):
                links, count = env.sem("links"), [0]

                def link(ins):
                    count[0] += 1
                    ins.then_inc(links, 1)
                    dve.wait_ge(links, count[0])

                dve.wait_ge(loaded, 32)
                for g in range(2 * FG):
                    quantise_rows(nc, link, w[:, g, :], w[:, g, :], top, tmp[:])
                    dve.sem_inc(ready, 1)

            @block.tensor
            def _(pe):
                for g in range(2 * FG):
                    pe.wait_ge(ready, g + 1)
                    if g >= 2:
                        pe.wait_ge(copied, g - 1)
                    for c in range(DC):
                        last = nc.tensor.transpose(ps[:, g % 2, c, :], w[:, g, c * P:(c + 1) * P], env.ident[:])
                    last.then_inc(turned, 1)

            @block.scalar
            def _(act):
                for g in range(2 * FG):
                    act.wait_ge(turned, g + 1)
                    nc.scalar.copy(wT[:, g], ps[:, g % 2]).then_inc(copied, 1)


def output_block(env, name, heads_out, gate, wo_dram, quantised=False, after_norm=False, feature_major=False):
    nc, io = env.nc, env.io
    env.prefix = f"{name}_out"
    loaded, ready, turned, copied = env.sem("loaded"), env.sem("ready"), env.sem("turned"), env.sem("copied")
    y_done, y_used, var_done, sd_done = env.sem("y_done"), env.sem("y_used"), env.sem("var_done"), env.sem("sd_done")
    normal, pool_steps = env.sem("normal"), env.sem("pool_steps")
    LOADS = 16 * (5 if after_norm else 2)
    with ExitStack() as local:
        def sb(n, shape, dt=F32):
            return local.enter_context(nc.sbuf_tensor(f"{name}_{n}", shape, dt))

        wo, bo, aT = sb("wo", [P, DC, D]), sb("bo", [P, D]), sb("aT", [P, 2, DC, P])
        top, tmp, delta = sb("out_top", [P, 2]), sb("out_tmp", [P, D]), sb("delta", [P, 2, D])
        if after_norm:
            gamma, beta, rs = sb("gamma", [P, D]), sb("beta", [P, D]), sb("rs", [P, 1])
            stats, meanvar, sd = sb("out_stats", [P, 2, 6]), sb("out_meanvar", [P, 2, 2]), sb("out_sd", [P, 2, 2])
        t_ps = local.enter_context(nc.psum_tensor(f"{name}_turn_ps", [P, 2, DC, P], F32))
        y_ps = local.enter_context(nc.psum_tensor(f"{name}_out_ps", [P, 2, D], F32))
        with nc.Block() as block:
            @block.sync
            def _(sp):
                sp.dma_start(wo[:], wo_dram).then_inc(loaded, 16)
                sp.dma_start(bo[:], io["bo"].partition_broadcast(P)).then_inc(loaded, 16)
                if after_norm:
                    sp.dma_start(gamma[:], io["gamma"].partition_broadcast(P)).then_inc(loaded, 16)
                    sp.dma_start(beta[:], io["beta"].partition_broadcast(P)).then_inc(loaded, 16)
                    sp.dma_start(rs[:], io["rs"].partition_broadcast(P)).then_inc(loaded, 16)

            @block.tensor
            def _(pe):
                pe.wait_ge(loaded, LOADS)

                def product(t):
                    if not feature_major:
                        pe.wait_ge(copied, t + 1)
                    if t >= 2:
                        pe.wait_ge(y_used, t - 1)
                    for c in range(DC):
                        lhsT = heads_out[:, c, t * P:(t + 1) * P] if feature_major else aT[:, t % 2, c, :]
                        last = nc.tensor.matmul(y_ps[:, t % 2, :], lhsT, wo[:, c, :],
                                                start=(c == 0), stop=(c == DC - 1))
                    last.then_inc(y_done, 1)

                for t in range(TILES):
                    if feature_major:
                        product(t)
                        continue
                    if quantised:
                        pe.wait_ge(ready, t + 1)
                    if t >= 2:
                        pe.wait_ge(copied, t - 1)
                    for c in range(DC):
                        last = nc.tensor.transpose(t_ps[:, t % 2, c, :], heads_out[:, t, c * P:(c + 1) * P], env.ident[:])
                    last.then_inc(turned, 1)
                    if t >= 1:
                        product(t - 1)
                if not feature_major:
                    product(TILES - 1)

            @block.scalar
            def _(act):
                def root(act, t):
                    act.wait_ge(var_done, t + 1)
                    nc.scalar.activation(sd[:, t % 2, 0:1], meanvar[:, t % 2, 1:2], ACT.Sqrt,
                                         bias=env.eps_ln[:]).then_inc(sd_done, 1)

                for t in range(TILES):
                    if not feature_major:
                        act.wait_ge(turned, t + 1)
                        if t >= 2:
                            act.wait_ge(y_done, t - 1)
                        nc.scalar.copy(aT[:, t % 2], t_ps[:, t % 2]).then_inc(copied, 1)
                    if after_norm and t >= 2:
                        root(act, t - 2)
                if after_norm:
                    root(act, TILES - 2)
                    root(act, TILES - 1)

            if after_norm:
                @block.gpsimd
                def _(pool):
                    for t in range(TILES):
                        d, x = delta[:, t % 2, :], env.x[:, t, :]
                        pool.wait_ge(normal, t + 1)
                        nc.gpsimd.tensor_tensor(d, d, gamma[:], ALU.mult).then_inc(pool_steps, 1)
                        pool.wait_ge(pool_steps, 3 * t + 1)
                        nc.gpsimd.tensor_tensor(d, d, beta[:], ALU.add).then_inc(pool_steps, 1)
                        pool.wait_ge(pool_steps, 3 * t + 2)
                        nc.gpsimd.tensor_tensor(x, x, d, ALU.add).then_inc(pool_steps, 1)
                    pool.wait_ge(pool_steps, 3 * TILES)

            @block.vector
            def _(dve):
                links, count = env.sem("links"), [0]

                def link(ins):
                    count[0] += 1
                    ins.then_inc(links, 1)
                    dve.wait_ge(links, count[0])

                def output(t):
                    d = delta[:, t % 2, :]
                    dve.wait_ge(y_done, t + 1)
                    if after_norm and t >= 2:
                        dve.wait_ge(pool_steps, 3 * (t - 1))
                    nc.vector.tensor_tensor(d, y_ps[:, t % 2, :], bo[:], ALU.add).then_inc(y_used, 1)
                    dve.wait_ge(y_used, t + 1)
                    if after_norm:
                        link(nc.vector.tensor_scalar(d, d, rs[:], None, ALU.mult))
                        link(nc.vector.bn_stats(stats[:, t % 2, :], d))
                        nc.vector.bn_aggr(meanvar[:, t % 2, :], stats[:, t % 2, :]).then_inc(var_done, 1)
                        dve.wait_ge(sd_done, t + 1)
                        link(nc.vector.reciprocal(sd[:, t % 2, 1:2], sd[:, t % 2, 0:1]))
                        nc.vector.tensor_scalar(d, d, meanvar[:, t % 2, 0:1], sd[:, t % 2, 1:2], ALU.subtract,
                                                ALU.mult).then_inc(normal, 1)
                    else:
                        link(nc.vector.scalar_tensor_tensor(env.x[:, t, :], d, gate, env.x[:, t, :], ALU.mult, ALU.add))

                dve.wait_ge(loaded, LOADS)
                if after_norm:
                    link(nc.vector.tensor_scalar(rs[:], rs[:], 0.0, 0.3, ALU.max, ALU.min))
                    link(nc.vector.tensor_scalar(gamma[:], gamma[:], gate, None, ALU.mult))
                    link(nc.vector.tensor_scalar(beta[:], beta[:], gate, None, ALU.mult))
                LAG = 2 if quantised else 0
                for t in range(TILES + LAG):
                    if quantised and t < TILES:
                        quantise_rows(nc, link, heads_out[:, t, :], heads_out[:, t, :], top, tmp[:])
                        dve.sem_inc(ready, 1)
                    if t >= LAG:
                        output(t - LAG)


def build(nc, io, out, stages):
    with ExitStack() as stack:
        env = Env(nc, stack, io)
        env.x = stack.enter_context(nc.sbuf_tensor("x", [P, TILES, D], F32))
        env.ident = stack.enter_context(nc.sbuf_tensor("ident", [P, P], F32))
        env.gates = stack.enter_context(nc.sbuf_tensor("gates", [P, 8], F32))
        env.tanh_gates = stack.enter_context(nc.sbuf_tensor("tanh_gates", [P, 8], F32))
        env.iota8 = stack.enter_context(nc.sbuf_tensor("iota8", [P, 8], F32))
        env.eps_ln = stack.enter_context(nc.sbuf_tensor("eps_ln", [P, 1], F32))
        setup_block(env)

        @contextmanager
        def sublayer():
            with nc.cleanup_on_exit(), ExitStack() as local:
                yield local

        def layer(prefix, *names):
            env.io = {n: io[f"{prefix}_{n}"] for n in names}

        def attention_layer(name, gate, **kinds):
            with sublayer() as local:
                sb = lambda n, s, d=F32: local.enter_context(nc.sbuf_tensor(n, s, d))
                layer(name, *[n[len(name) + 1:] for n in io if n.startswith(name)])
                env.io["ctxT"] = io["ctxT"]
                env.xT, env.ctxT = sb(f"{name}_xT", [P, DC, TOK]), sb(f"{name}_ctxT", [P, DC, BATCH * CTX])
                env.prefix = name
                env.ctx_loaded = env.sem("ctx_loaded")
                masked, linear = kinds.get("masked", False), kinds.get("linear", False)
                heads_out = sb(f"{name}_heads", [P, TILES, D] if linear else [P, DC, TOK])
                keep_mask = None
                quantised = kinds.get("quantised", False)
                if quantised:
                    wq_scratch = nc.dram_tensor("wq_scratch", (D // P, P, D), F32, kind="Internal").ap()
                    env.io["wq"] = wq_scratch
                    env.io["wo"] = nc.dram_tensor("wp_scratch", (P, DC, D), F32, kind="Internal").ap()
                    quantise_weights_block(env, name, wq_scratch, env.io["wo"])
                if masked:
                    keep_mask = sb("keep_mask", [P, 2, BATCH * CTX // P])
                    env.io["mask"] = io["mask"]
                    key_mask_block(env, name, keep_mask)
                norm_block(env, name, quantised=quantised, load_context=True)
                if linear:
                    env.io["mask_f"] = io["mask_f"]
                    linear_attention_block(env, name, heads_out)
                elif masked:
                    masked_attention_block(env, name, heads_out, keep_mask)
                else:
                    softmax_attention_block(env, name, heads_out)
                if quantised:
                    aT, heads_out = heads_out, sb(f"{name}_rows", [P, TILES, D])
                    token_major_block(env, name, aT, heads_out)
                output_block(env, name, heads_out, gate, env.io["wo"], quantised, kinds.get("after_norm", False),
                             feature_major=not linear and not quantised)

        def x_halves(name, local):
            return [local.enter_context(nc.sbuf_tensor(f"{name}_x_{n}", [P, DC, TOK], F32R)) for n in ("high", "low")]

        @contextmanager
        def x_hat(name, x_parts):
            with nc.sbuf_tensor(f"{name}_xT", [P, DC, TOK], F32) as env.xT:
                norm_block(env, name, split=x_parts)
                yield

        def expert_layer(name, gate, chunks, groups, shared, normalise):
            with sublayer() as local:
                layer(name, "w1", "w2", "w3", "router")
                weight = local.enter_context(nc.sbuf_tensor(f"{name}_weight", [P, TILES, groups], F32))
                x_parts = x_halves(name, local)

                def route(first):
                    with x_hat(name, x_parts):
                        expert_weights_block(env, name, groups, shared, normalise, gate, weight, first)

                ffn_block(env, name, chunks, weight, x_parts, meanwhile=route)

        if "L0_attn" in stages:
            attention_layer("L0_attn", env.tanh_gates[:, 0:1], linear=True)
        if "L0_ffn" in stages:
            layer("L0_ffn", "w1", "w2", "w3")
            with sublayer() as local:
                sb = lambda n, s, d=F32: local.enter_context(nc.sbuf_tensor(n, s, d))
                scale, half, neg_half = sb("scale", [P, 3]), sb("half", [P, 3]), sb("neg_half", [P, 3])
                weight = sb("weight", [P, 1])
                ternary_scales(env, "L0_ffn", scale, half, neg_half, env.tanh_gates[:, 4:5], weight)
                x_parts = x_halves("L0_ffn", local)
                with x_hat("L0_ffn", x_parts):
                    pass
                ffn_block(env, "L0_ffn", [P, P], weight, x_parts, ternary=(scale, half, neg_half))
        if "L1_attn" in stages:
            attention_layer("L1_attn", env.tanh_gates[:, 1:2], masked=True, after_norm=True)
        if "L1_ffn" in stages:
            with sublayer() as local:
                sb = lambda n, s, d=F32: local.enter_context(nc.sbuf_tensor(n, s, d))
                layer("L1_ffn", "w1", "w3", "wq", "keys")
                G = io["L1_ffn_w1"].shape[0]
                sims, bar = sb("sims", [P, TILES, PEER_HEADS, KEY_ROWS + NK]), sb("bar", [P, TILES * PEER_HEADS])
                extra = sb("extra", [P, G, TILES])
                x_parts = x_halves("L1_ffn", local)

                def score_keys(first):
                    with x_hat("L1_ffn", x_parts):
                        product_keys_block(env, "L1_ffn", sims, bar, extra, G, first)

                ffn_block(env, "L1_ffn", [P] * 4, env.tanh_gates[:, 5:6], x_parts, peer=(sims, bar, extra),
                          meanwhile=score_keys)
        if "L2_attn" in stages:
            attention_layer("L2_attn", env.tanh_gates[:, 2:3], quantised=True)
        if "L2_ffn" in stages:
            expert_layer("L2_ffn", env.tanh_gates[:, 6:7], [P, P], 8, 0, True)
        if "L3_attn" in stages:
            attention_layer("L3_attn", env.tanh_gates[:, 3:4])
        if "L3_ffn" in stages:
            expert_layer("L3_ffn", env.tanh_gates[:, 7:8], [P, P, 96], 12, 4, False)
        store_block(env, out)


def lay_out(inputs):
    import numpy as np

    def up(w, group):
        g = w.shape[0] // group
        return w.reshape(g, group, DC, P).transpose(0, 3, 2, 1).reshape(g, P, DC * group)

    def rows(w):
        return w.reshape(DC, P, w.shape[1]).transpose(1, 0, 2)

    i = {k: np.asarray(v) for k, v in inputs.items()}
    a = {k: i[k] for k in ("x", "g_xattn", "g_ffn")}
    a["L0_ffn_w1"], a["L0_ffn_w2"] = up(i["L0_ffn_W_up"], 256), up(i["L0_ffn_W_gate"], 256)
    a["L0_ffn_w3"] = i["L0_ffn_W_down"].T.reshape(8, 256, D)
    a["L1_ffn_w1"], a["L1_ffn_w3"] = up(i["L1_ffn_e_down"], 512), i["L1_ffn_e_up"].reshape(8, 512, D)
    a["L1_ffn_wq"] = rows(i["L1_ffn_Wq"])
    a["L1_ffn_keys"] = i["L1_ffn_keys"].transpose(3, 2, 0, 1)
    a["L2_ffn_w1"] = up(i["L2_ffn_wi_0"].transpose(0, 2, 1).reshape(-1, D), 256)
    a["L2_ffn_w2"] = up(i["L2_ffn_wi_1"].transpose(0, 2, 1).reshape(-1, D), 256)
    a["L2_ffn_w3"], a["L2_ffn_router"] = i["L2_ffn_wo"], rows(i["L2_ffn_w_gate"])
    s, w13 = i["L3_ffn_shared_gate_up_w"], i["L3_ffn_w13"]
    inter = w13.shape[1] // 2
    a["L3_ffn_w1"] = up(np.concatenate([s[:s.shape[0] // 2], w13[:, :inter].reshape(-1, D)]), inter)
    a["L3_ffn_w2"] = up(np.concatenate([s[s.shape[0] // 2:], w13[:, inter:].reshape(-1, D)]), inter)
    a["L3_ffn_w3"] = np.concatenate([i["L3_ffn_shared_down_w"].T.reshape(-1, inter, D),
                                     i["L3_ffn_w2"].transpose(0, 2, 1)])
    a["L3_ffn_router"] = rows(np.concatenate([i["L3_ffn_gate_w"], i["L3_ffn_shared_gate_w"]]).T)
    a["ctxT"] = rows(i["ctx_2048"].reshape(-1, D).T)
    a["mask"] = i["mask_BxS2_ik0"].reshape(-1, P).T

    def column(b):
        return b.reshape(DC, P, 1)

    for n in (0, 1, 3):
        for m in ("q", "k"):
            a[f"L{n}_attn_w{m}"] = up(i[f"L{n}_xattn_W{m}"], P)
            a[f"L{n}_attn_b{m}"] = column(i[f"L{n}_xattn_b{m}"])
        for m in ("v", "o"):
            a[f"L{n}_attn_w{m}"], a[f"L{n}_attn_b{m}"] = rows(i[f"L{n}_xattn_W{m}"].T), i[f"L{n}_xattn_b{m}"]
    a["L1_attn_wv"], a["L1_attn_bv"] = up(i["L1_xattn_Wv"], P), i["L1_xattn_bv"].reshape(DC, P)
    a["L3_attn_wv"], a["L3_attn_bv"] = up(i["L3_xattn_Wv"], P), i["L3_xattn_bv"].reshape(-1, 32).T
    a["L0_attn_wqf"], a["L0_attn_wkf"] = i["L0_xattn_Wqf"].T, i["L0_xattn_Wkf"].T
    a["mask_f"] = i["mask_BxS2_ff1"].reshape(-1, P).T
    a["L1_attn_gamma"], a["L1_attn_beta"] = i["L1_xattn_ln_gamma"], i["L1_xattn_ln_beta"]
    a["L1_attn_rs"] = i["L1_xattn_residual_scale"].reshape(1)
    a["L2_attn_wq_rows"], a["L2_attn_wp_rows"] = i["L2_xattn_wq"], i["L2_xattn_wp"]
    a["L2_attn_wk"], a["L2_attn_wv"] = up(i["L2_xattn_wkv"][:D], P), up(i["L2_xattn_wkv"][D:], P)
    a["L2_attn_bq"], a["L2_attn_bk"] = column(i["L2_xattn_bq"]), column(i["L2_xattn_bkv"][:D])
    a["L2_attn_bv"], a["L2_attn_bo"] = i["L2_xattn_bkv"][D:].reshape(-1, 32).T, i["L2_xattn_bp"]
    return {k: np.ascontiguousarray(v) for k, v in a.items()}


STAGES = ("L0_attn", "L0_ffn", "L1_attn", "L1_ffn", "L2_attn", "L2_ffn", "L3_attn", "L3_ffn")


def kernel(**inputs):
    import concourse.bacc as bacc
    from concourse.bass_utils import run_bass_kernel_spmd

    nc = bacc.Bacc("TRN2", target_bir_lowering=False, num_devices=1)
    arrays, io = {}, {}
    for name, a in lay_out(inputs).items():
        arrays[f"in_{name}"] = a
        io[name] = nc.dram_tensor(f"in_{name}", a.shape, mybir.dt.from_np(a.dtype), kind="ExternalInput").ap()
    out = nc.dram_tensor("out_x", (BATCH, SEQ, D), F32, kind="ExternalOutput").ap()
    build(nc, io, out, STAGES)
    r = run_bass_kernel_spmd(nc, [arrays], core_ids=[0])
    return r.results[0]["out_x"]
```
